# Optimizing a Trainium2 kernel written in Bass

```python
import numpy as np
import jax
import jax.numpy as jnp

def _softmax(x, axis=-1):
    return jax.nn.softmax(x, axis=axis)

def _gelu(x):
    return jax.nn.gelu(x, approximate=True)

def _silu(x):
    return jax.nn.silu(x)

def _sigmoid(x):
    return jax.nn.sigmoid(x)

def _layernorm(x, axis=-1, eps=1e-05):
    m = jnp.mean(x, axis=axis, keepdims=True)
    v = jnp.var(x, axis=axis, keepdims=True)
    return (x - m) / jnp.sqrt(v + eps)

def _scatter_add(tgt, idx, src, axis=0):
    return tgt.at[idx].add(src)

def _segment_sum(src, seg, n):
    return jax.ops.segment_sum(src, seg, n)
kernel_name = 'mk_decoder_postln_d1_seqx_r4_ca297a'

def setup_inputs(seed: int=0):
    np.random.seed(seed)
    _w = jnp.asarray

    def _rec_inputs():
        import jax
        import jax.numpy as jnp
        _rk = jax.random.key(seed)
        x = -0.0002928 + 1 * jax.random.normal(jax.random.fold_in(_rk, 1), (4, 1024, 256), jnp.float32)
        _lenS = 1024 - jax.random.randint(jax.random.fold_in(_rk, 7), (4,), 0, max(1, 1024 // 4) + 1, jnp.int32)
        _lenS2 = 77 - jax.random.randint(jax.random.fold_in(_rk, 8), (4,), 0, max(1, 77 // 4) + 1, jnp.int32)
        _ctx_1024P = jax.random.normal(jax.random.fold_in(_rk, 11), (4, 16, 256), jnp.float32)
        _ctx_1024c = jax.random.dirichlet(jax.random.fold_in(_rk, 511), 0.3 * jnp.ones((16,), jnp.float32), (4, 77))
        _ctx_1024t = jnp.einsum('bsk,bkd->bsd', _ctx_1024c, _ctx_1024P)
        _ctx_1024t = _ctx_1024t * jax.lax.rsqrt(jnp.mean(jnp.square(_ctx_1024t)) + 1e-12) * 0.953939
        ctx_1024 = -1.39393e-06 + 0.999914 * (_ctx_1024t + 0.3 * jax.random.normal(jax.random.fold_in(_rk, 611), (4, 77, 256), jnp.float32))
        _validS = jnp.arange(1024)[None, :] < _lenS[:, None]
        _validS2 = jnp.arange(77)[None, :] < _lenS2[:, None]
        _causal = jnp.tril(jnp.ones((1024, 1024), dtype=bool))
        mask_Bx1xSxS2_if1 = jnp.where(jnp.ones((4, 1, 1024, 77), dtype=bool), 1, 0).astype(jnp.int32)
        return (x, ctx_1024, mask_Bx1xSxS2_if1)
    x, ctx_1024, mask_Bx1xSxS2_if1 = _rec_inputs()

    def _L0_attn_setup():
        import jax, jax.numpy as jnp
        import numpy as np
        NUM_HEADS = 16
        LN_EPS = 1e-05
        NORM_EPS = 1e-12

        def _l2norm(t):
            return t / jnp.maximum(jnp.linalg.norm(t, axis=-1, keepdims=True), NORM_EPS)

        def _forward(x, Wq, Wk, Wv, Wf1, Wf2, Wg, Wo1, Wo2, ln_w, Wout):
            B, N, D = x.shape
            H = NUM_HEADS
            HD = D // H
            q = jax.nn.silu(x @ Wq)
            k = jax.nn.silu(x @ Wk)
            v = jax.nn.silu(x @ Wv)
            log_f = jax.nn.log_sigmoid(x @ Wf1 @ Wf2)
            gamma = -jax.nn.sigmoid(x @ Wg)
            q = q.reshape(B, N, H, HD)
            k = k.reshape(B, N, H, HD)
            v = v.reshape(B, N, H, HD)
            log_f = log_f.reshape(B, N, H, HD)
            k = _l2norm(k)
            a = k * gamma[..., None]

            def step(S, inp):
                qt, kt, vt, at, gft = inp
                bs1 = jnp.einsum('bhk,bhkv->bhv', kt, S)
                S1 = S + at[..., :, None] * bs1[..., None, :]
                S2 = jnp.exp(gft)[..., None] * S1
                bs2 = jnp.einsum('bhk,bhkv->bhv', kt, S2)
                S3 = S2 + at[..., :, None] * bs2[..., None, :] + kt[..., :, None] * vt[..., None, :]
                o = jnp.einsum('bhk,bhkv->bhv', qt, S3)
                return (S3, o)
            to_time = lambda t: jnp.moveaxis(t, 1, 0)
            S0 = jnp.zeros((B, H, HD, HD), dtype=x.dtype)
            _, o = jax.lax.scan(step, S0, (to_time(q), to_time(k), to_time(v), to_time(a), to_time(log_f)))
            o = jnp.moveaxis(o, 0, 1)
            z = jnp.zeros_like(o)
            out3 = jnp.stack([z, z, o], axis=2).reshape(B, 3 * N, H, HD)
            out = out3[:, -N:]
            out = out.reshape(B, N, D)
            gate = jax.nn.sigmoid(x @ Wo1 @ Wo2)
            out = out * gate
            mu = jnp.mean(out, axis=-1, keepdims=True)
            var = jnp.mean((out - mu) ** 2, axis=-1, keepdims=True)
            out = (out - mu) * jax.lax.rsqrt(var + LN_EPS) * ln_w
            return out @ Wout
        key = jax.random.key(seed)
        ks = jax.random.split(key, 12)
        B, N, D = (2, 256, 256)
        HD = D // NUM_HEADS
        s = 0.02
        inp = {'x': jax.random.normal(ks[0], (B, N, D), dtype=jnp.float32), 'Wq': jax.random.normal(ks[1], (D, D), dtype=jnp.float32) * s, 'Wk': jax.random.normal(ks[2], (D, D), dtype=jnp.float32) * s, 'Wv': jax.random.normal(ks[3], (D, D), dtype=jnp.float32) * s, 'Wf1': jax.random.normal(ks[4], (D, HD), dtype=jnp.float32) * s, 'Wf2': jax.random.normal(ks[5], (HD, D), dtype=jnp.float32) * s, 'Wg': jax.random.normal(ks[6], (D, NUM_HEADS), dtype=jnp.float32) * s, 'Wo1': jax.random.normal(ks[7], (D, HD), dtype=jnp.float32) * s, 'Wo2': jax.random.normal(ks[8], (HD, D), dtype=jnp.float32) * s, 'ln_w': jnp.ones((D,), dtype=jnp.float32), 'Wout': jax.random.normal(ks[9], (D, D), dtype=jnp.float32) * s}
        return inp
    _L0_attn_all = _L0_attn_setup()
    _L0_attn_in = {k: v for k, v in _L0_attn_all.items() if k in ('Wq', 'Wk', 'Wv', 'Wf1', 'Wf2', 'Wg', 'Wo1', 'Wo2', 'ln_w', 'Wout')}
    del _L0_attn_all

    def _L0_xattn_setup():
        import jax, jax.numpy as jnp
        import numpy as np
        from math import sqrt
        H = 16
        key = jax.random.key(seed)
        ks = jax.random.split(key, 8)
        B, Sq, Skv, Dq, Dkv, Dall = (2, 512, 512, 256, 256, 256)
        x = jax.random.normal(ks[0], (B, Sq, Dq), dtype=jnp.float32)
        y = jax.random.normal(ks[1], (B, Skv, Dkv), dtype=jnp.float32)
        attention_mask = jnp.ones((B, 1, Sq, Skv), dtype=jnp.int32)
        Wq = jax.random.normal(ks[2], (Dall, Dq), dtype=jnp.float32) * 0.02
        Wk = jax.random.normal(ks[3], (Dall, Dkv), dtype=jnp.float32) * 0.02
        Wv = jax.random.normal(ks[4], (Dall, Dkv), dtype=jnp.float32) * 0.02
        Wo = jax.random.normal(ks[5], (Dq, Dall), dtype=jnp.float32) * 0.02
        bo = jnp.zeros((Dq,), dtype=jnp.float32)
        return {'x': x, 'y': y, 'attention_mask': attention_mask, 'Wq': Wq, 'Wk': Wk, 'Wv': Wv, 'Wo': Wo, 'bo': bo}
    _L0_xattn_all = _L0_xattn_setup()
    _L0_xattn_in = {k: v for k, v in _L0_xattn_all.items() if k in ('Wq', 'Wk', 'Wv', 'Wo', 'bo')}
    del _L0_xattn_all

    def _L0_ffn_setup():
        import jax, jax.numpy as jnp
        import numpy as np
        D = 256
        F = 4 * D
        E = 8
        NS = 2
        TOP_K = 2
        B, S = (2, 256)
        key = jax.random.key(seed)
        ks = jax.random.split(key, 7)
        w = 1.0 / np.sqrt(D)
        wf = 1.0 / np.sqrt(F)
        return {'x': jax.random.normal(ks[0], (B, S, D), jnp.float32), 'centroids': jax.random.normal(ks[1], (E, D), jnp.float32) * w, 'routing_bias': jnp.zeros((E,), jnp.float32), 'Wfc_r': jax.random.normal(ks[2], (E, F, D), jnp.float32) * w, 'Wproj_r': jax.random.normal(ks[3], (E, D, F), jnp.float32) * wf, 'Wfc_sh': jax.random.normal(ks[4], (NS, F, D), jnp.float32) * w, 'Wproj_sh': jax.random.normal(ks[5], (NS, D, F), jnp.float32) * wf}
    _L0_ffn_all = _L0_ffn_setup()
    _L0_ffn_in = {k: v for k, v in _L0_ffn_all.items() if k in ('centroids', 'routing_bias', 'Wfc_r', 'Wproj_r', 'Wfc_sh', 'Wproj_sh')}
    del _L0_ffn_all
    return {'x': x, 'ctx_1024': ctx_1024, 'mask_Bx1xSxS2_if1': mask_Bx1xSxS2_if1, 'L0_attn_Wq': _L0_attn_in['Wq'], 'L0_attn_Wk': _L0_attn_in['Wk'], 'L0_attn_Wv': _L0_attn_in['Wv'], 'L0_attn_Wf1': _L0_attn_in['Wf1'], 'L0_attn_Wf2': _L0_attn_in['Wf2'], 'L0_attn_Wg': _L0_attn_in['Wg'], 'L0_attn_Wo1': _L0_attn_in['Wo1'], 'L0_attn_Wo2': _L0_attn_in['Wo2'], 'L0_attn_ln_w': _L0_attn_in['ln_w'], 'L0_attn_Wout': _L0_attn_in['Wout'], 'L0_xattn_Wq': _L0_xattn_in['Wq'], 'L0_xattn_Wk': _L0_xattn_in['Wk'], 'L0_xattn_Wv': _L0_xattn_in['Wv'], 'L0_xattn_Wo': _L0_xattn_in['Wo'], 'L0_xattn_bo': _L0_xattn_in['bo'], 'L0_ffn_centroids': _L0_ffn_in['centroids'], 'L0_ffn_routing_bias': _L0_ffn_in['routing_bias'], 'L0_ffn_Wfc_r': _L0_ffn_in['Wfc_r'], 'L0_ffn_Wproj_r': _L0_ffn_in['Wproj_r'], 'L0_ffn_Wfc_sh': _L0_ffn_in['Wfc_sh'], 'L0_ffn_Wproj_sh': _L0_ffn_in['Wproj_sh']}

def reference(x, ctx_1024, mask_Bx1xSxS2_if1, L0_attn_Wq, L0_attn_Wk, L0_attn_Wv, L0_attn_Wf1, L0_attn_Wf2, L0_attn_Wg, L0_attn_Wo1, L0_attn_Wo2, L0_attn_ln_w, L0_attn_Wout, L0_xattn_Wq, L0_xattn_Wk, L0_xattn_Wv, L0_xattn_Wo, L0_xattn_bo, L0_ffn_centroids, L0_ffn_routing_bias, L0_ffn_Wfc_r, L0_ffn_Wproj_r, L0_ffn_Wfc_sh, L0_ffn_Wproj_sh):
    import jax
    import jax.numpy as jnp

    def _L0_attn_ref(x, Wq, Wk, Wv, Wf1, Wf2, Wg, Wo1, Wo2, ln_w, Wout):
        import jax, jax.numpy as jnp
        import numpy as np
        NUM_HEADS = 16
        LN_EPS = 1e-05
        NORM_EPS = 1e-12

        def _l2norm(t):
            return t / jnp.maximum(jnp.linalg.norm(t, axis=-1, keepdims=True), NORM_EPS)

        def _forward(x, Wq, Wk, Wv, Wf1, Wf2, Wg, Wo1, Wo2, ln_w, Wout):
            B, N, D = x.shape
            H = NUM_HEADS
            HD = D // H
            q = jax.nn.silu(x @ Wq)
            k = jax.nn.silu(x @ Wk)
            v = jax.nn.silu(x @ Wv)
            log_f = jax.nn.log_sigmoid(x @ Wf1 @ Wf2)
            gamma = -jax.nn.sigmoid(x @ Wg)
            q = q.reshape(B, N, H, HD)
            k = k.reshape(B, N, H, HD)
            v = v.reshape(B, N, H, HD)
            log_f = log_f.reshape(B, N, H, HD)
            k = _l2norm(k)
            a = k * gamma[..., None]

            def step(S, inp):
                qt, kt, vt, at, gft = inp
                bs1 = jnp.einsum('bhk,bhkv->bhv', kt, S)
                S1 = S + at[..., :, None] * bs1[..., None, :]
                S2 = jnp.exp(gft)[..., None] * S1
                bs2 = jnp.einsum('bhk,bhkv->bhv', kt, S2)
                S3 = S2 + at[..., :, None] * bs2[..., None, :] + kt[..., :, None] * vt[..., None, :]
                o = jnp.einsum('bhk,bhkv->bhv', qt, S3)
                return (S3, o)
            to_time = lambda t: jnp.moveaxis(t, 1, 0)
            S0 = jnp.zeros((B, H, HD, HD), dtype=x.dtype)
            _, o = jax.lax.scan(step, S0, (to_time(q), to_time(k), to_time(v), to_time(a), to_time(log_f)))
            o = jnp.moveaxis(o, 0, 1)
            z = jnp.zeros_like(o)
            out3 = jnp.stack([z, z, o], axis=2).reshape(B, 3 * N, H, HD)
            out = out3[:, -N:]
            out = out.reshape(B, N, D)
            gate = jax.nn.sigmoid(x @ Wo1 @ Wo2)
            out = out * gate
            mu = jnp.mean(out, axis=-1, keepdims=True)
            var = jnp.mean((out - mu) ** 2, axis=-1, keepdims=True)
            out = (out - mu) * jax.lax.rsqrt(var + LN_EPS) * ln_w
            return out @ Wout
        return _forward(x, Wq, Wk, Wv, Wf1, Wf2, Wg, Wo1, Wo2, ln_w, Wout)

    def _L0_xattn_ref(x, y, attention_mask, Wq, Wk, Wv, Wo, bo):
        import jax, jax.numpy as jnp
        import numpy as np
        from math import sqrt
        H = 16
        B, Sq, _ = x.shape
        Dall = Wq.shape[0]
        Dh = Dall // H
        q = (x @ Wq.T).reshape(B, Sq, H, Dh).transpose(0, 2, 1, 3)
        k = (y @ Wk.T).reshape(B, -1, H, Dh).transpose(0, 2, 1, 3)
        v = (y @ Wv.T).reshape(B, -1, H, Dh).transpose(0, 2, 1, 3)
        scores = jnp.einsum('bhqd,bhkd->bhqk', q, k)
        mask = attention_mask == 0
        scores = jnp.where(mask, jnp.float32(-1000000000.0), scores)
        attn = jax.nn.softmax(scores / sqrt(Dh), axis=-1)
        out = jnp.einsum('bhqk,bhkd->bhqd', attn, v)
        out = out.transpose(0, 2, 1, 3).reshape(B, Sq, Dall)
        return out @ Wo.T + bo

    def _L0_ffn_ref(x, centroids, routing_bias, Wfc_r, Wproj_r, Wfc_sh, Wproj_sh):
        import jax, jax.numpy as jnp
        import numpy as np
        D = 256
        F = 4 * D
        E = 8
        NS = 2
        TOP_K = 2
        B, S = (2, 256)
        raw = jnp.einsum('bsd,ed->bse', x, centroids)
        routing_scores = jax.nn.sigmoid(raw)
        balanced = jax.nn.sigmoid(raw + routing_bias)
        _, top_idx = jax.lax.top_k(balanced, TOP_K)
        gathered = jnp.take_along_axis(routing_scores, top_idx, axis=-1)
        top_w = jax.nn.softmax(gathered, axis=-1)
        combine = jnp.sum(jax.nn.one_hot(top_idx, E, dtype=x.dtype) * top_w[..., None], axis=-2)
        h_sh = jax.nn.gelu(jnp.einsum('bsd,nfd->bsnf', x, Wfc_sh), approximate=False)
        shared_out = jnp.einsum('bsnf,ndf->bsd', h_sh, Wproj_sh)
        h_r = jax.nn.gelu(jnp.einsum('bsd,efd->bsef', x, Wfc_r), approximate=False)
        expert_out = jnp.einsum('bsef,edf->bsed', h_r, Wproj_r)
        routed_out = jnp.einsum('bsed,bse->bsd', expert_out, combine)
        return x + shared_out + routed_out
    x = _layernorm(x + _L0_attn_ref(x, L0_attn_Wq, L0_attn_Wk, L0_attn_Wv, L0_attn_Wf1, L0_attn_Wf2, L0_attn_Wg, L0_attn_Wo1, L0_attn_Wo2, L0_attn_ln_w, L0_attn_Wout), axis=-1)
    x = _layernorm(x + _L0_xattn_ref(x, ctx_1024, mask_Bx1xSxS2_if1, L0_xattn_Wq, L0_xattn_Wk, L0_xattn_Wv, L0_xattn_Wo, L0_xattn_bo), axis=-1)
    x = _layernorm(x + _L0_ffn_ref(x, L0_ffn_centroids, L0_ffn_routing_bias, L0_ffn_Wfc_r, L0_ffn_Wproj_r, L0_ffn_Wfc_sh, L0_ffn_Wproj_sh), axis=-1)
    return x

_drawn_inputs = setup_inputs


def setup_inputs(seed=0):
    import zlib

    import numpy as np

    out = dict(_drawn_inputs(seed))
    spreads = {'L0_attn_ln_w': (1.0, 0.2), 'L0_xattn_bo': (0.0, 0.1), 'L0_ffn_routing_bias': (0.0, 0.1)}
    factors = {'L0_attn_Wf1': 8.0,
     'L0_attn_Wf2': 8.0,
     'L0_attn_Wg': 22.438,
     'L0_attn_Wo1': 8.0,
     'L0_attn_Wo2': 8.0,
     'L0_xattn_Wq': 8.0,
     'L0_xattn_Wk': 8.0}
    for name, (base, spread) in spreads.items():
        noise = np.random.default_rng([zlib.crc32(name.encode()), seed]).standard_normal(out[name].shape)
        drawn = base * np.exp(spread * noise) if base else spread * noise
        out[name] = jnp.asarray(drawn.astype(out[name].dtype))
    for name, factor in factors.items():
        out[name] = (out[name] * factor).astype(out[name].dtype)
    return out
```

```python
from contextlib import ExitStack

import concourse.bass as bass
from concourse import mybir

F32 = mybir.dt.float32
I32 = mybir.dt.int32
ALU = mybir.AluOpType
ACT = mybir.ActivationFunctionType
AX = mybir.AxisListType

B, N, D = 4, 1024, 256
H, HD = 16, 16
SK = 77
NSH, NR, F = 2, 8, 1024
NE = NSH + NR
P = 128
KC = D // P
FG = F // P
G = 114
W = B * G
ROWS = 9 * G
FREE, BOUND = 6, 3
TILES = FREE + BOUND
QH = 4
T = 32
NBLK = N // T
RING = 4
OG = 8
O_FIRST = (3 * N - N) // 3
HV, HC = 8, 4
LN_EPS = 1e-5
NORM_EPS = 1e-12
QSCALE = HD ** -0.5
MASKED = -1e9 * QSCALE
HUGE = 3e38

PAIRS = FREE // 2
ITERS = NE * PAIRS
KEEP_EP = 3
KEEP_IT = KEEP_EP * 2 * PAIRS
assert KEEP_IT * T <= O_FIRST and ITERS + 2 == NBLK
PREP = 23
LAY = 6
STEP = 8
LN_LAST_FREE = 2 * FREE
LN_BOUND = LN_LAST_FREE + FREE
LN_LAST_BOUND = LN_BOUND + 3 * BOUND


def decoder_layer(nc, x, xT, ctxT, mask, wkv, wqr, wf1, wf2, wg, wo1, wo2, ln_w, wout,
                  cqT, ckT, cvT, coT, cbo, centT, rbias, wfcT, wpT, out):
    with ExitStack() as ctx:
        def sb(name, shape, dt=F32):
            return ctx.enter_context(nc.sbuf_tensor(name, shape, dt))

        def sem(name):
            return ctx.enter_context(nc.semaphore(name))

        ident = sb("ident", [P, P])
        ones = sb("ones", [1, P])
        head_mask = sb("head_mask", [P, 8])
        neg_half, neg_one = sb("neg_half", [P, H]), sb("neg_one", [P, H])
        ln_eps = sb("ln_eps", [P, H])
        index8 = sb("index8", [G, NR])
        w_kv = sb("w_kv", [P, KC, 2 * D])
        w_q = sb("w_q", [P, KC, D])
        w_f1 = sb("w_f1", [P, KC, HD])
        w_f2 = sb("w_f2", [HD, D])
        w_g = sb("w_g", [P, KC, H])
        w_o1 = sb("w_o1", [P, KC, HD])
        w_o2 = sb("w_o2", [HD, D])
        w_out = sb("w_out", [P, KC, D])
        lnw = sb("lnw", [G, D])
        c_q = sb("c_q", [P, KC, D])
        c_o = sb("c_o", [P, KC, D])
        c_bo = sb("c_bo", [1, D])
        cent = sb("cent", [P, KC, NR])
        r_bias = sb("r_bias", [1, NR])
        keys = sb("keys", [P, KC, B, 8, SK])
        vals = sb("vals", [SK, B, H, HD + 1])

        x2T = sb("x2T", [P, FREE, KC, W])
        acc = sb("acc", [G, FREE, B, D])
        comb = sb("comb", [G, NE, TILES, B])

        xin = sb("xin", [G, B, D])
        x1 = sb("x1", [G, B, D])
        arena = sb("arena", [P, 3 * KC * W + B * D])
        hT = arena[:, 0:FG * W].rearrange("p (g w) -> p g w", g=FG)
        xtf, qT, attT = (arena[:, i * KC * W:(i + 1) * KC * W].rearrange("p (c w) -> p c w", c=KC) for i in range(3))
        att = arena[0:G, 3 * KC * W:].rearrange("g (b d) -> g b d", b=B)
        imask = sb("imask", [G, B, SK], I32)
        cap = sb("cap", [G, B, SK])
        probs = sb("probs", [G, 2, H, SK])
        eT = sb("eT", [SK, H, G])
        mx = sb("mx", [G, 2, H])
        rden = sb("rden", [G, H])
        stats = sb("stats", [G, B, 6])
        mv = sb("mv", [G, B, 2])
        rstd = sb("rstd", [G, B])
        rt = sb("rt", [G, B, 2 * NR])
        spare = probs[:, 1].rearrange("g h k -> g (h k)")
        rbuf = spare[:, 0:8 * B * NR].rearrange("g (i b e) -> g i b e", i=8, b=B)
        xo1T = spare[0:HD, 0:W]
        rone = sb("rone", [G, 8, B])
        gate = sb("gate", [G, B, D])
        x2 = gate

        fc = sb("fc", [P, 2, KC, F])
        pj = sb("pj", [P, 2, FG, D])

        xtp = sb("xtp", [P, KC, B, T])
        xf1T = sb("xf1T", [HD, P])
        raw = sb("raw", [P, 3, D])
        sig = sb("sig", [P, 3, D])
        beta = sb("beta", [P, H])
        kraw, ksq, fk = sig[:, 0], raw[:, 0], sig[:, 1]
        tree = sb("tree", [P, H, 8])
        hsum = sb("hsum", [P, 4, H])
        tm = sb("tm", [P, 6, D])
        rec = sb("rec", [P, 5, HD, T])
        vrec = sb("vrec", [P, HV, T])
        prod = sb("prod", [P, 2, 2, HV, HD + 1])
        u = sb("u", [P, 2, 2, HC])
        terms = sb("terms", [P, 2, 3, HC, HD])
        S = sb("S", [P, RING, HV, HD])
        oprod = sb("oprod", [P, 2 * OG, HV, HD])
        osum = sb("osum", [P, T, HV])
        otm = sb("otm", [P, H, 2, HV])

        ps = ctx.enter_context(nc.psum_tensor("ps", [P, 8, 512], F32))
        o_dram = nc.dram_tensor("o_dram", [B, N, D], F32).ap()

        attn_w_in, xattn_w_in, ctx_in = sem("attn_w_in"), sem("xattn_w_in"), sem("ctx_in")
        xt_in, expert_in, tile_in, mask_in, bound_in = (
            sem("xt_in"), [sem("even_expert_in"), sem("odd_expert_in")], sem("tile_in"), sem("mask_in"), sem("bound_in"))
        o_stored, out_stored = sem("o_stored"), sem("out_stored")
        pool_set, pool_const, dve_const, acc_set = sem("pool_set"), sem("pool_const"), sem("dve_const"), sem("acc_set")
        ctx_k_ps, ctx_v_ps, ctx_done = sem("ctx_k_ps"), sem("ctx_v_ps"), sem("ctx_done")
        prep_ps, prep_ps2, prep_act, prep_act2, sum_seen, prep_pool = (
            sem("prep_ps"), sem("prep_ps2"), sem("prep_act"), sem("prep_act2"), sem("sum_seen"),
            sem("prep_pool"))
        block_laid, block_seen, v_placed, step_done, decayed, o_terms, o_sums, o_ready = (
            sem("block_laid"), sem("block_seen"), sem("v_placed"), sem("step_done"), sem("decayed"), sem("o_terms"), sem("o_sums"), sem("o_ready"))
        ln_stats, stats_seen, ln_mv, ln_rstd, ln_out = sem("ln_stats"), sem("stats_seen"), sem("ln_mv"), sem("ln_rstd"), sem("ln_out")
        x1T_ps, x1T_sb, q_ps, q_sb = sem("x1T_ps"), sem("x1T_sb"), sem("q_ps"), sem("q_sb")
        cap_half, cap_done, sc_ps, capped, max_done, shifted, exp_done = (
            sem("cap_half"), sem("cap_done"), sem("sc_ps"), sem("capped"), sem("max_done"),
            sem("shifted"), sem("exp_done"))
        eT_ps, eT_sb, av_ps, rden_done, att_done = (
            sem("eT_ps"), sem("eT_sb"), sem("av_ps"), sem("rden_done"), sem("att_done"))
        attT_ps, attT_sb, wo_ps, resid = sem("attT_ps"), sem("attT_sb"), sem("wo_ps"), sem("resid")
        x2T_ps, x2T_sb, rt_ps, rt_sb, route, w_done, comb_done = (
            sem("x2T_ps"), sem("x2T_sb"), sem("rt_ps"), sem("rt_sb"), sem("route"), sem("w_done"),
            sem("comb_done"))
        gx_ps, gx_sb, xo1_ps, xo1_sb, gate_ps, gate_sb, gated, weighted = (
            sem("gx_ps"), sem("gx_sb"), sem("xo1_ps"), sem("xo1_sb"), sem("gate_ps"), sem("gate_sb"),
            sem("gated"), sem("weighted"))
        gT_ps, gT_sb, wout_ps, x_plus = sem("gT_ps"), sem("gT_sb"), sem("wout_ps"), sem("x_plus")
        fc_ps, gelu_done, y_ps, y_used = sem("fc_ps"), sem("gelu_done"), sem("y_ps"), sem("y_used")

        xT_v = xT.rearrange("b (c p) t -> p c b t", p=P)
        wfc_v = wfcT.rearrange("e (c p) f -> e p c f", p=P)
        wp_v = wpT.rearrange("e (g p) d -> e p g d", p=P)

        def chunked(w):
            return w.rearrange("(c p) n -> p c n", p=P)

        def one(v, i, n=1):
            return v[i:i + n] if isinstance(i, int) else v[bass.ds(i, n)]

        def later(blk):
            return not isinstance(blk, int) or blk > 0

        def row(v):
            return v.rearrange("(a n) -> a n", a=1)

        block = ctx.enter_context(nc.Block())

        @block.sync
        def _(sp):
            def load_steps(blk):
                if later(blk):
                    sp.wait_ge(prep_ps2, blk * 2)
                for c in range(KC):
                    sp.dma_start(xtp[:, c], xT_v[:, c, :, blk * T:(blk + 1) * T] if isinstance(blk, int)
                                 else xT_v[:, c, :, bass.ds(blk * T, T)]).then_inc(xt_in, 16)

            def load_expert(e, par):
                sp.dma_start(fc[:, par], one(wfc_v, e).rearrange("e p c f -> p (e c) f")).then_inc(expert_in[par], 16)
                sp.dma_start(pj[:, par], one(wp_v, e).rearrange("e p g d -> p (e g) d")).then_inc(expert_in[par], 16)

            def load_tile(m):
                sp.dma_start(xin[:, :, :], one(x, m).rearrange("m g b d -> g (m b) d")).then_inc(tile_in, 16)
                sp.dma_start(imask[:, :, :], one(mask, m).rearrange("m g b k -> g (m b) k")).then_inc(mask_in, 16)

            def store_tile(m, norms):
                sp.wait_ge(ln_out, norms * B)
                sp.dma_start(one(out, m).rearrange("m g b d -> g (m b) d"), x1[:, :, :]).then_inc(out_stored, 16)

            def store_o(blk):
                sp.wait_ge(o_ready, blk - (KEEP_IT - 1))
                for b in range(B):
                    sp.dma_start(one(o_dram[b], blk * T, T), otm[b * T:(b + 1) * T].rearrange("t h a v -> t (h a v)")
                                 ).then_inc(o_stored, 16)

            sp.sem_inc(o_stored, 1)
            sp.sem_inc(out_stored, 1)
            load_steps(0)
            for dst, src in ((w_kv, wkv), (w_f1, wf1), (w_g, wg), (w_q, wqr), (w_o1, wo1), (w_out, wout)):
                sp.dma_start(dst[:, :, :], chunked(src)).then_inc(attn_w_in, 16)
            sp.dma_start(w_f2[:, :], wf2).then_inc(attn_w_in, 16)
            sp.dma_start(w_o2[:, :], wo2).then_inc(attn_w_in, 16)
            for b in range(B):
                sp.dma_start(hT[:, 0:KC, b * SK:(b + 1) * SK], chunked(ctxT[b])).then_inc(ctx_in, 16)
            sp.dma_start(hT[:, 2:4, 0:D], chunked(ckT)).then_inc(ctx_in, 16)
            sp.dma_start(hT[:, 4:6, 0:D], chunked(cvT)).then_inc(ctx_in, 16)
            for dst, src in ((c_q, cqT), (c_o, coT), (cent, centT)):
                sp.dma_start(dst[:, :, :], chunked(src)).then_inc(xattn_w_in, 16)
            sp.dma_start(c_bo[:, :], row(cbo)).then_inc(xattn_w_in, 16)
            sp.dma_start(r_bias[:, :], row(rbias)).then_inc(xattn_w_in, 16)
            sp.dma_start(lnw[:, :], row(ln_w).to_broadcast([G, D])).then_inc(xattn_w_in, 16)
            load_tile(0)
            load_expert(0, 0)
            load_steps(1)

            with sp.Fori(1, FREE) as it:
                sp.wait_ge(ln_out, it * 8 - 4)
                load_tile(it)

            def iterations(ep, par, keep):
                with sp.Fori(0, PAIRS) as pr:
                    it = pr + (ep * (2 * PAIRS) + par * PAIRS)
                    load_steps(it + 2)
                    if keep:
                        store_o(it)

            def expert_pair(ep, keep, last=False):
                sp.wait_ge(y_ps, ep * (2 * FREE * B) + 1)
                load_expert(ep * 2 + 1, 1)
                iterations(ep, 0, keep)
                if not last:
                    sp.wait_ge(y_ps, ep * (2 * FREE * B) + FREE * B)
                    load_expert(ep * 2 + 2, 0)
                iterations(ep, 1, keep)

            with sp.Fori(0, KEEP_EP) as ep:
                expert_pair(ep, False)
            expert_pair(3, True)
            expert_pair(4, True, last=True)
            store_o(NBLK - 2)
            store_o(NBLK - 1)

            with sp.Fori(0, FREE) as it:
                store_tile(it, it + (LN_LAST_FREE + 1))

            sp.wait_ge(o_stored, (NBLK - KEEP_IT) * B * 16 + 1)
            with sp.Fori(0, BOUND) as j:
                sp.wait_ge(ln_out, j * 12 + 4 * LN_BOUND)
                load_tile(j + FREE)
                for b in range(B):
                    sp.dma_start(att[:, b], one(o_dram[b], j * G + O_FIRST, G)).then_inc(bound_in, 16)

            with sp.Fori(0, NE // 2 - 1) as k:
                sp.wait_ge(y_ps, k * (2 * BOUND * B) + (NE * FREE * B + BOUND * B))
                load_expert(k * -2 + (NE - 3), 1)
                sp.wait_ge(y_ps, k * (2 * BOUND * B) + (NE * FREE * B + 2 * BOUND * B))
                load_expert(k * -2 + (NE - 4), 0)
            with sp.Fori(0, BOUND) as j:
                store_tile(j + FREE, j + (LN_LAST_BOUND + 1))
            sp.wait_ge(out_stored, 16 * TILES + 1)

        @block.tensor
        def _(pe):
            mm = nc.tensor.matmul

            def prep_first(blk):
                pe.wait_ge(xt_in, blk * 32 + 32)
                if later(blk):
                    pe.wait_ge(prep_act2, blk * 3)
                xt = [xtp[:, c].rearrange("p b t -> p (b t)") for c in range(KC)]
                for c in range(KC):
                    i = mm(ps[:, 7, 384:400], xt[c], w_g[:, c], start=c == 0, stop=c == KC - 1)
                i.then_inc(prep_ps, 1)
                for c in range(KC):
                    i = mm(ps[0:HD, 7, 256:384], w_f1[:, c], xt[c], start=c == 0, stop=c == KC - 1)
                i.then_inc(prep_ps, 1)
                for c in range(KC):
                    i = mm(ps[:, 6, :], xt[c], w_kv[:, c], start=c == 0, stop=c == KC - 1)
                i.then_inc(prep_ps, 1)

            def prep_second(blk):
                pe.wait_ge(prep_act, blk * 4 + 2)
                mm(ps[:, 7, 0:D], xf1T[:, :], w_f2[:, :], start=True, stop=True).then_inc(prep_ps2, 1)
                pe.wait_ge(prep_act, blk * 4 + 4)
                xt = [xtp[:, c].rearrange("p b t -> p (b t)") for c in range(KC)]
                for c in range(KC):
                    i = mm(ps[:, 6, 0:D], xt[c], w_q[:, c], start=c == 0, stop=c == KC - 1)
                i.then_inc(prep_ps2, 1)

            def turn(src, ready, done, base_ready):
                for c in range(KC):
                    for b in range(B):
                        if c == 0:
                            pe.wait_ge(ready, base_ready + (b + 1))
                        i = nc.tensor.transpose(ps[:, 4 + c, b * G:(b + 1) * G], src[:, b, c * P:(c + 1) * P],
                                                ident[0:G, 0:G])
                    i.then_inc(done, 1)

            def attention_rows(j):
                it = j + FREE
                pe.wait_ge(x2T_sb, it * 2)
                pe.wait_ge(rt_sb, it)
                pe.wait_ge(tile_in, it * 16 + 16)
                for c in range(KC):
                    for b in range(B):
                        i = nc.tensor.transpose(ps[:, 4 + c, b * G:(b + 1) * G], xin[:, b, c * P:(c + 1) * P],
                                                ident[0:G, 0:G])
                    i.then_inc(gx_ps, 1)
                pe.wait_ge(gx_sb, j * 2 + 2)
                for c in range(KC):
                    i = mm(ps[0:HD, 6, 0:W], w_o1[:, c], xtf[:, c], start=c == 0, stop=c == KC - 1)
                i.then_inc(xo1_ps, 1)
                pe.wait_ge(xo1_sb, j + 1)
                for b in range(B):
                    i = mm(ps[0:G, b // 2, (b % 2) * D:(b % 2 + 1) * D], xo1T[:, b * G:(b + 1) * G], w_o2[:, :],
                           start=True, stop=True)
                i.then_inc(gate_ps, 1)
                turn(att, weighted, gT_ps, j * 4)
                pe.wait_ge(gT_sb, j * 2 + 2)
                for b in range(B):
                    for c in range(KC):
                        i = mm(ps[0:G, 6 + b // 2, (b % 2) * D:(b % 2 + 1) * D], attT[:, c, b * G:(b + 1) * G],
                               w_out[:, c], start=c == 0, stop=c == KC - 1)
                i.then_inc(wout_ps, 1)

            def scores(it, b):
                pe.wait_ge(capped, it * 4 + (b + 1))
                for q in range(H // QH):
                    c, h = q // 2, (q % 2) * QH
                    i = mm(ps[0:G, q, 0:QH * SK], qT[:, c, b * G:(b + 1) * G],
                           keys[:, c, b, h:h + QH].rearrange("p h k -> p (h k)"), start=True, stop=True)
                i.then_inc(sc_ps, 1)

            def weights_turned(it, b):
                pe.wait_ge(exp_done, it * 4 + (b + 1))
                for q in range(H // QH):
                    if q == 3:
                        pe.wait_ge(eT_sb, it * 16 + (4 * b + 1))
                    for h in range(QH):
                        i = nc.tensor.transpose(ps[0:SK, 4 + q % 3, h * G:(h + 1) * G],
                                                probs[:, b % 2, q * QH + h], ident[0:G, 0:G])
                    i.then_inc(eT_ps, 1)

            def weighted_values(it, b):
                pe.wait_ge(eT_sb, it * 16 + (4 * b + 4))
                pe.wait_ge(att_done, it * 4 + (b + 1))
                for h in range(H):
                    i = mm(ps[0:G, 7, h * (HD + 1):(h + 1) * (HD + 1)], eT[:, h], vals[:, b, h],
                           start=True, stop=True)
                i.then_inc(av_ps, 1)

            def tile(it, norm1):
                turn(x1, ln_out, x1T_ps, norm1 * 4)
                pe.wait_ge(x1T_sb, it * 2 + 2)
                for half in range(KC):
                    for c in range(KC):
                        i = mm(ps[:, 6 + half, 0:W], c_q[:, c, half * P:(half + 1) * P], xtf[:, c],
                               start=c == 0, stop=c == KC - 1)
                    i.then_inc(q_ps, 1)
                pe.wait_ge(q_sb, it * 2 + 2)
                scores(it, 0)
                for b in range(B):
                    if b + 1 < B:
                        scores(it, b + 1)
                    weights_turned(it, b)
                    weighted_values(it, b)
                turn(att, att_done, attT_ps, it * 4 + 1)
                pe.wait_ge(attT_sb, it * 2 + 2)
                for b in range(B):
                    o = ps[0:G, 6 + b // 2, (b % 2) * D:(b % 2 + 1) * D]
                    mm(o, ones[:, 0:G], c_bo[:, :], start=True, stop=False)
                    for c in range(KC):
                        i = mm(o, attT[:, c, b * G:(b + 1) * G], c_o[:, c], start=False, stop=c == KC - 1)
                    i.then_inc(wo_ps, 1)
                turn(x2, ln_out, x2T_ps, norm1 * 4 + 4)
                pe.wait_ge(x2T_sb, it * 2 + 2)
                for b in range(B):
                    for biased in range(2):
                        o = ps[0:G, 0, (2 * b + biased) * NR:(2 * b + biased + 1) * NR]
                        for c in range(KC):
                            i = mm(o, attT[:, c, b * G:(b + 1) * G], cent[:, c], start=c == 0,
                                   stop=c == KC - 1 and not biased)
                        if biased:
                            i = mm(o, ones[:, 0:G], r_bias[:, :], start=False, stop=True)
                i.then_inc(rt_ps, 1)

            def up(unit, m, par):
                for g in range(FG):
                    pe.wait_ge(gelu_done, unit * FG + (g + 1))
                    for c in range(KC):
                        i = mm(ps[:, g % 2, 0:W], fc[:, par, c, g * P:(g + 1) * P],
                               x2T[:, m, c] if isinstance(m, int) else
                               x2T[:, bass.ds(m, 1), c].rearrange("p m w -> p (m w)"),
                               start=c == 0, stop=c == KC - 1)
                    i.then_inc(fc_ps, 1)

            def down(unit, pos, par):
                for b in range(B):
                    pe.wait_ge(y_used, unit * B + (b // 2 * 2 + 2))
                    for g in range(FG):
                        if b == 0:
                            pe.wait_ge(gelu_done, unit * FG + (g + 3))
                        i = mm(ps[0:G, 2 + 2 * pos + b // 2, (b % 2) * D:(b % 2 + 1) * D],
                               hT[:, g, b * G:(b + 1) * G], pj[:, par, g], start=g == 0, stop=g == FG - 1)
                    i.then_inc(y_ps, 1)

            pe.wait_ge(pool_const, 1)
            pe.wait_ge(attn_w_in, 8 * 16)
            prep_first(0)
            prep_second(0)
            pe.wait_ge(ctx_in, 6 * 16)
            for half in range(KC):
                for c in range(KC):
                    i = mm(ps[:, half, 0:B * SK], hT[:, 2 + c, half * P:(half + 1) * P], hT[:, c, 0:B * SK],
                           start=c == 0, stop=c == KC - 1)
                i.then_inc(ctx_k_ps, 1)
            for b in range(B):
                for c in range(KC):
                    i = mm(ps[0:SK, 2 + b // 2, (b % 2) * D:(b % 2 + 1) * D], hT[:, c, b * SK:(b + 1) * SK],
                           hT[:, 4 + c, 0:D], start=c == 0, stop=c == KC - 1)
                i.then_inc(ctx_v_ps, 1)
            pe.wait_ge(xattn_w_in, 6 * 16)
            pe.wait_ge(ctx_done, KC + B)
            pe.wait_ge(prep_act2, 3)
            with pe.Fori(0, FREE) as it:
                tile(it, it * 2)

            pe.wait_ge(rt_sb, FREE)

            def expert_pair(ep):
                for par in range(2):
                    with pe.Fori(0, PAIRS) as pr:
                        pe.wait_ge(expert_in[par], ep * 32 + 32)
                        it = pr + (ep * (2 * PAIRS) + par * PAIRS)
                        prep_first(it + 1)
                        up(it * 2, pr * 2, par)
                        prep_second(it + 1)
                        down(it * 2, 0, par)
                        up(it * 2 + 1, pr * 2 + 1, par)
                        down(it * 2 + 1, 1, par)

            with pe.Fori(0, NE // 2) as ep:
                expert_pair(ep)
            prep_first(NBLK - 1)
            prep_second(NBLK - 1)

            with pe.Fori(0, BOUND) as j:
                attention_rows(j)
                tile(j + FREE, j * 3 + (LN_BOUND + 1))
            pe.wait_ge(rt_sb, TILES)
            with pe.Fori(0, NE // 2) as k:
                for n, par in ((0, 1), (1, 0)):
                    pe.wait_ge(expert_in[par], k * 32 + 32 * (NE // 2))
                    for m in range(BOUND):
                        unit = k * (2 * BOUND) + (NE * FREE + n * BOUND + m)
                        up(unit, m, par)
                        down(unit, (n * BOUND + m) % 2, par)

        @block.scalar
        def _(act):
            fn = nc.scalar.activation

            def prep_first(blk):
                act.wait_ge(prep_ps, blk * 3 + 2)
                fn(xf1T[:, :], ps[0:HD, 7, 256:384], ACT.Copy).then_inc(prep_act, 1)
                if later(blk):
                    act.wait_ge(prep_pool, blk * PREP)
                fn(beta[:, :], ps[:, 7, 384:400], ACT.Sigmoid).then_inc(prep_act, 1)
                act.wait_ge(prep_ps, blk * 3 + 3)
                kv = ps[:, 6, :].rearrange("p (c d) -> p c d", c=2)
                fn(raw[:, 0:2], kv, ACT.Copy).then_inc(prep_act, 1)
                fn(sig[:, 0:2], kv, ACT.Sigmoid).then_inc(prep_act, 1)

            def prep_second(blk):
                act.wait_ge(prep_ps2, blk * 2 + 1)
                if later(blk):
                    act.wait_ge(block_laid, blk * LAY)
                fn(tm[:, 3], ps[:, 7, 0:D], ACT.Sigmoid).then_inc(prep_act2, 1)
                act.wait_ge(prep_ps2, blk * 2 + 2)
                fn(raw[:, 2], ps[:, 6, 0:D], ACT.Copy).then_inc(prep_act2, 1)
                fn(sig[:, 2], ps[:, 6, 0:D], ACT.Sigmoid).then_inc(prep_act2, 1)

            def out_of_banks(dst, ready, done, base, scale=1.0, first=4):
                for c in range(KC):
                    act.wait_ge(ready, base + (c + 1))
                    fn(dst[:, c], ps[:, first + c, 0:W], ACT.Copy, scale=scale).then_inc(done, 1)

            def attention_rows(j):
                out_of_banks(xtf, gx_ps, gx_sb, j * 2)
                act.wait_ge(xo1_ps, j + 1)
                act.wait_ge(comb_done, j * 3 + FREE * 3)
                fn(xo1T[:, :], ps[0:HD, 6, 0:W], ACT.Copy).then_inc(xo1_sb, 1)
                act.wait_ge(gate_ps, j + 1)
                fn(gate[:, :, :].rearrange("g (a b) d -> g a (b d)", a=2), ps[0:G, 0:2, :], ACT.Sigmoid
                   ).then_inc(gate_sb, 1)
                out_of_banks(attT, gT_ps, gT_sb, j * 2)

            def exps(it, b):
                act.wait_ge(shifted, it * 4 + (b + 1))
                fn(probs[:, b % 2], probs[:, b % 2], ACT.Exp).then_inc(exp_done, 1)

            def weights_out(it, b):
                for q in range(H // QH):
                    act.wait_ge(eT_ps, it * 16 + (4 * b + q + 1))
                    fn(eT[:, q * QH:(q + 1) * QH].rearrange("k h g -> k (h g)"), ps[0:SK, 4 + q % 3, 0:W], ACT.Copy
                       ).then_inc(eT_sb, 1)

            def tile(it, slot, norm2):
                out_of_banks(xtf, x1T_ps, x1T_sb, it * 2)
                out_of_banks(qT, q_ps, q_sb, it * 2, QSCALE, 6)
                exps(it, 0)
                for b in range(B):
                    if b + 1 < B:
                        exps(it, b + 1) if b == 0 else None
                    weights_out(it, b)
                    if 0 < b + 1 < B - 1:
                        exps(it, b + 2)
                out_of_banks(attT, attT_ps, attT_sb, it * 2)
                act.wait_ge(ln_out, norm2 * 4 + 4)
                fn(acc[:, bass.ds(slot, 1)].rearrange("g m b d -> g (m b d)"), x2[:, :, :].rearrange("g b d -> g (b d)"),
                   ACT.Copy, scale=2.0).then_inc(acc_set, 1)
                for c in range(KC):
                    act.wait_ge(x2T_ps, it * 2 + (c + 1))
                    fn(x2T[:, bass.ds(slot, 1), c].rearrange("p m w -> p (m w)"), ps[:, 4 + c, 0:W], ACT.Copy
                       ).then_inc(acc_set, 1)
                    fn(attT[:, c], ps[:, 4 + c, 0:W], ACT.Copy).then_inc(x2T_sb, 1)
                act.wait_ge(rt_ps, it + 1)
                fn(rt[:, :, :].rearrange("g b e -> g (b e)"), ps[0:G, 0, 0:B * 2 * NR], ACT.Sigmoid).then_inc(rt_sb, 1)
                act.wait_ge(route, it * 14 + 14)
                fn(rone[:, 5], rone[:, 4], ACT.Sigmoid).then_inc(w_done, 1)
                fn(rone[:, 6], rone[:, 4], ACT.Sigmoid, scale=-1.0).then_inc(w_done, 1)

            def gelus(unit):
                for g in range(FG):
                    act.wait_ge(fc_ps, unit * FG + (g + 1))
                    fn(hT[:, g], ps[:, g % 2, 0:W], ACT.Gelu).then_inc(gelu_done, 1)

            act.sem_inc(gelu_done, 2)
            prep_first(0)
            prep_second(0)
            with act.Fori(0, FREE) as it:
                tile(it, it, it * 2 + 1)
            with act.Fori(0, ITERS) as it:
                prep_first(it + 1)
                gelus(it * 2)
                prep_second(it + 1)
                gelus(it * 2 + 1)
            prep_first(NBLK - 1)
            prep_second(NBLK - 1)
            with act.Fori(0, BOUND) as j:
                attention_rows(j)
                tile(j + FREE, j, j * 3 + (LN_BOUND + 2))
            with act.Fori(NE * FREE, NE * TILES) as unit:
                gelus(unit)

        @block.gpsimd
        def _(pool):
            tt = nc.gpsimd.tensor_tensor

            def rsqrt(norm):
                pool.wait_ge(ln_mv, norm * B + B)
                tt(rstd[:, :], mv[:, :, 1], ln_eps[0:G, 0:B], ALU.add).then_inc(ln_rstd, 1)
                pool.wait_ge(ln_rstd, norm * 2 + 1)
                tt(rstd[:, :], rstd[:, :], neg_half[0:G, 0:B], ALU.pow).then_inc(ln_rstd, 1)

            def shifts(it):
                for b in range(B):
                    pool.wait_ge(max_done, it * B + (b + 1))
                    tt(probs[:, b % 2], probs[:, b % 2], mx[:, b % 2].unsqueeze(2).to_broadcast([G, H, SK]), ALU.subtract
                       ).then_inc(shifted, 1)

            heads = lambda a: a.rearrange("p (h d) -> p h d", h=H)
            by_head = lambda a: a.unsqueeze(2).to_broadcast([P, H, HD])

            def preparations(blk):

                def tree_sum(src, dst):
                    return [lambda: tt(tree[:, :, 0:8], heads(src)[:, :, 0:8], heads(src)[:, :, 8:16], ALU.add),
                            lambda: tt(tree[:, :, 0:4], tree[:, :, 0:4], tree[:, :, 4:8], ALU.add),
                            lambda: tt(tree[:, :, 0:2], tree[:, :, 0:2], tree[:, :, 2:4], ALU.add),
                            lambda: tt(dst, tree[:, :, 0], tree[:, :, 1], ALU.add)]

                def k_raw():
                    pool.wait_ge(prep_act, blk * 4 + 4)
                    return tt(kraw[:, :], raw[:, 0], sig[:, 0], ALU.mult)

                def v_silu():
                    if later(blk):
                        pool.wait_ge(block_laid, blk * LAY)
                    return tt(tm[:, 4], raw[:, 1], sig[:, 1], ALU.mult)

                def f_k():
                    pool.wait_ge(prep_act2, blk * 3 + 1)
                    return tt(fk[:, :], tm[:, 3], tm[:, 1], ALU.mult)

                def minus_beta():
                    pool.wait_ge(prep_act, blk * 4 + 2)
                    return tt(hsum[:, 3], beta[:, :], neg_one[:, :], ALU.mult)

                def q_silu():
                    pool.wait_ge(prep_act2, blk * 3 + 3)
                    return tt(tm[:, 5], raw[:, 2], sig[:, 2], ALU.mult)

                def norm_floor():
                    pool.sem_inc(sum_seen, 1)
                    return nc.gpsimd.tensor_scalar(hsum[:, 0], hsum[:, 0], NORM_EPS * NORM_EPS, None, ALU.max)

                ops = [k_raw, v_silu, lambda: tt(ksq[:, :], kraw[:, :], kraw[:, :], ALU.mult)]
                ops += tree_sum(ksq[:, :], hsum[:, 0])
                ops += [norm_floor,
                        lambda: tt(hsum[:, 1], hsum[:, 0], neg_half[:, :], ALU.pow),
                        lambda: tt(heads(tm[:, 1]), heads(kraw[:, :]), by_head(hsum[:, 1]), ALU.mult),
                        f_k, lambda: tt(ksq[:, :], fk[:, :], tm[:, 1], ALU.mult)]
                ops += tree_sum(ksq[:, :], hsum[:, 2])
                ops += [minus_beta,
                        lambda: tt(hsum[:, 2], hsum[:, 2], hsum[:, 3], ALU.mult),
                        lambda: tt(heads(tm[:, 0]), heads(fk[:, :]), by_head(hsum[:, 3]), ALU.mult),
                        lambda: tt(heads(ksq[:, :]), heads(tm[:, 1]), by_head(hsum[:, 2]), ALU.mult),
                        lambda: tt(ksq[:, :], ksq[:, :], fk[:, :], ALU.add),
                        lambda: tt(heads(tm[:, 2]), heads(ksq[:, :]), by_head(hsum[:, 3]), ALU.mult), q_silu]
                assert len(ops) == PREP
                return ops

            def prepare(blk, i, op):
                if i:
                    pool.wait_ge(prep_pool, blk * PREP + i)
                op().then_inc(prep_pool, 1)

            def steps(blk, keep, following):
                ops = list(enumerate(preparations(following))) if following is not None else []
                def place_v(t):
                    nc.gpsimd.tensor_copy(prod[:, t % 2, 1, :, HD], vrec[:, :, t]).then_inc(v_placed, 1)

                pool.wait_ge(block_laid, blk * LAY + LAY)
                pool.sem_inc(block_seen, 1)
                place_v(0)
                for t in range(T):
                    for h in range(2):
                        pool.wait_ge(step_done, blk * (T * STEP) + (t * STEP + 1 + h))
                        tt(terms[:, h, 0], S[:, (t - 1) % RING, h * HC:(h + 1) * HC],
                           rec[:, 3, :, t].unsqueeze(1).to_broadcast([P, HC, HD]), ALU.mult).then_inc(decayed, 1)
                    if t + 1 < T:
                        place_v(t + 1)
                    if keep and t % 2:
                        pool.wait_ge(step_done, blk * (T * STEP) + (t * STEP + STEP + 2))
                        tt(oprod[:, (t - 1) % (2 * OG):(t - 1) % (2 * OG) + 2], S[:, (t - 1) % RING:(t - 1) % RING + 2],
                           rec[:, 4, :, t - 1:t + 1].rearrange("p d t -> p t d").unsqueeze(2).to_broadcast([P, 2, HV, HD]),
                           ALU.mult).then_inc(o_terms, 1)
                    if t >= 4 and ops:
                        i, op = ops.pop(0)
                        prepare(following, i, op)

            nc.gpsimd.memset(ident[:, :], 0.0).then_inc(pool_set, 1)
            nc.gpsimd.memset(ones[:, :], 1.0).then_inc(pool_set, 1)
            nc.gpsimd.memset(head_mask[:, :], 1.0).then_inc(pool_set, 1)
            for const, value in ((neg_half, -0.5), (neg_one, -1.0), (ln_eps, LN_EPS)):
                nc.gpsimd.memset(const[:, :], value).then_inc(pool_set, 1)
            nc.gpsimd.iota(index8[:, :], pattern=[[1, NR]], base=-NR, channel_multiplier=0,
                           allow_small_or_imprecise_dtypes=True).then_inc(pool_set, 1)
            pool.wait_ge(pool_set, 7)
            nc.gpsimd.affine_select(out=head_mask[:, :], in_=head_mask[:, :], compare_op=ALU.is_ge, fill=0.0, base=0,
                                    pattern=[[-HD, 8]], channel_multiplier=1).then_inc(pool_set, 1)
            pool.wait_ge(pool_set, 8)
            nc.gpsimd.affine_select(out=head_mask[:, :], in_=head_mask[:, :], compare_op=ALU.is_ge, fill=0.0, base=HD - 1,
                                    pattern=[[HD, 8]], channel_multiplier=-1).then_inc(pool_set, 1)
            pool.wait_ge(pool_set, 9)
            nc.gpsimd.affine_select(out=ident[:, :], in_=ident[:, :], compare_op=ALU.not_equal, fill=1.0, base=0,
                                    pattern=[[-1, P]], channel_multiplier=1).then_inc(pool_const, 1)
            for i, op in enumerate(preparations(0)):
                prepare(0, i, op)
            with pool.Fori(0, FREE) as it:
                rsqrt(it * 2)
                shifts(it)
                rsqrt(it * 2 + 1)
            with pool.Fori(0, KEEP_IT) as it:
                steps(it, False, it + 1)
            with pool.Fori(KEEP_IT, NBLK - 1) as it:
                steps(it, True, it + 1)
            steps(NBLK - 1, True, None)
            with pool.Fori(LN_LAST_FREE, LN_BOUND) as norm:
                rsqrt(norm)
            with pool.Fori(0, BOUND) as j:
                rsqrt(j * 3 + LN_BOUND)
                rsqrt(j * 3 + (LN_BOUND + 1))
                shifts(j + FREE)
                rsqrt(j * 3 + (LN_BOUND + 2))
            with pool.Fori(LN_LAST_BOUND, LN_LAST_BOUND + BOUND) as norm:
                rsqrt(norm)

        @block.vector
        def _(dve):
            tt = nc.vector.tensor_tensor

            def layer_norm(norm, src, dst):
                for b in range(B):
                    nc.vector.bn_stats(stats[:, b], src(b)).then_inc(ln_stats, 1)
                dve.wait_ge(ln_stats, norm * B + B)
                dve.sem_inc(stats_seen, 1)
                for b in range(B):
                    nc.vector.bn_aggr(mv[:, b], stats[:, b]).then_inc(ln_mv, 1)
                dve.wait_ge(ln_rstd, norm * 2 + 2)
                for b in range(B):
                    nc.vector.tensor_scalar(dst(b), src(b), mv[:, b, 0:1], rstd[:, b:b + 1], ALU.subtract, ALU.mult
                                            ).then_inc(ln_out, 1)

            def attention_rows(j):
                dve.wait_ge(gate_sb, j + 1)
                dve.wait_ge(bound_in, j * (B * 16) + B * 16)
                tt(att[:, :, :], att[:, :, :], gate[:, :, :], ALU.mult).then_inc(gated, 1)
                dve.wait_ge(gated, j + 1)
                layer_norm(j * 3 + LN_BOUND, lambda b: att[:, b], lambda b: att[:, b])
                for b in range(B):
                    dve.wait_ge(ln_out, j * 12 + (LN_BOUND * B + b + 1))
                    tt(att[:, b], att[:, b], lnw[:, :], ALU.mult).then_inc(weighted, 1)
                dve.wait_ge(wout_ps, j + 1)
                tt(xin[:, :, :].rearrange("g (a b) d -> g a (b d)", a=2), ps[0:G, 6:8, :],
                   xin[:, :, :].rearrange("g (a b) d -> g a (b d)", a=2), ALU.add).then_inc(x_plus, 1)
                dve.wait_ge(x_plus, j + 1)

            def cap_and_max(it, b):
                p = probs[:, b % 2]
                dve.wait_ge(sc_ps, it * B + (b + 1))
                tt(p.rearrange("g (q h) k -> g q h k", q=H // QH),
                   ps[0:G, 0:4, 0:QH * SK].rearrange("g q (h k) -> g q h k", h=QH),
                   cap[:, b].unsqueeze(1).unsqueeze(1).to_broadcast([G, H // QH, QH, SK]), ALU.min).then_inc(capped, 1)
                dve.wait_ge(capped, it * B + (b + 2))
                nc.vector.tensor_reduce(mx[:, b % 2], p, AX.X, ALU.max).then_inc(max_done, 1)

            def attended(it, b):
                o = ps[0:G, 7, 0:H * (HD + 1)].rearrange("g (h d) -> g h d", h=H)
                dve.wait_ge(av_ps, it * B + (b + 1))
                dve.wait_ge(att_done, it * B + (b + 1))
                nc.vector.reciprocal(rden[:, :], o[:, :, HD]).then_inc(rden_done, 1)
                dve.wait_ge(rden_done, it * B + (b + 1))
                tt(att[:, b].rearrange("g (h d) -> g h d", h=H), o[:, :, 0:HD],
                   rden[:, :].unsqueeze(2).to_broadcast([G, H, HD]), ALU.mult).then_inc(att_done, 1)

            def routing(it):
                raw_s, biased = rt[:, :, 0:NR], rt[:, :, NR:2 * NR]
                wide = lambda i: rone[:, i].unsqueeze(2).to_broadcast([G, B, NR])
                index = index8[:, :].unsqueeze(1).to_broadcast([G, B, NR])
                red = nc.vector.tensor_reduce
                n = 0

                def then(ins):
                    nonlocal n
                    n += 1
                    ins.then_inc(route, 1)
                    dve.wait_ge(route, it * 14 + n)

                dve.wait_ge(rt_sb, it + 1)
                for i, scores in ((0, biased), (3, rbuf[:, 3])):
                    top, first, eq, cand, hot = rone[:, i // 3 * 2], rone[:, i // 3 * 2 + 1], rbuf[:, i // 3 * 4], \
                        rbuf[:, i // 3 * 4 + 1], rbuf[:, i // 3 * 4 + 2]
                    then(red(top, scores, AX.X, ALU.max))
                    then(tt(eq, scores, wide(i // 3 * 2), ALU.is_equal))
                    then(tt(cand, eq, index, ALU.mult))
                    then(red(first, cand, AX.X, ALU.min))
                    then(tt(hot, index, wide(i // 3 * 2 + 1), ALU.is_equal))
                    if i == 0:
                        then(nc.vector.scalar_tensor_tensor(rbuf[:, 3], rbuf[:, 2], -4.0, biased, ALU.mult, ALU.add))
                then(tt(rbuf[:, 7], rbuf[:, 2], rbuf[:, 6], ALU.subtract))
                then(tt(rbuf[:, 7], rbuf[:, 7], raw_s, ALU.mult))
                then(red(rone[:, 4], rbuf[:, 7], AX.X, ALU.add))
                assert n == 14
                dve.wait_ge(w_done, it * 2 + 2)
                tt(rbuf[:, 0], rbuf[:, 2], wide(5), ALU.mult).then_inc(comb_done, 1)
                tt(rbuf[:, 1], rbuf[:, 6], wide(6), ALU.mult).then_inc(comb_done, 1)
                dve.wait_ge(comb_done, it * 3 + 2)
                tt(comb[:, NSH:NE, bass.ds(it, 1)].rearrange("g e m b -> g b (e m)"), rbuf[:, 0], rbuf[:, 1], ALU.add
                   ).then_inc(comb_done, 1)

            def tile(it, norm1):
                dve.wait_ge(mask_in, it * 16 + 16)
                nc.vector.tensor_scalar(cap[:, :, :], imask[:, :, :], 0.0, HUGE, ALU.not_equal, ALU.mult).then_inc(cap_half, 1)
                dve.wait_ge(cap_half, it + 1)
                nc.vector.tensor_scalar(cap[:, :, :], cap[:, :, :], MASKED, None, ALU.add).then_inc(cap_done, 1)
                dve.wait_ge(cap_done, it + 1)
                layer_norm(norm1, lambda b: xin[:, b], lambda b: x1[:, b])
                cap_and_max(it, 0)
                cap_and_max(it, 1)
                attended(it, 0)
                cap_and_max(it, 2)
                attended(it, 1)
                cap_and_max(it, 3)
                attended(it, 2)
                attended(it, 3)
                dve.wait_ge(wo_ps, it * B + B)
                flat = x1[:, :, :].rearrange("g (a b) d -> g a (b d)", a=2)
                tt(flat, ps[0:G, 6:8, :], flat, ALU.add).then_inc(resid, 1)
                dve.wait_ge(resid, it + 1)
                layer_norm(norm1 + 1, lambda b: x1[:, b], lambda b: x2[:, b])
                routing(it)

            def add_expert(unit, pos, e, m, b):
                dve.wait_ge(y_ps, unit * B + (b // 2 * 2 + 2))
                a = acc[:, m - FREE, b] if isinstance(m, int) else acc[:, bass.ds(m, 1), b].rearrange("g m d -> g (m d)")
                w = comb[:, bass.ds(e, 1), m, b:b + 1] if isinstance(m, int) else \
                    comb[:, bass.ds(e, 1), bass.ds(m, 1), b:b + 1].rearrange("g e m b -> g e (m b)")
                nc.vector.scalar_tensor_tensor(a, ps[0:G, 2 + 2 * pos + b // 2, (b % 2) * D:(b % 2 + 1) * D],
                                               w.rearrange("g e b -> g (e b)"), a, ALU.mult, ALU.add).then_inc(y_used, 1)

            def lay_out(blk):
                dve.wait_ge(prep_pool, blk * PREP + PREP)
                if later(blk):
                    dve.wait_ge(decayed, blk * (2 * T))
                    dve.wait_ge(step_done, blk * (T * STEP) + 2)
                for i, comp in ((0, 0), (1, 1), (2, 2), (3, 3), (4, 5)):
                    src = tm[:, comp].rearrange("p (h d) -> p d h", h=H).unsqueeze(3).to_broadcast([P, HD, H, 2])
                    nc.vector.transpose(rec[:, i], src).then_inc(block_laid, 1)
                nc.vector.transpose(vrec[:, :, :],
                                    tm[:, 4].rearrange("p (g v) -> p v g", v=HV)).then_inc(block_laid, 1)

            def outputs(blk, g):
                dve.wait_ge(o_terms, (blk - KEEP_IT) * (T // 2) + (g + 1) * (OG // 2))
                nc.vector.tensor_reduce(osum[:, g * OG:(g + 1) * OG].rearrange("p t v -> p (t v)"),
                                        oprod[:, g % 2 * OG:(g % 2 + 1) * OG].rearrange("p t v d -> p (t v) d"),
                                        AX.X, ALU.add).then_inc(o_sums, 1)

            def steps(blk, keep, between=None):
                base = blk * (T * STEP) + 2
                dve.wait_ge(block_laid, blk * LAY + LAY)
                for t in range(T):
                    at = base + t * STEP
                    for h in range(2):
                        cols = slice(h * HC, (h + 1) * HC)
                        dve.wait_ge(step_done, at + (h - 1))
                        tt(prod[:, t % 2, :, cols, 0:HD],
                           S[:, (t - 1) % RING, cols].unsqueeze(1).to_broadcast([P, 2, HC, HD]),
                           rec[:, 1:3, :, t].unsqueeze(2).to_broadcast([P, 2, HC, HD]), ALU.mult).then_inc(step_done, 1)
                    for h in range(2):
                        dve.wait_ge(step_done, at + (1 + h))
                        dve.wait_ge(v_placed, blk * T + (t + 1))
                        nc.vector.tensor_reduce(u[:, h], prod[:, t % 2, :, h * HC:(h + 1) * HC], AX.X, ALU.add
                                                ).then_inc(step_done, 1)
                    for h in range(2):
                        dve.wait_ge(step_done, at + (3 + h))
                        tt(terms[:, h, 1:3], u[:, h].unsqueeze(3).to_broadcast([P, 2, HC, HD]),
                           rec[:, 0:2, :, t].unsqueeze(2).to_broadcast([P, 2, HC, HD]), ALU.mult).then_inc(step_done, 1)
                    for h in range(2):
                        dve.wait_ge(step_done, at + (5 + h))
                        dve.wait_ge(decayed, blk * (2 * T) + (2 * t + h + 1))
                        nc.vector.tensor_reduce(S[:, t % RING, h * HC:(h + 1) * HC].rearrange("p v d -> p (v d)"),
                                                terms[:, h].rearrange("p n v d -> p (v d) n"), AX.X, ALU.add
                                                ).then_inc(step_done, 1)
                    if keep and t > OG and t % OG == OG // 2:
                        outputs(blk, t // OG - 1)
                    if between is not None:
                        between(t)
                if keep:
                    outputs(blk, T // OG - 1)
                    n = blk - KEEP_IT
                    dve.wait_ge(o_sums, n * (T // OG) + T // OG)
                    dve.wait_ge(o_stored, n * (B * 16) + 1)
                    nc.vector.transpose(otm[:, :, :, :].rearrange("p h a v -> p v (h a)"),
                                        osum[:, :, :].rearrange("p t v -> p v t")).then_inc(o_ready, 1)

            dve.sem_inc(capped, 1)
            dve.sem_inc(att_done, 1)
            dve.sem_inc(y_used, 2 * B)
            for h in range(2):
                nc.vector.memset(S[:, RING - 1, h * HC:(h + 1) * HC], 0.0).then_inc(step_done, 1)
            nc.vector.memset(prod[:, :, 0, :, HD], 0.0).then_inc(dve_const, 1)
            nc.vector.memset(vals[:, :, :, :], 1.0).then_inc(dve_const, 1)
            nc.vector.memset(comb[:, 0:NSH], 1.0).then_inc(dve_const, 1)
            dve.wait_ge(dve_const, 3)
            dve.wait_ge(pool_const, 1)
            for c in range(KC):
                dve.wait_ge(ctx_k_ps, c + 1)
                tt(keys[:, c], ps[:, c, 0:B * SK].rearrange("p (b k) -> p b k", b=B).unsqueeze(2).to_broadcast([P, B, 8, SK]),
                   head_mask[:, :].unsqueeze(1).unsqueeze(3).to_broadcast([P, B, 8, SK]), ALU.mult).then_inc(ctx_done, 1)
            for b in range(B):
                dve.wait_ge(ctx_v_ps, b // 2 * 2 + 2)
                nc.vector.tensor_copy(vals[:, b, :, 0:HD], ps[0:SK, 2 + b // 2, (b % 2) * D:(b % 2 + 1) * D].rearrange(
                    "k (h d) -> k h d", h=H)).then_inc(ctx_done, 1)
            lay_out(0)

            with dve.Fori(0, FREE) as it:
                dve.wait_ge(tile_in, it * 16 + 16)
                tile(it, it * 2)
            dve.wait_ge(comb_done, FREE * 3)

            def iteration(it, e, pr, keep):
                def between(t):
                    if 16 <= t < 16 + B:
                        add_expert(it * 2, 0, e, pr * 2, t - 16)
                    if t >= T - B:
                        add_expert(it * 2 + 1, 1, e, pr * 2 + 1, t - (T - B))
                steps(it, keep, between)
                lay_out(it + 1)

            for lo, hi, keep in ((0, KEEP_EP * 2, False), (KEEP_EP * 2, NE, True)):
                with dve.Fori(lo, hi) as e:
                    with dve.Fori(0, PAIRS) as pr:
                        iteration(pr + e * PAIRS, e, pr, keep)
            steps(NBLK - 2, True)
            lay_out(NBLK - 1)
            steps(NBLK - 1, True)

            dve.wait_ge(y_used, NE * FREE * B + 2 * B)
            with dve.Fori(0, FREE) as it:
                dve.wait_ge(out_stored, it * 16 + 1)
                layer_norm(it + LN_LAST_FREE, lambda b: acc[:, bass.ds(it, 1), b].rearrange("g m d -> g (m d)"),
                           lambda b: x1[:, b])
            dve.wait_ge(out_stored, FREE * 16 + 1)
            with dve.Fori(0, BOUND) as j:
                dve.wait_ge(tile_in, j * 16 + (FREE * 16 + 16))
                attention_rows(j)
                tile(j + FREE, j * 3 + (LN_BOUND + 1))
            dve.wait_ge(comb_done, TILES * 3)
            with dve.Fori(0, NE // 2) as k:
                for n in range(2):
                    for m in range(BOUND):
                        unit = k * (2 * BOUND) + (NE * FREE + n * BOUND + m)
                        for b in range(B):
                            add_expert(unit, (n * BOUND + m) % 2, k * -2 + (NE - 1 - n), FREE + m, b)
            dve.wait_ge(y_used, NE * TILES * B + 2 * B)
            with dve.Fori(0, BOUND) as j:
                dve.wait_ge(out_stored, j * 16 + (FREE * 16 + 1))
                layer_norm(j + LN_LAST_BOUND, lambda b: acc[:, bass.ds(j, 1), b].rearrange("g m d -> g (m d)"),
                           lambda b: x1[:, b])


def kernel(x, ctx_1024, mask_Bx1xSxS2_if1, L0_attn_Wq, L0_attn_Wk, L0_attn_Wv, L0_attn_Wf1, L0_attn_Wf2, L0_attn_Wg,
           L0_attn_Wo1, L0_attn_Wo2, L0_attn_ln_w, L0_attn_Wout, L0_xattn_Wq, L0_xattn_Wk, L0_xattn_Wv, L0_xattn_Wo,
           L0_xattn_bo, L0_ffn_centroids, L0_ffn_routing_bias, L0_ffn_Wfc_r, L0_ffn_Wproj_r, L0_ffn_Wfc_sh,
           L0_ffn_Wproj_sh):
    import numpy as np
    import concourse.bacc as bacc
    from concourse.bass_utils import run_bass_kernel_spmd as run

    x, mask = np.asarray(x), np.asarray(mask_Bx1xSxS2_if1)[:, 0]
    classes = [1, 2, 0]

    def tiled(a):
        padded = np.zeros((B, ROWS, a.shape[-1]), a.dtype)
        padded[:, :N] = a
        return padded.reshape(B, ROWS // 3, 3, -1)[:, :, classes].transpose(2, 1, 0, 3).reshape(TILES, G, B, -1)

    t = lambda a: np.swapaxes(np.asarray(a), -1, -2)
    arrays = dict(
        x=tiled(x), xT=t(x), ctxT=t(ctx_1024), mask=tiled(mask),
        wkv=np.concatenate([np.asarray(L0_attn_Wk), np.asarray(L0_attn_Wv)], 1), wqr=L0_attn_Wq, wf1=L0_attn_Wf1,
        wf2=L0_attn_Wf2, wg=L0_attn_Wg, wo1=L0_attn_Wo1, wo2=L0_attn_Wo2, ln_w=L0_attn_ln_w, wout=L0_attn_Wout,
        cqT=t(L0_xattn_Wq), ckT=t(L0_xattn_Wk), cvT=t(L0_xattn_Wv), coT=t(L0_xattn_Wo), cbo=L0_xattn_bo,
        centT=t(L0_ffn_centroids), rbias=L0_ffn_routing_bias,
        wfcT=t(np.concatenate([np.asarray(L0_ffn_Wfc_sh), np.asarray(L0_ffn_Wfc_r)])),
        wpT=t(np.concatenate([np.asarray(L0_ffn_Wproj_sh), np.asarray(L0_ffn_Wproj_r)])))
    arrays = {f"in_{k}": np.ascontiguousarray(v) for k, v in arrays.items()}
    nc = bacc.Bacc("TRN2", target_bir_lowering=False, num_devices=1)
    args = [nc.dram_tensor(k, a.shape, mybir.dt.from_np(a.dtype), kind="ExternalInput").ap() for k, a in arrays.items()]
    args.append(nc.dram_tensor("out_0", (TILES, G, B, D), F32, kind="ExternalOutput").ap())
    decoder_layer(nc, *args)
    r = run(nc, [arrays], core_ids=[0])
    rows = r.results[0]["out_0"].reshape(3, ROWS // 3, B, D)
    return rows[np.argsort(classes)].transpose(2, 1, 0, 3).reshape(B, ROWS, D)[:, :N]
```

```python
from contextlib import ExitStack

import concourse.bass as bass
from concourse import mybir

F32 = mybir.dt.float32
I32 = mybir.dt.int32
ALU = mybir.AluOpType
ACT = mybir.ActivationFunctionType
AX = mybir.AxisListType

B, N, D = 4, 1024, 256
H, HD = 16, 16
SK = 77
NSH, NR, F = 2, 8, 1024
NE = NSH + NR
P = 128
KC = D // P
FG = F // P
W = B * P
TILES = N // P
QH = 4
HV, HC = 8, 4
T = 32
NBLK = N // T
Q = 4
assert Q * T == P
O_FIRST = (3 * N - N) // 3
KEEP = O_FIRST // T
FIRST_BOUND = O_FIRST // P
RING = 4
OG = 4
MAX_PASSES = W // P
LN_EPS = 1e-5
NORM_EPS = 1e-12
QSCALE = HD ** -0.5
MASKED = 1e9 * QSCALE
HUGE = 3e38
FAR = 4096.0
PREP = 20
LAY = 6
STEP = 8
ROUTE = 26


def decoder_layer(nc, x, xT, ctxT, mask, wkv, wqr, wf1, wf2, wg, wo1, wo2, ln_w, wout,
                  cqT, ckT, cvT, coT, cbo, centT, rbias, wfcT, wpT, out):
    with ExitStack() as ctx:
        def sb(name, shape, dt=F32):
            return ctx.enter_context(nc.sbuf_tensor(name, shape, dt))

        def sem(name):
            return ctx.enter_context(nc.semaphore(name))

        ident, twice = sb("ident", [P, P]), sb("twice", [P, P])
        before, ones = sb("before", [P, P]), sb("ones", [P, P])
        slots = sb("slots", [P, W])
        head_mask = sb("head_mask", [P, 8])
        quad_mask = sb("quad_mask", [P, QH])
        neg_half, neg_one, ln_eps = sb("neg_half", [P, H]), sb("neg_one", [P, H]), sb("ln_eps", [P, H])
        index8 = sb("index8", [P, NR])
        pass_at = sb("pass_at", [1, MAX_PASSES])
        lower = sb("lower", [1, NR + 1, NR])
        w_kv = sb("w_kv", [P, KC, 2 * D])
        w_q = sb("w_q", [P, KC, D])
        w_f1 = sb("w_f1", [P, KC, HD])
        w_f2 = sb("w_f2", [HD, D])
        w_g = sb("w_g", [P, KC, H])
        w_o1 = sb("w_o1", [P, KC, HD])
        w_o2 = sb("w_o2", [HD, D])
        w_out = sb("w_out", [P, KC, D])
        lnw = sb("lnw", [P, D])
        c_q = sb("c_q", [P, KC, D])
        c_o = sb("c_o", [P, KC, D])
        c_bo = sb("c_bo", [1, D])
        cent = sb("cent", [P, KC, NR])
        r_bias = sb("r_bias", [1, NR])
        keys = sb("keys", [P, KC, B, QH, SK])
        vals = sb("vals", [SK, B, H, HD + 1])

        xin = sb("xin", [P, B, D])
        x1 = sb("x1", [P, B, D])
        xtf = sb("xtf", [P, KC, W])
        qT = sb("qT", [P, KC, W])
        att = sb("att", [P, B, D])
        imask = sb("imask", [P, B, SK], I32)
        cap = sb("cap", [P, B, SK])
        probs = sb("probs", [P, B, H, SK])
        least = sb("least", [P, B, H])
        eT = sb("eT", [SK, H, P])
        avs = sb("avs", [P, 2, H, HD + 1])
        rden = sb("rden", [P, H])
        stats = sb("stats", [P, B, 6])
        mv = sb("mv", [P, B, 2])
        rstd = sb("rstd", [P, B])
        gate = sb("gate", [P, B, D])
        x2 = gate
        xo1T = qT[0:HD, 0]
        o_rows = sb("o_rows", [P, B, D])

        rt = sb("rt", [P, B, 2 * NR])
        rbuf = sb("rbuf", [P, 8, B, NR])
        rone = sb("rone", [P, 8, B])
        chosen = sb("chosen", [P, B, NR])
        w_tok, neg_w = sb("w_tok", [P, B, NR]), sb("neg_w", [P, B, NR])
        neg_slot = sb("neg_slot", [P, B, NR])
        over = sb("over", [1, NR, MAX_PASSES])
        passes = sb("passes", [1, NR])
        lterm = sb("lterm", [1, NR + 1, NR])
        first_pass = sb("first_pass", [1, NR + 1])
        pass_base = sb("pass_base", [1, 1])
        bounds = sb("bounds", [1, NR + 1], I32)

        x2f = sb("x2f", [P, B, D])
        x2T = sb("x2T", [P, KC, W])
        fc = sb("fc", [P, 2, KC, F])
        pj = sb("pj", [P, 2, FG, D])
        hT = sb("hT", [P, FG, W])
        far = sb("far", [P, B, P])
        sel, sel_w = sb("sel", [P, B, P]), sb("sel_w", [P, B, P])
        selT = sb("selT", [P, B, P])
        xg = sb("xg", [P, KC, P])
        y = sb("y", [P, D])
        y_out = sb("y_out", [P, B, D])
        tiny = sb("tiny", [1, 1])

        xtp = sb("xtp", [P, 2, KC, B, T])
        xf1T = sb("xf1T", [HD, P])
        graw = sb("graw", [P, H])
        act3 = sb("act3", [P, 2, 3, D])
        fbuf = sb("fbuf", [P, 2, D])
        beta = sb("beta", [P, 2, H])
        ksq = sb("ksq", [P, D])
        fk = sb("fk", [P, D])
        tree = sb("tree", [P, H, 8])
        hsum = sb("hsum", [P, 4, H])
        tm = sb("tm", [P, 3, D])
        rec = sb("rec", [P, 5, HD, T])
        vrec = sb("vrec", [P, HV, T])
        prod = sb("prod", [P, 2, 2, HV, HD + 1])
        u = sb("u", [P, 2, 2, HC])
        terms = sb("terms", [P, 2, 3, HC, HD])
        S = sb("S", [P, RING, HV, HD])
        oprod = sb("oprod", [P, 2 * OG, HV, HD])
        osum = sb("osum", [P, T, HV])
        otm = sb("otm", [P, H, 2, HV])

        ps = ctx.enter_context(nc.psum_tensor("ps", [P, 8, 512], F32))
        ACC, UP, GATHER, A0, A1, PRE = 0, 2, 4, 5, 6, 7
        TURNED = UP, UP + 1, A0, A1

        (attn_w_in, xattn_w_in, ctx_in, xt_in0, xt_in1, expert_in0, expert_in1, tile_in, mask_in, o_stored, out_stored,
         pool_set, pool_const, dve_const, ctx_k_ps, ctx_v_ps, ctx_done, prep_a_ps, prep_b_ps, xf1_sb, fq_sb,
         kv_sb, sum_seen, prep_pool, block_laid, block_seen, v_placed, step_done, decayed, o_terms, o_sums, o_ready,
         cap_half, cap_done, x1T_ps, x1T_sb, q_ps, q_sb, sc_ps, sc_sb, capped, min_done, exp_done, eT_ps, eT_sb, av_ps,
         av_sb, rden_done, att_done, attT_ps, attT_sb, wo_ps, resid, x2T_ps, x2f_sb, x2T_sb, rt_ps, rt_sb, route,
         w_done, picked, pos_ps, bounds_done, bounds_seen_pe, bounds_seen_act, gx_ps, gx_sb, xo1_ps, xo1_sb, gate_ps,
         gate_sb, gated, weighted, gT_ps, gT_sb, wout_ps, x_plus, sh_ps, sh_gelu, expert_used0, expert_used1, acc_ps,
         acc_sb, warm, far_done, sel_done, selw_done, gather_ps, xg_sb, up_ps, gelu_done, selT_ps, selT_sb, y_ps, y_sb) = map(sem, """
            attn_w_in xattn_w_in ctx_in xt_in0 xt_in1 expert_in0 expert_in1 tile_in mask_in o_stored out_stored pool_set
            pool_const dve_const ctx_k_ps ctx_v_ps ctx_done prep_a_ps prep_b_ps xf1_sb fq_sb kv_sb sum_seen
            prep_pool block_laid block_seen v_placed step_done decayed o_terms o_sums o_ready cap_half cap_done x1T_ps
            x1T_sb q_ps q_sb sc_ps sc_sb capped min_done exp_done eT_ps eT_sb av_ps av_sb rden_done att_done attT_ps
            attT_sb wo_ps resid x2T_ps x2f_sb x2T_sb rt_ps rt_sb route w_done picked pos_ps bounds_done bounds_seen_pe
            bounds_seen_act gx_ps gx_sb xo1_ps xo1_sb gate_ps gate_sb gated weighted gT_ps gT_sb wout_ps x_plus sh_ps
            sh_gelu expert_used0 expert_used1 acc_ps acc_sb warm far_done sel_done selw_done gather_ps xg_sb up_ps
            gelu_done selT_ps selT_sb y_ps y_sb""".split())
        xt_in = xt_in0, xt_in1
        expert_in, expert_used = (expert_in0, expert_in1), (expert_used0, expert_used1)
        ln_stats, ln_seen, ln_mv, ln_rstd, ln_out = ([sem(f"{what}{kind}") for kind in range(4)] for what in
                                                     ("stats", "stats_seen", "mv", "rstd", "norm"))
        LN_GATE, LN_1, LN_2, LN_3 = range(4)

        xT_v = xT.rearrange("b (c p) t -> p c b t", p=P)
        wfc_v = wfcT.rearrange("e (c p) f -> e p c f", p=P)
        wp_v = wpT.rearrange("e (g p) d -> e p g d", p=P)

        def chunked(w):
            return w.rearrange("(c p) n -> p c n", p=P)

        def one(v, i, n=1):
            return v[i:i + n] if isinstance(i, int) else v[bass.ds(i, n)]

        def row(v):
            return v.rearrange("(a n) -> a n", a=1)

        def later(blk):
            return not isinstance(blk, int) or blk > 0

        def halves(t):
            return t.rearrange("g (a b) d -> g a (b d)", a=2)

        block = ctx.enter_context(nc.Block())

        @block.sync
        def _(sp):
            def load_xt(blk, par):
                if not isinstance(blk, int) or blk >= 2:
                    sp.wait_ge(prep_b_ps, blk - 1)
                for c in range(KC):
                    sp.dma_start(xtp[:, par, c], xT_v[:, c, :, blk * T:(blk + 1) * T] if isinstance(blk, int)
                                 else xT_v[:, c, :, bass.ds(blk * T, T)]).then_inc(xt_in[par], 16)

            def load_expert(i, order):
                sp.dma_start(fc[:, i % 2], wfc_v[order[i]]).then_inc(expert_in[i % 2], 16)
                sp.dma_start(pj[:, i % 2], wp_v[order[i]]).then_inc(expert_in[i % 2], 16)

            def load_tile(m):
                sp.dma_start(xin[:, :, :], one(x, m).rearrange("m g b d -> g (m b) d")).then_inc(tile_in, 16)
                sp.dma_start(imask[:, :, :], one(mask, m).rearrange("m g b k -> g (m b) k")).then_inc(mask_in, 16)

            def next_tile(m):
                sp.wait_ge(ln_out[LN_1], m * B)
                sp.wait_ge(cap_half, m)
                load_tile(m)

            def next_expert(m, i, order):
                sp.wait_ge(expert_used[i % 2], m * (NE // 2) + (i // 2 + 1))
                load_expert((i + 2) % NE, order)

            def store_tile(m):
                sp.wait_ge(ln_out[LN_3], m * B + B)
                sp.dma_start(one(out, m).rearrange("m g b d -> g (m b) d"), y_out[:, :, :]).then_inc(out_stored, 16)

            def store_o(blk):
                sp.wait_ge(o_ready, blk - (KEEP - 1))
                first = max(O_FIRST - blk * T, 0)
                at = blk % Q * T
                for b in range(B):
                    sp.dma_start(o_rows[at + first:at + T, b], otm[b * T + first:(b + 1) * T].rearrange("t h a v -> t (h a v)")
                                 ).then_inc(o_stored, 16)

            def period(p, f=None, tile=None, bound=False, blocks=Q, stores=(None,) * Q, final=False):
                def xt(q):
                    if q < blocks:
                        load_xt(p * Q + (Q + q), q % 2)

                def used(i):
                    if f is not None:
                        next_expert(f, i, BOUND_ORDER if bound else FREE_ORDER)

                def outputs(q):
                    if stores[q] is not None:
                        store_o(stores[q])

                xt(0)
                used(0)
                used(1)
                used(2)
                outputs(0)
                used(3)
                xt(1)
                if tile is not None:
                    next_tile(tile)
                used(4)
                outputs(1)
                used(5)
                xt(2)
                used(6)
                outputs(2)
                used(7)
                if not final:
                    used(8)
                    used(9)
                xt(3)
                outputs(3)

            sp.sem_inc(o_stored, 1)
            sp.sem_inc(out_stored, 1)
            load_xt(0, 0)
            for dst, src in ((w_f1, wf1), (w_g, wg), (w_kv, wkv), (w_q, wqr)):
                sp.dma_start(dst[:, :, :], chunked(src)).then_inc(attn_w_in, 16)
            sp.dma_start(w_f2[:, :], wf2).then_inc(attn_w_in, 16)
            load_xt(1, 1)
            for b in range(B):
                sp.dma_start(hT[:, 0:KC, b * SK:(b + 1) * SK], chunked(ctxT[b])).then_inc(ctx_in, 16)
            sp.dma_start(hT[:, 2:4, 0:D], chunked(ckT)).then_inc(ctx_in, 16)
            sp.dma_start(hT[:, 4:6, 0:D], chunked(cvT)).then_inc(ctx_in, 16)
            load_tile(0)
            for dst, src in ((c_q, cqT), (c_o, coT), (cent, centT), (w_o1, wo1), (w_out, wout)):
                sp.dma_start(dst[:, :, :], chunked(src)).then_inc(xattn_w_in, 16)
            sp.dma_start(w_o2[:, :], wo2).then_inc(xattn_w_in, 16)
            sp.dma_start(c_bo[:, :], row(cbo)).then_inc(xattn_w_in, 16)
            sp.dma_start(r_bias[:, :], row(rbias)).then_inc(xattn_w_in, 16)
            sp.dma_start(lnw[:, :], row(ln_w).to_broadcast([P, D])).then_inc(xattn_w_in, 16)
            load_xt(2, 0)
            load_xt(3, 1)
            load_expert(0, FREE_ORDER)
            load_expert(1, FREE_ORDER)

            period(0, tile=1)
            with sp.Fori(1, FIRST_BOUND) as p:
                period(p, p - 1, tile=p + 1)
                store_tile(p - 1)
            period(5, 4, stores=(None, None, 21, 22))
            store_o(23)
            store_tile(4)
            period(6, tile=6, stores=(24, 25, 26, 27))
            period(7, 5, tile=7, bound=True, blocks=0, stores=(28, 29, 30, 31))
            store_tile(5)
            period(8, 6, bound=True, blocks=0)
            store_tile(6)
            period(9, 7, blocks=0, final=True)
            store_tile(7)
            sp.wait_ge(out_stored, 16 * TILES + 1)

        @block.tensor
        def _(pe):
            mm = nc.tensor.matmul

            def prepare(pair, par):
                blk = pair * 2 + par
                xt = [xtp[:, par, c].rearrange("p b t -> p (b t)") for c in range(KC)]
                pe.wait_ge(xt_in[par], pair * (16 * KC) + 16 * KC)
                if later(blk):
                    pe.wait_ge(kv_sb, blk)
                for c in range(KC):
                    mm(ps[0:HD, PRE, 0:P], w_f1[:, c], xt[c], start=c == 0, stop=c == KC - 1)
                for c in range(KC):
                    i = mm(ps[:, PRE, P:P + H], xt[c], w_g[:, c], start=c == 0, stop=c == KC - 1)
                i.then_inc(prep_a_ps, 1)
                pe.wait_ge(xf1_sb, blk * 2 + 2)
                for c in range(KC):
                    i = mm(ps[:, A0, :], xt[c], w_kv[:, c], start=c == 0, stop=c == KC - 1)
                for c in range(KC):
                    i = mm(ps[:, A1, 0:D], xt[c], w_q[:, c], start=c == 0, stop=c == KC - 1)
                i = mm(ps[:, PRE, D:2 * D], xf1T[:, :], w_f2[:, :], start=True, stop=True)
                i.then_inc(prep_b_ps, 1)

            def turn(src, done):
                for c in range(KC):
                    for b in range(B):
                        i = nc.tensor.transpose(ps[:, A0 + c, b * P:(b + 1) * P], src[:, b, c * P:(c + 1) * P], ident[:, :])
                    i.then_inc(done, 1)

            def gate_rows(n):
                pe.wait_ge(tile_in, n * 16 + (FIRST_BOUND * 16 + 16))
                turn(xin, gx_ps)
                pe.wait_ge(gx_sb, n * 2 + 2)
                for c in range(KC):
                    i = mm(ps[0:HD, A0, :], w_o1[:, c], xtf[:, c], start=c == 0, stop=c == KC - 1)
                i.then_inc(xo1_ps, 1)
                pe.wait_ge(xo1_sb, n + 1)
                for b in range(B):
                    i = mm(ps[:, A0 + b // 2, (b % 2) * D:(b % 2 + 1) * D], xo1T[:, b * P:(b + 1) * P], w_o2[:, :],
                           start=True, stop=True)
                i.then_inc(gate_ps, 1)

            def project_rows(n):
                pe.wait_ge(weighted, n * B + B)
                turn(att, gT_ps)
                pe.wait_ge(gT_sb, n * 2 + 2)
                for b in range(B):
                    for c in range(KC):
                        i = mm(ps[:, A0 + b // 2, (b % 2) * D:(b % 2 + 1) * D], xtf[:, c, b * P:(b + 1) * P],
                               w_out[:, c], start=c == 0, stop=c == KC - 1)
                i.then_inc(wout_ps, 1)

            def queries(m):
                pe.wait_ge(ln_out[LN_1], m * B + B)
                turn(x1, x1T_ps)
                pe.wait_ge(x1T_sb, m * 2 + 2)
                for half in range(KC):
                    for c in range(KC):
                        i = mm(ps[:, A0 + half, :], c_q[:, c, half * P:(half + 1) * P], xtf[:, c],
                               start=c == 0, stop=c == KC - 1)
                    i.then_inc(q_ps, 1)
                pe.wait_ge(q_sb, m * 2 + 2)

            def scores(m):
                for b in range(B):
                    for half in range(2):
                        if b:
                            pe.wait_ge(sc_sb, m * (2 * B) + (2 * b + half - 1))
                        for g in range(2):
                            rows = slice(QH * HD * g, QH * HD * (g + 1))
                            i = mm(ps[:, (UP, A0)[half] + g, 0:QH * SK],
                                   qT[rows, half, b * P:(b + 1) * P], keys[rows, half, b].rearrange("p h k -> p (h k)"),
                                   start=True, stop=True)
                        i.then_inc(sc_ps, 1)

            def turn_weights(m, b):
                pe.wait_ge(exp_done, m * B + (b + 1))
                for q in range(H // QH):
                    for h in range(QH):
                        i = nc.tensor.transpose(ps[0:SK, TURNED[q], h * P:(h + 1) * P], probs[:, b, q * QH + h], ident[:, :])
                    i.then_inc(eT_ps, 1)

            def weigh_values(m, b):
                pe.wait_ge(eT_sb, m * (4 * B) + (4 * b + 4))
                if b:
                    pe.wait_ge(av_sb, m * B + b)
                for h in range(H):
                    i = mm(ps[:, GATHER, h * (HD + 1):(h + 1) * (HD + 1)], eT[:, h], vals[:, b, h], start=True, stop=True)
                i.then_inc(av_ps, 1)

            def project(m):
                pe.wait_ge(att_done, m * B + B)
                turn(att, attT_ps)
                pe.wait_ge(attT_sb, m * 2 + 2)
                for b in range(B):
                    o = ps[:, A0 + b // 2, (b % 2) * D:(b % 2 + 1) * D]
                    mm(o, ones[0:1, :], c_bo[:, :], start=True, stop=False)
                    for c in range(KC):
                        i = mm(o, xtf[:, c, b * P:(b + 1) * P], c_o[:, c], start=False, stop=c == KC - 1)
                i.then_inc(wo_ps, 1)

            def router(m):
                pe.wait_ge(ln_out[LN_2], m * B + B)
                turn(x2, x2T_ps)
                pe.wait_ge(x2T_sb, m * 2 + 2)
                for b in range(B):
                    for biased in range(2):
                        o = ps[:, A0, (2 * b + biased) * NR:(2 * b + biased + 1) * NR]
                        for c in range(KC):
                            i = mm(o, x2T[:, c, b * P:(b + 1) * P], cent[:, c], start=c == 0,
                                   stop=c == KC - 1 and not biased)
                        if biased:
                            i = mm(o, ones[0:1, :], r_bias[:, :], start=False, stop=True)
                i.then_inc(rt_ps, 1)

            def places(m):
                pe.wait_ge(picked, m + 1)
                n = B * NR
                for b in range(B):
                    o = ps[:, GATHER, b * NR:(b + 1) * NR]
                    for a in range(b):
                        mm(o, ones[:, :], chosen[:, a], start=a == 0, stop=False)
                    mm(o, before[:, :], chosen[:, b], start=b == 0, stop=True)
                for b in range(B):
                    i = mm(ps[:, GATHER, n:n + NR], ones[:, :], chosen[:, b], start=b == 0, stop=b == B - 1)
                i.then_inc(pos_ps, 1)

            def shared(m, i, e, between):
                par = i % 2
                pe.wait_ge(expert_in[par], m * (16 * NE) + 32 * (i // 2 + 1))
                if e == 0:
                    pe.wait_ge(x2T_sb, m * 2 + 2)
                for g in range(FG):
                    pe.wait_ge(sh_gelu, m * (2 * FG) + (e * FG + g + 1))
                    for c in range(KC):
                        ins = mm(ps[:, UP + g % 2, :], fc[:, par, c, g * P:(g + 1) * P], x2T[:, c],
                                 start=c == 0, stop=c == KC - 1)
                    ins.then_inc(sh_ps, 1)
                between()
                if e == 0:
                    pe.wait_ge(acc_sb, m * 2 + 1)
                for g in range(FG):
                    pe.wait_ge(sh_gelu, m * (2 * FG) + (e * FG + g + 3))
                    for b in range(B):
                        ins = mm(ps[:, ACC + b // 2, (b % 2) * D:(b % 2 + 1) * D], hT[:, g, b * P:(b + 1) * P], pj[:, par, g],
                                 start=e == 0 and g == 0 and b % 2 == 0, stop=False)
                ins.then_inc(expert_used[par], 1)

            def load_bounds(m):
                pe.wait_ge(bounds_done, m + 1)
                pe.sem_inc(bounds_seen_pe, 1)
                return [pe.value_load(bounds[0:1, e:e + 1], min_val=0, max_val=TILES * NR * MAX_PASSES)
                        for e in range(NR + 1)]

            def routed(m, place, lo, hi):
                par = place % 2
                pe.wait_ge(expert_in[par], m * (16 * NE) + 32 * (place // 2 + 1))
                with pe.If(lo < hi), pe.Fori(lo, hi) as n:
                    pe.wait_ge(sel_done, n + 1)
                    for c in range(KC):
                        for b in range(B):
                            i = mm(ps[:, GATHER, c * P:(c + 1) * P], x2f[:, b, c * P:(c + 1) * P], sel[:, b],
                                   start=b == 0, stop=b == B - 1)
                    i.then_inc(gather_ps, 1)
                    pe.wait_ge(selw_done, n * B + B)
                    for b in range(B):
                        i = nc.tensor.transpose(ps[:, PRE, b * P:(b + 1) * P], sel_w[:, b], ident[:, :])
                    i.then_inc(selT_ps, 1)
                    pe.wait_ge(xg_sb, n + 1)
                    for g in range(FG):
                        for c in range(KC):
                            i = mm(ps[:, UP + g // 4, g % 4 * P:(g % 4 + 1) * P], fc[:, par, c, g * P:(g + 1) * P], xg[:, c],
                                   start=c == 0, stop=c == KC - 1)
                        if g % 4 == 3:
                            i.then_inc(up_ps, 1)
                    for g in range(FG):
                        if g % 4 == 0:
                            pe.wait_ge(gelu_done, n * 2 + (g // 4 + 1))
                        i = mm(ps[:, UP, 0:D], hT[:, g, 0:P], pj[:, par, g], start=g == 0, stop=g == FG - 1)
                    i.then_inc(y_ps, 1)
                    pe.wait_ge(selT_sb, n + 1)
                    pe.wait_ge(y_sb, n + 1)
                    for b in range(B):
                        mm(ps[:, ACC + b // 2, (b % 2) * D:(b % 2 + 1) * D], selT[:, b], y[:, :], start=False, stop=False)
                pe.sem_inc(expert_used[par], 1)

            def residual(m):
                pe.wait_ge(x2f_sb, m + 1)
                for b in range(B):
                    i = mm(ps[:, ACC + b // 2, (b % 2) * D:(b % 2 + 1) * D], twice[:, :], x2f[:, b], start=False, stop=b % 2 == 1)
                i.then_inc(acc_ps, 1)

            def period(p, f=None, m=None, bound=False, preps=Q):
                order = BOUND_ORDER if bound else FREE_ORDER
                bnd = []

                def prep(q):
                    if q < preps:
                        prepare(p * (Q // 2) + (q // 2 + 1), q % 2)

                def expert(i, between=lambda: None):
                    e = order[i]
                    if f is None:
                        between()
                    elif e < NSH:
                        shared(f, i, e, between)
                    else:
                        if not bnd:
                            bnd.extend(load_bounds(f))
                        routed(f, i, bnd[e - NSH], bnd[e - NSH + 1])

                def banks_read(q):
                    done = p * Q + (min(q, preps - 1) + 3)
                    pe.wait_ge(kv_sb, min(done, NBLK) if isinstance(p, int) else done)

                if bound:
                    banks_read(-1)
                    gate_rows(m - FIRST_BOUND)
                expert(0, lambda: prep(0))
                if bound:
                    expert(1)
                    banks_read(0)
                    project_rows(m - FIRST_BOUND)
                    expert(2)
                    expert(3)
                if m is not None:
                    banks_read(0)
                    queries(m)
                    scores(m)
                if bound:
                    expert(4)
                else:
                    expert(1)
                    expert(2)
                if m is not None:
                    pe.wait_ge(sc_sb, m * (2 * B) + 2 * B)
                expert(5 if bound else 3, lambda: prep(1))
                if m is not None:
                    turn_weights(m, 0)
                at = 6 if bound else 4
                expert(at)
                if m is not None:
                    weigh_values(m, 0)
                    turn_weights(m, 1)
                expert(at + 1)
                if m is not None:
                    weigh_values(m, 1)
                    turn_weights(m, 2)
                prep(2)
                expert(at + 2)
                if m is not None:
                    banks_read(2)
                    weigh_values(m, 2)
                    turn_weights(m, 3)
                expert(at + 3)
                if m is not None:
                    weigh_values(m, 3)
                if not bound:
                    expert(8)
                    if m is not None:
                        project(m)
                    expert(9)
                if f is not None:
                    residual(f)
                if bound:
                    project(m)
                if m is not None:
                    router(m)
                prep(3)
                if m is not None:
                    places(m)

            pe.wait_ge(pool_const, 1)
            pe.wait_ge(attn_w_in, 5 * 16)
            prepare(0, 0)
            prepare(0, 1)
            pe.wait_ge(ctx_in, 6 * 16)
            for half in range(KC):
                for c in range(KC):
                    i = mm(ps[:, UP + half, 0:B * SK], hT[:, 2 + c, half * P:(half + 1) * P], hT[:, c, 0:B * SK],
                           start=c == 0, stop=c == KC - 1)
                i.then_inc(ctx_k_ps, 1)
            for b in range(B):
                for c in range(KC):
                    i = mm(ps[0:SK, ACC + b // 2, (b % 2) * D:(b % 2 + 1) * D], hT[:, c, b * SK:(b + 1) * SK],
                           hT[:, 4 + c, 0:D], start=c == 0, stop=c == KC - 1)
                i.then_inc(ctx_v_ps, 1)
            pe.wait_ge(xattn_w_in, 9 * 16)
            pe.wait_ge(ctx_done, KC + B)
            period(0, m=0)
            with pe.Fori(1, FIRST_BOUND) as p:
                period(p, f=p - 1, m=p)
            period(5, f=4)
            period(6, m=5, bound=True)
            period(7, f=5, m=6, bound=True, preps=NBLK - 7 * Q - 2)
            period(8, f=6, m=7, bound=True, preps=0)
            period(9, f=7, preps=0)

        @block.scalar
        def _(act):
            fn = nc.scalar.activation

            def prepare(blk, par):
                act.wait_ge(prep_a_ps, blk + 1)
                fn(xf1T[:, :], ps[0:HD, PRE, 0:P], ACT.Copy).then_inc(xf1_sb, 1)
                fn(graw[:, :], ps[:, PRE, P:P + H], ACT.Copy).then_inc(xf1_sb, 1)
                act.wait_ge(xf1_sb, blk * 2 + 2)
                if not isinstance(blk, int) or blk >= 2:
                    act.wait_ge(block_laid, blk * LAY - LAY)
                fn(beta[:, par], graw[:, :], ACT.Sigmoid).then_inc(fq_sb, 1)
                act.wait_ge(prep_b_ps, blk + 1)
                fn(fbuf[:, par], ps[:, PRE, D:2 * D], ACT.Sigmoid).then_inc(fq_sb, 1)
                fn(act3[:, par, 2], ps[:, A1, 0:D], ACT.Silu).then_inc(fq_sb, 1)
                fn(act3[:, par, 0:2].rearrange("p c d -> p (c d)"), ps[:, A0, :], ACT.Silu).then_inc(kv_sb, 1)

            def out_of_banks(dst, ready, done, m, scale=1.0):
                for c in range(KC):
                    act.wait_ge(ready, m * 2 + (c + 1))
                    fn(dst[:, c], ps[:, A0 + c, :], ACT.Copy, scale=scale).then_inc(done, 1)

            def gate_rows(n):
                out_of_banks(xtf, gx_ps, gx_sb, n)
                act.wait_ge(xo1_ps, n + 1)
                fn(xo1T, ps[0:HD, A0, :], ACT.Copy).then_inc(xo1_sb, 1)
                act.wait_ge(gate_ps, n + 1)
                fn(halves(gate[:, :, :]), ps[:, A0:A0 + 2, :], ACT.Sigmoid).then_inc(gate_sb, 1)

            def project_rows(n):
                out_of_banks(xtf, gT_ps, gT_sb, n)

            def queries(m):
                out_of_banks(xtf, x1T_ps, x1T_sb, m)
                out_of_banks(qT, q_ps, q_sb, m, -QSCALE)

            def scores(m):
                for b in range(B):
                    for half in range(2):
                        act.wait_ge(sc_ps, m * (2 * B) + (2 * b + half + 1))
                        first = (UP, A0)[half]
                        fn(probs[:, b, half * 8:(half + 1) * 8].rearrange("g (q h) k -> g q (h k)", q=2),
                           ps[:, first:first + 2, 0:QH * SK], ACT.Copy).then_inc(sc_sb, 1)

            def exponentials(m):
                for b in range(B):
                    act.wait_ge(min_done, m * B + (b + 1))
                    for h in range(H):
                        i = fn(probs[:, b, h], probs[:, b, h], ACT.Exp, bias=least[:, b, h:h + 1], scale=-1.0)
                    i.then_inc(exp_done, 1)

            def turn_weights(m, b):
                for q in range(H // QH):
                    act.wait_ge(eT_ps, m * (4 * B) + (4 * b + q + 1))
                    fn(eT[:, q * QH:(q + 1) * QH].rearrange("k h g -> k (h g)"), ps[0:SK, TURNED[q], :], ACT.Copy
                       ).then_inc(eT_sb, 1)

            def weigh_values(m, b):
                act.wait_ge(av_ps, m * B + (b + 1))
                if b >= 2:
                    act.wait_ge(att_done, m * B + (b - 1))
                fn(avs[:, b % 2].rearrange("g h d -> g (h d)"), ps[:, GATHER, 0:H * (HD + 1)], ACT.Copy).then_inc(av_sb, 1)

            def project(m):
                out_of_banks(xtf, attT_ps, attT_sb, m)

            def router(m):
                out_of_banks(x2T, x2T_ps, x2T_sb, m)
                act.wait_ge(rt_ps, m + 1)
                fn(rt[:, :, :].rearrange("g b e -> g (b e)"), ps[:, A0, 0:B * 2 * NR], ACT.Sigmoid).then_inc(rt_sb, 1)
                act.wait_ge(ln_out[LN_2], m * B + B)
                fn(x2f[:, :, :].rearrange("g b d -> g (b d)"), x2[:, :, :].rearrange("g b d -> g (b d)"), ACT.Copy
                   ).then_inc(x2f_sb, 1)

            def weights(m):
                act.wait_ge(route, m * ROUTE + 14)
                fn(rone[:, 5], rone[:, 4], ACT.Sigmoid).then_inc(w_done, 1)
                fn(rone[:, 6], rone[:, 4], ACT.Sigmoid, scale=-1.0).then_inc(w_done, 1)

            def shared(m, e, between):
                for g in range(FG):
                    act.wait_ge(sh_ps, m * (2 * FG) + (e * FG + g + 1))
                    fn(hT[:, g], ps[:, UP + g % 2, :], ACT.Gelu).then_inc(sh_gelu, 1)
                between()

            def load_bounds(m):
                act.wait_ge(bounds_done, m + 1)
                act.sem_inc(bounds_seen_act, 1)
                return [act.value_load(bounds[0:1, e:e + 1], min_val=0, max_val=TILES * NR * MAX_PASSES)
                        for e in range(NR + 1)]

            def routed(r, lo, hi):
                fn(tiny[:, :], tiny[:, :], ACT.Gelu).then_inc(warm, 1)
                with act.If(lo < hi), act.Fori(lo, hi) as n:
                    first = nc.s_assert_within(n - lo, 0, MAX_PASSES - 1, skip_runtime_bounds_check_because=
                                               "a pass is counted for each 128 of the tile's 512 tokens at most")
                    for b in range(B):
                        fn(far[:, b], slots[:, bass.ds(first * P, P)], ACT.Abs, bias=neg_slot[:, b, r:r + 1]).then_inc(far_done, 1)
                    act.wait_ge(far_done, n * B + B)
                    fn(sel[:, :, :], far[:, :, :], ACT.Relu, scale=-1.0, bias=1.0).then_inc(sel_done, 1)
                    for b in range(B):
                        fn(sel_w[:, b], far[:, b], ACT.Relu, scale=neg_w[:, b, r:r + 1], bias=w_tok[:, b, r:r + 1]
                           ).then_inc(selw_done, 1)
                    act.wait_ge(gather_ps, n + 1)
                    fn(xg[:, :, :].rearrange("p c n -> p (c n)"), ps[:, GATHER, 0:KC * P], ACT.Copy).then_inc(xg_sb, 1)
                    act.wait_ge(selT_ps, n + 1)
                    fn(selT[:, :, :].rearrange("p b n -> p (b n)"), ps[:, PRE, :], ACT.Copy).then_inc(selT_sb, 1)
                    for k in range(2):
                        act.wait_ge(up_ps, n * 2 + (k + 1))
                        fn(hT[:, 4 * k:4 * k + 4, 0:P], ps[:, UP + k, :].rearrange("p (g n) -> p g n", g=4), ACT.Gelu
                           ).then_inc(gelu_done, 1)
                    act.wait_ge(y_ps, n + 1)
                    fn(y[:, :], ps[:, UP, 0:D], ACT.Copy).then_inc(y_sb, 1)

            def sums(m):
                act.wait_ge(acc_ps, m + 1)
                act.wait_ge(out_stored, m * 16 + 1)
                for a in range(2):
                    fn(halves(y_out[:, :, :])[:, a], ps[:, ACC + a, :], ACT.Copy).then_inc(acc_sb, 1)

            def period(p, f=None, m=None, bound=False, preps=Q):
                order = BOUND_ORDER if bound else FREE_ORDER
                bnd = []

                def prep(q):
                    if q < preps:
                        prepare(p * Q + (q + 2), q % 2)

                def expert(i, between=lambda: None):
                    e = order[i]
                    if f is None:
                        between()
                    elif e < NSH:
                        shared(f, e, between)
                    else:
                        if not bnd:
                            bnd.extend(load_bounds(f))
                        routed(e - NSH, bnd[e - NSH], bnd[e - NSH + 1])

                def middle():
                    prep(1)
                    if m is not None:
                        exponentials(m)

                if bound:
                    gate_rows(m - FIRST_BOUND)
                expert(0, lambda: prep(0))
                if bound:
                    expert(1)
                    project_rows(m - FIRST_BOUND)
                    expert(2)
                    expert(3)
                if m is not None:
                    queries(m)
                    scores(m)
                if bound:
                    expert(4)
                else:
                    expert(1)
                    expert(2)
                expert(5 if bound else 3, middle)
                if m is not None:
                    turn_weights(m, 0)
                at = 6 if bound else 4
                expert(at)
                if m is not None:
                    weigh_values(m, 0)
                    turn_weights(m, 1)
                expert(at + 1)
                if m is not None:
                    weigh_values(m, 1)
                    turn_weights(m, 2)
                prep(2)
                expert(at + 2)
                if m is not None:
                    weigh_values(m, 2)
                    turn_weights(m, 3)
                expert(at + 3)
                if m is not None:
                    weigh_values(m, 3)
                if not bound:
                    expert(8)
                    if m is not None:
                        project(m)
                    expert(9)
                if f is not None:
                    sums(f)
                if bound:
                    project(m)
                if m is not None:
                    router(m)
                prep(3)
                if m is not None:
                    weights(m)

            act.sem_inc(sh_gelu, 2)
            act.sem_inc(acc_sb, 1)
            prepare(0, 0)
            prepare(1, 1)
            act.wait_ge(pool_const, 1)
            period(0, m=0)
            with act.Fori(1, FIRST_BOUND) as p:
                period(p, f=p - 1, m=p)
            period(5, f=4)
            period(6, m=5, bound=True)
            period(7, f=5, m=6, bound=True, preps=NBLK - 7 * Q - 2)
            period(8, f=6, m=7, bound=True, preps=0)
            period(9, f=7, preps=0)

        @block.gpsimd
        def _(pool):
            tt = nc.gpsimd.tensor_tensor

            def rsqrt(kind, n):
                pool.wait_ge(ln_mv[kind], n * B + B)
                tt(rstd[:, :], mv[:, :, 1], ln_eps[:, 0:B], ALU.add).then_inc(ln_rstd[kind], 1)
                pool.wait_ge(ln_rstd[kind], n * 2 + 1)
                tt(rstd[:, :], rstd[:, :], neg_half[:, 0:B], ALU.pow).then_inc(ln_rstd[kind], 1)

            heads = lambda a: a.rearrange("p (h d) -> p h d", h=H)
            by_head = lambda a: a.unsqueeze(2).to_broadcast([P, H, HD])

            def preparations(blk, par):
                k_silu = act3[:, par, 0]

                def tree_sum(src, dst):
                    return [lambda: tt(tree[:, :, 0:8], heads(src)[:, :, 0:8], heads(src)[:, :, 8:16], ALU.add),
                            lambda: tt(tree[:, :, 0:4], tree[:, :, 0:4], tree[:, :, 4:8], ALU.add),
                            lambda: tt(tree[:, :, 0:2], tree[:, :, 0:2], tree[:, :, 2:4], ALU.add),
                            lambda: tt(dst, tree[:, :, 0], tree[:, :, 1], ALU.add)]

                def k_square():
                    pool.wait_ge(kv_sb, blk + 1)
                    return tt(ksq[:, :], k_silu, k_silu, ALU.mult)

                def norm_floor():
                    pool.sem_inc(sum_seen, 1)
                    return nc.gpsimd.tensor_scalar(hsum[:, 0], hsum[:, 0], NORM_EPS * NORM_EPS, None, ALU.max)

                def k_normal():
                    if later(blk):
                        pool.wait_ge(block_laid, blk * LAY)
                    return tt(heads(tm[:, 1]), heads(k_silu), by_head(hsum[:, 1]), ALU.mult)

                ops = [k_square]
                ops += tree_sum(ksq[:, :], hsum[:, 0])
                ops += [norm_floor,
                        lambda: tt(hsum[:, 1], hsum[:, 0], neg_half[:, :], ALU.pow),
                        k_normal,
                        lambda: tt(fk[:, :], fbuf[:, par], tm[:, 1], ALU.mult),
                        lambda: tt(ksq[:, :], fk[:, :], tm[:, 1], ALU.mult)]
                ops += tree_sum(ksq[:, :], hsum[:, 2])
                ops += [lambda: tt(hsum[:, 3], beta[:, par], neg_one[:, :], ALU.mult),
                        lambda: tt(hsum[:, 2], hsum[:, 2], hsum[:, 3], ALU.mult),
                        lambda: tt(heads(tm[:, 0]), heads(fk[:, :]), by_head(hsum[:, 3]), ALU.mult),
                        lambda: tt(heads(ksq[:, :]), heads(tm[:, 1]), by_head(hsum[:, 2]), ALU.mult),
                        lambda: tt(ksq[:, :], ksq[:, :], fk[:, :], ALU.add),
                        lambda: tt(heads(tm[:, 2]), heads(ksq[:, :]), by_head(hsum[:, 3]), ALU.mult)]
                assert len(ops) == PREP
                return ops

            def prepare(blk, i, op):
                if i:
                    pool.wait_ge(prep_pool, blk * PREP + i)
                op().then_inc(prep_pool, 1)

            def steps(blk, par, keep, following=True, norms=()):
                ops = list(enumerate(preparations(blk + 1, 1 - par))) if following else []

                def place_v(t):
                    nc.gpsimd.tensor_copy(prod[:, t % 2, 1, :, HD], vrec[:, :, t]).then_inc(v_placed, 1)

                pool.wait_ge(block_laid, blk * LAY + LAY)
                pool.sem_inc(block_seen, 1)
                place_v(0)
                for t in range(T):
                    for h in range(2):
                        pool.wait_ge(step_done, blk * (T * STEP) + (t * STEP + 1 + h))
                        tt(terms[:, h, 0], S[:, (t - 1) % RING, h * HC:(h + 1) * HC],
                           rec[:, 3, :, t].unsqueeze(1).to_broadcast([P, HC, HD]), ALU.mult).then_inc(decayed, 1)
                    if t + 1 < T:
                        place_v(t + 1)
                    if keep and t % 2:
                        pool.wait_ge(step_done, blk * (T * STEP) + (t * STEP + STEP + 2))
                        tt(oprod[:, (t - 1) % (2 * OG):(t - 1) % (2 * OG) + 2], S[:, (t - 1) % RING:(t - 1) % RING + 2],
                           rec[:, 4, :, t - 1:t + 1].rearrange("p d t -> p t d").unsqueeze(2).to_broadcast([P, 2, HV, HD]),
                           ALU.mult).then_inc(o_terms, 1)
                    for at, kind, n in norms:
                        if t == at:
                            rsqrt(kind, n)
                    if t >= 4 and ops:
                        i, op = ops.pop(0)
                        prepare(blk + 1, i, op)

            consts = 0

            def const(ins):
                nonlocal consts
                consts += 1
                ins.then_inc(pool_set, 1)

            def ordered():
                pool.wait_ge(pool_set, consts)

            memset, select = nc.gpsimd.memset, nc.gpsimd.affine_select
            for dst, value in ((ident[:, :], 0.0), (twice[:, :], 0.0), (before[:, :], 1.0), (ones[:, :], 1.0), (head_mask[:, :], 1.0),
                               (lower[:, :, :], 1.0), (neg_half[:, :], -0.5), (neg_one[:, :], -1.0), (ln_eps[:, :], LN_EPS),
                               (o_rows[:, :, :], 0.0), (tiny[:, :], 0.0)):
                const(memset(dst, value))
            for dst, step, n, base in ((index8[:, :], 1, NR, -NR), (slots[:, :], 1, W, 0), (pass_at[:, :], P, MAX_PASSES, 0)):
                const(nc.gpsimd.iota(dst, pattern=[[step, n]], base=base, channel_multiplier=0,
                                     allow_small_or_imprecise_dtypes=True))
            ordered()
            const(select(out=ident[:, :], in_=ident[:, :], compare_op=ALU.not_equal, fill=1.0, base=0, pattern=[[-1, P]],
                         channel_multiplier=1))
            const(select(out=twice[:, :], in_=twice[:, :], compare_op=ALU.not_equal, fill=2.0, base=0, pattern=[[-1, P]],
                         channel_multiplier=1))
            const(select(out=before[:, :], in_=before[:, :], compare_op=ALU.is_gt, fill=0.0, base=0, pattern=[[1, P]],
                         channel_multiplier=-1))
            const(select(out=lower[:, :, :], in_=lower[:, :, :], compare_op=ALU.is_gt, fill=0.0, base=0,
                         pattern=[[1, NR + 1], [-1, NR]], channel_multiplier=0))
            const(select(out=head_mask[:, :], in_=head_mask[:, :], compare_op=ALU.is_ge, fill=0.0, base=0, pattern=[[-HD, 8]],
                         channel_multiplier=1))
            ordered()
            select(out=head_mask[:, :], in_=head_mask[:, :], compare_op=ALU.is_ge, fill=0.0, base=HD - 1, pattern=[[HD, 8]],
                   channel_multiplier=-1).then_inc(pool_const, 1)
            for i, op in enumerate(preparations(0, 0)):
                prepare(0, i, op)

            def free_period(p):
                for q in range(Q):
                    steps(p * Q + q, q % 2, False, norms=[(min(FREE_AT[kind] + 1, P - 1) - q * T, kind, p) for kind in (LN_1, LN_2)])

            def bound_period(p):
                for q in range(Q):
                    steps(p * Q + q, q % 2, True, p * Q + q + 1 < NBLK,
                          [(min(BOUND_AT[kind] + 1, P - 1) - q * T, kind, n) for kind, n in ((LN_GATE, p - 6), (LN_1, p - 1), (LN_2, p - 1))])

            free_period(0)
            with pool.Fori(1, FIRST_BOUND) as p:
                free_period(p)
                rsqrt(LN_3, p - 1)
            steps(KEEP - 1, 0, False)
            for blk in range(KEEP, KEEP + 3):
                steps(blk, blk % 2, True)
            rsqrt(LN_3, 4)
            bound_period(6)
            bound_period(7)
            rsqrt(LN_3, 5)
            rsqrt(LN_GATE, 2)
            rsqrt(LN_1, 7)
            rsqrt(LN_2, 7)
            rsqrt(LN_3, 6)
            rsqrt(LN_3, 7)

        @block.vector
        def _(dve):
            tt = nc.vector.tensor_tensor
            red = nc.vector.tensor_reduce

            def due(t, first, count):
                return [i for i in range(count) if min(first + i, P - 1) == t]

            def layer_norm(t, at, kind, n, src, dst, ready=None):
                for b in due(t, at - B, B):
                    if b == 0 and ready is not None:
                        dve.wait_ge(*ready)
                    nc.vector.bn_stats(stats[:, b], src[:, b]).then_inc(ln_stats[kind], 1)
                if due(t, at, 1):
                    dve.wait_ge(ln_stats[kind], n * B + B)
                    dve.sem_inc(ln_seen[kind], 1)
                    for b in range(B):
                        nc.vector.bn_aggr(mv[:, b], stats[:, b]).then_inc(ln_mv[kind], 1)
                for b in due(t, at + 3, B):
                    if b == 0:
                        dve.wait_ge(ln_rstd[kind], n * 2 + 2)
                    nc.vector.tensor_scalar(dst[:, b], src[:, b], mv[:, b, 0:1], rstd[:, b:b + 1], ALU.subtract, ALU.mult
                                            ).then_inc(ln_out[kind], 1)

            def add_banks(t, at, dst, ready, done):
                for a in due(t, at, 2):
                    dve.wait_ge(*ready)
                    tt(halves(dst)[:, a], ps[:, A0 + a, :], halves(dst)[:, a], ALU.add).then_inc(done, 1)

            def caps(t, m):
                if t == 0:
                    dve.wait_ge(mask_in, m * 16 + 16)
                    nc.vector.tensor_scalar(cap[:, :, :], imask[:, :, :], 0.0, -HUGE, ALU.not_equal, ALU.mult).then_inc(cap_half, 1)
                if t == 1:
                    dve.wait_ge(cap_half, m + 1)
                    nc.vector.tensor_scalar(cap[:, :, :], cap[:, :, :], MASKED, None, ALU.add).then_inc(cap_done, 1)

            def bound_rows(t, n, at):
                for a in due(t, at["gated"], 2):
                    dve.wait_ge(gate_sb, n + 1)
                    dve.wait_ge(o_stored, n * (Q * B * 16) + ((FIRST_BOUND * Q + Q - KEEP) * B * 16 + 1))
                    tt(halves(att)[:, a], halves(o_rows[:, :, :])[:, a], halves(gate[:, :, :])[:, a], ALU.mult).then_inc(gated, 1)
                layer_norm(t, at[LN_GATE], LN_GATE, n, att, att, (gated, n * 2 + 2))
                for b in due(t, at["weighted"], B):
                    dve.wait_ge(ln_out[LN_GATE], n * B + (b + 1))
                    tt(att[:, b], att[:, b], lnw[:, :], ALU.mult).then_inc(weighted, 1)
                add_banks(t, at["x_plus"], xin[:, :, :], (wout_ps, n + 1), x_plus)

            def minima(t, m, at):
                for i in due(t, at, 2 * B):
                    b = i // 2
                    if i % 2 == 0:
                        dve.wait_ge(cap_done, m + 1)
                        dve.wait_ge(sc_sb, m * (2 * B) + (2 * b + 2))
                        tt(probs[:, b], probs[:, b], cap[:, b].unsqueeze(1).to_broadcast([P, H, SK]), ALU.max).then_inc(capped, 1)
                    else:
                        dve.wait_ge(capped, m * B + (b + 1))
                        red(least[:, b], probs[:, b], AX.X, ALU.min).then_inc(min_done, 1)

            def attended(t, m, b, at):
                if due(t, at, 1):
                    if b:
                        dve.wait_ge(att_done, m * B + b)
                    dve.wait_ge(av_sb, m * B + (b + 1))
                    nc.vector.reciprocal(rden[:, :], avs[:, b % 2, :, HD]).then_inc(rden_done, 1)
                if due(t, at + 1, 1):
                    dve.wait_ge(rden_done, m * B + (b + 1))
                    tt(att[:, b].rearrange("g (h d) -> g h d", h=H), avs[:, b % 2, :, 0:HD],
                       rden[:, :].unsqueeze(2).to_broadcast([P, H, HD]), ALU.mult).then_inc(att_done, 1)

            def routing(m, part):
                raw_s, biased = rt[:, :, 0:NR], rt[:, :, NR:2 * NR]
                wide = lambda i: rone[:, i].unsqueeze(2).to_broadcast([P, B, NR])
                index = index8[:, :].unsqueeze(1).to_broadcast([P, B, NR])
                first_hot, second_hot = rbuf[:, 2], rbuf[:, 6]
                ts, copy = nc.vector.tensor_scalar, nc.vector.tensor_copy
                n = ROUTE_PARTS[part]

                def then(ins):
                    nonlocal n
                    n += 1
                    ins.then_inc(route, 1)

                def after():
                    dve.wait_ge(route, m * ROUTE + n)

                def highest(scores, top):
                    then(red(rone[:, top], scores, AX.X, ALU.max))

                def equal_first(scores, top, r):
                    after()
                    then(tt(rbuf[:, r], scores, wide(top), ALU.is_equal))
                    after()
                    then(tt(rbuf[:, r + 1], rbuf[:, r], index, ALU.mult))
                    after()
                    then(red(rone[:, top + 1], rbuf[:, r + 1], AX.X, ALU.min))
                    after()
                    then(tt(rbuf[:, r + 2], index, wide(top + 1), ALU.is_equal))

                if part == 0:
                    dve.wait_ge(rt_sb, m + 1)
                    highest(biased, 0)
                if part == 1:
                    equal_first(biased, 0, 0)
                if part == 2:
                    after()
                    then(nc.vector.scalar_tensor_tensor(rbuf[:, 3], first_hot, -4.0, biased, ALU.mult, ALU.add))
                    after()
                    highest(rbuf[:, 3], 2)
                if part == 3:
                    equal_first(rbuf[:, 3], 2, 4)
                if part == 4:
                    after()
                    tt(chosen[:, :, :], first_hot, second_hot, ALU.add).then_inc(picked, 1)
                    then(tt(rbuf[:, 7], first_hot, second_hot, ALU.subtract))
                    after()
                    then(tt(rbuf[:, 7], rbuf[:, 7], raw_s, ALU.mult))
                    after()
                    then(red(rone[:, 4], rbuf[:, 7], AX.X, ALU.add))
                if part == 5:
                    dve.wait_ge(picked, m + 1)
                    then(ts(neg_slot[:, :, :], chosen[:, :, :], FAR, -FAR, ALU.mult, ALU.add))
                    after()
                    dve.wait_ge(pos_ps, m + 1)
                    then(tt(neg_slot[:, :, :], neg_slot[:, :, :], ps[:, GATHER, 0:B * NR].rearrange("g (b e) -> g b e", b=B),
                            ALU.subtract))
                    total = ps[0:1, GATHER, B * NR:B * NR + NR].unsqueeze(2).to_broadcast([1, NR, MAX_PASSES])
                    then(tt(over[:, :, :], total, pass_at[:, :].unsqueeze(1).to_broadcast([1, NR, MAX_PASSES]), ALU.is_gt))
                    after()
                    then(red(passes[:, :], over[:, :, :], AX.X, ALU.add))
                    after()
                    then(tt(lterm[:, :, :], lower[:, :, :], passes[:, :].unsqueeze(1).to_broadcast([1, NR + 1, NR]), ALU.mult))
                    after()
                    then(red(first_pass[:, :], lterm[:, :, :], AX.X, ALU.add))
                    after()
                    then(tt(first_pass[:, :], first_pass[:, :], pass_base[:, :].to_broadcast([1, NR + 1]), ALU.add))
                    after()
                    then(copy(pass_base[:, :], first_pass[:, NR:NR + 1]))
                if part == 6:
                    dve.wait_ge(w_done, m * 2 + 2)
                    then(tt(rbuf[:, 0], first_hot, wide(5), ALU.mult))
                    then(tt(rbuf[:, 1], second_hot, wide(6), ALU.mult))
                    after()
                    then(tt(w_tok[:, :, :], rbuf[:, 0], rbuf[:, 1], ALU.add))
                    after()
                    then(ts(neg_w[:, :, :], w_tok[:, :, :], -1.0, None, ALU.mult))
                    after()
                    copy(bounds[:, :], first_pass[:, :]).then_inc(bounds_done, 1)
                assert n == ROUTE_PARTS[part + 1]

            def attention_after(t, m, bound, at):
                caps(t, m)
                if bound:
                    n = m - FIRST_BOUND
                    bound_rows(t, n, at)
                    layer_norm(t, at[LN_1], LN_1, m, xin[:, :, :], x1[:, :, :], (x_plus, n * 2 + 2))
                else:
                    layer_norm(t, at[LN_1], LN_1, m, xin[:, :, :], x1[:, :, :], (tile_in, m * 16 + 16))
                minima(t, m, at["minima"])
                for b in range(B):
                    attended(t, m, b, at["attended"][b])
                add_banks(t, at["resid"], x1[:, :, :], (wo_ps, m + 1), resid)
                layer_norm(t, at[LN_2], LN_2, m, x1[:, :, :], x2[:, :, :], (resid, m * 2 + 2))
                for part in due(t, at["routing"], len(ROUTE_PARTS) - 1):
                    routing(m, part)

            def last_norm(m):
                for t in range(B + 3 + B):
                    layer_norm(t, B, LN_3, m, y_out[:, :, :], y_out[:, :, :], (acc_sb, m * 2 + 3))

            def lay_out(blk, par):
                dve.wait_ge(prep_pool, blk * PREP + PREP)
                if later(blk):
                    dve.wait_ge(decayed, blk * (2 * T))
                    dve.wait_ge(step_done, blk * (T * STEP) + 2)
                for i, src in enumerate((tm[:, 0], tm[:, 1], tm[:, 2], fbuf[:, par], act3[:, par, 2])):
                    wide = src.rearrange("p (h d) -> p d h", h=H).unsqueeze(3).to_broadcast([P, HD, H, 2])
                    nc.vector.transpose(rec[:, i], wide).then_inc(block_laid, 1)
                nc.vector.transpose(vrec[:, :, :], act3[:, par, 1].rearrange("p (g v) -> p v g", v=HV)).then_inc(block_laid, 1)

            def outputs(blk, g):
                dve.wait_ge(o_terms, (blk - KEEP) * (T // 2) + (g + 1) * (OG // 2))
                red(osum[:, g * OG:(g + 1) * OG].rearrange("p t v -> p (t v)"),
                    oprod[:, g % 2 * OG:(g % 2 + 1) * OG].rearrange("p t v d -> p (t v) d"), AX.X, ALU.add).then_inc(o_sums, 1)

            def steps(blk, keep, after=lambda t: None):
                base = blk * (T * STEP) + 2
                dve.wait_ge(block_laid, blk * LAY + LAY)
                for t in range(T):
                    at = base + t * STEP
                    for h in range(2):
                        cols = slice(h * HC, (h + 1) * HC)
                        dve.wait_ge(step_done, at + (h - 1))
                        tt(prod[:, t % 2, :, cols, 0:HD],
                           S[:, (t - 1) % RING, cols].unsqueeze(1).to_broadcast([P, 2, HC, HD]),
                           rec[:, 1:3, :, t].unsqueeze(2).to_broadcast([P, 2, HC, HD]), ALU.mult).then_inc(step_done, 1)
                    for h in range(2):
                        dve.wait_ge(step_done, at + (1 + h))
                        dve.wait_ge(v_placed, blk * T + (t + 1))
                        red(u[:, h], prod[:, t % 2, :, h * HC:(h + 1) * HC], AX.X, ALU.add).then_inc(step_done, 1)
                    for h in range(2):
                        dve.wait_ge(step_done, at + (3 + h))
                        tt(terms[:, h, 1:3], u[:, h].unsqueeze(3).to_broadcast([P, 2, HC, HD]),
                           rec[:, 0:2, :, t].unsqueeze(2).to_broadcast([P, 2, HC, HD]), ALU.mult).then_inc(step_done, 1)
                    for h in range(2):
                        dve.wait_ge(step_done, at + (5 + h))
                        dve.wait_ge(decayed, blk * (2 * T) + (2 * t + h + 1))
                        red(S[:, t % RING, h * HC:(h + 1) * HC].rearrange("p v d -> p (v d)"),
                            terms[:, h].rearrange("p n v d -> p (v d) n"), AX.X, ALU.add).then_inc(step_done, 1)
                    if keep and t > OG and t % OG == OG // 2:
                        outputs(blk, t // OG - 1)
                    after(t)
                if keep:
                    n = blk - KEEP
                    outputs(blk, T // OG - 1)
                    dve.wait_ge(o_sums, n * (T // OG) + T // OG)
                    dve.wait_ge(o_stored, n * (B * 16) + 1)
                    nc.vector.transpose(otm[:, :, :, :].rearrange("p h a v -> p v (h a)"),
                                        osum[:, :, :].rearrange("p t v -> p v t")).then_inc(o_ready, 1)

            def period(p, m, bound):
                for q in range(Q):
                    steps(p * Q + q, bound, lambda t: attention_after(q * T + t, m, bound, BOUND_AT if bound else FREE_AT))
                    if not isinstance(p, int) or p * Q + q + 1 < NBLK:
                        lay_out(p * Q + (q + 1), (q + 1) % 2)

            for h in range(2):
                nc.vector.memset(S[:, RING - 1, h * HC:(h + 1) * HC], 0.0).then_inc(step_done, 1)
            nc.vector.memset(prod[:, :, 0, :, HD], 0.0).then_inc(dve_const, 1)
            nc.vector.memset(vals[:, :, :, :], 1.0).then_inc(dve_const, 1)
            nc.vector.memset(pass_base[:, :], 0.0).then_inc(dve_const, 1)
            dve.wait_ge(pool_const, 1)
            red(quad_mask[:, :], head_mask[:, :].rearrange("p (g j) -> p j g", j=QH), AX.X, ALU.add).then_inc(dve_const, 1)
            dve.wait_ge(dve_const, 4)
            for c in range(KC):
                dve.wait_ge(ctx_k_ps, c + 1)
                tt(keys[:, c], ps[:, UP + c, 0:B * SK].rearrange("p (b k) -> p b k", b=B).unsqueeze(2).to_broadcast([P, B, QH, SK]),
                   quad_mask[:, :].unsqueeze(1).unsqueeze(3).to_broadcast([P, B, QH, SK]), ALU.mult).then_inc(ctx_done, 1)
            for b in range(B):
                dve.wait_ge(ctx_v_ps, b // 2 * 2 + 2)
                nc.vector.tensor_copy(vals[:, b, :, 0:HD], ps[0:SK, ACC + b // 2, (b % 2) * D:(b % 2 + 1) * D].rearrange(
                    "k (h d) -> k h d", h=H)).then_inc(ctx_done, 1)
            lay_out(0, 0)
            period(0, 0, False)
            with dve.Fori(1, FIRST_BOUND) as p:
                period(p, p, False)
                last_norm(p - 1)
            for q in range(Q):
                blk = FIRST_BOUND * Q + q
                steps(blk, blk >= KEEP)
                lay_out(blk + 1, (q + 1) % 2)
            last_norm(4)
            period(6, 5, True)
            period(7, 6, True)
            last_norm(5)
            for t in range(P):
                attention_after(t, 7, True, BOUND_AT)
            last_norm(6)
            last_norm(7)


FREE_ORDER = 0, 2, 3, 1, 4, 5, 6, 7, 8, 9
BOUND_ORDER = 0, 2, 3, 4, 5, 1, 6, 7, 8, 9
ROUTE_PARTS = 0, 1, 5, 7, 11, 14, 22, ROUTE
FREE_AT = {1: 6, "minima": 23, "attended": (67, 76, 90, 101), "resid": 112, 2: 118, "routing": 125}
BOUND_AT = {"gated": 5, 0: 11, "weighted": 18, "x_plus": 31, 1: 37, "minima": 54, "attended": (92, 102, 114, 124),
            "resid": 127, 2: 133, "routing": 140}


def kernel(x, ctx_1024, mask_Bx1xSxS2_if1, L0_attn_Wq, L0_attn_Wk, L0_attn_Wv, L0_attn_Wf1, L0_attn_Wf2, L0_attn_Wg,
           L0_attn_Wo1, L0_attn_Wo2, L0_attn_ln_w, L0_attn_Wout, L0_xattn_Wq, L0_xattn_Wk, L0_xattn_Wv, L0_xattn_Wo,
           L0_xattn_bo, L0_ffn_centroids, L0_ffn_routing_bias, L0_ffn_Wfc_r, L0_ffn_Wproj_r, L0_ffn_Wfc_sh,
           L0_ffn_Wproj_sh):
    import numpy as np
    import concourse.bacc as bacc
    from concourse.bass_utils import run_bass_kernel_spmd as run

    x, mask = np.asarray(x), np.asarray(mask_Bx1xSxS2_if1)[:, 0]
    order = np.argsort(np.arange(N) % 3 == 0, kind="stable")
    tiled = lambda a: a[:, order].reshape(B, TILES, P, -1).transpose(1, 2, 0, 3)
    t = lambda a: np.swapaxes(np.asarray(a), -1, -2)
    arrays = dict(
        x=tiled(x), xT=t(x), ctxT=t(ctx_1024), mask=tiled(mask),
        wkv=np.concatenate([np.asarray(L0_attn_Wk), np.asarray(L0_attn_Wv)], 1), wqr=L0_attn_Wq, wf1=L0_attn_Wf1,
        wf2=L0_attn_Wf2, wg=L0_attn_Wg, wo1=L0_attn_Wo1, wo2=L0_attn_Wo2, ln_w=L0_attn_ln_w, wout=L0_attn_Wout,
        cqT=t(L0_xattn_Wq), ckT=t(L0_xattn_Wk), cvT=t(L0_xattn_Wv), coT=t(L0_xattn_Wo), cbo=L0_xattn_bo,
        centT=t(L0_ffn_centroids), rbias=L0_ffn_routing_bias,
        wfcT=t(np.concatenate([np.asarray(L0_ffn_Wfc_sh), np.asarray(L0_ffn_Wfc_r)])),
        wpT=t(np.concatenate([np.asarray(L0_ffn_Wproj_sh), np.asarray(L0_ffn_Wproj_r)])))
    arrays = {f"in_{k}": np.ascontiguousarray(v) for k, v in arrays.items()}
    nc = bacc.Bacc("TRN2", target_bir_lowering=False, num_devices=1)
    args = [nc.dram_tensor(k, a.shape, mybir.dt.from_np(a.dtype), kind="ExternalInput").ap() for k, a in arrays.items()]
    args.append(nc.dram_tensor("out_0", (TILES, P, B, D), F32, kind="ExternalOutput").ap())
    decoder_layer(nc, *args)
    r = run(nc, [arrays], core_ids=[0])
    rows = r.results[0]["out_0"].transpose(2, 0, 1, 3).reshape(B, N, D)
    return rows[:, np.argsort(order)]
```

```python
from contextlib import ExitStack

import concourse.bass as bass
from concourse import mybir

F32 = mybir.dt.float32
I32 = mybir.dt.int32
ALU = mybir.AluOpType
ACT = mybir.ActivationFunctionType
AX = mybir.AxisListType

B, N, D = 4, 1024, 256
H, HD = 16, 16
SK = 77
NSH, NR, F = 2, 8, 1024
NE = NSH + NR
P = 128
KC = D // P
FG = F // P
W = B * P
TILES = N // P
QH = 4
HV, HC = 8, 4
T = 32
NBLK = N // T
Q = 4
assert Q * T == P
O_FIRST = (3 * N - N) // 3
KEEP = O_FIRST // T
FIRST_BOUND = O_FIRST // P
RING = 4
OG = 4
MAX_PASSES = W // P
LN_EPS = 1e-5
NORM_EPS = 1e-12
QSCALE = HD ** -0.5
MASKED = 1e9 * QSCALE
HUGE = 3e38
FAR = 4096.0
PREP = 23
PREP_COST = 2, 1, 1, 1, 1, 1, 3, 3, 3, 3, 3, 2, 2, 1, 1, 1, 1, 1, 1, 3, 3, 2, 3
PREP_FROM = 6
LAY = 6
EXPERTS = range(NE)
LATE = NE - 5
STEP = 8
ROUTE = 25


def decoder_layer(nc, x, xT, ctxT, mask, wkv, wqr, wf1, wf2, wg, wo1, wo2, ln_w, wout,
                  cqT, ckT, cvT, coT, cbo, centT, rbias, wfcT, wpT, out):
    with ExitStack() as ctx:
        def sb(name, shape, dt=F32):
            return ctx.enter_context(nc.sbuf_tensor(name, shape, dt))

        def sem(name):
            return ctx.enter_context(nc.semaphore(name))

        ident, twice = sb("ident", [P, P]), sb("twice", [P, P])
        before, ones = sb("before", [P, P]), sb("ones", [P, P])
        slots = sb("slots", [P, W + P])
        head_mask = sb("head_mask", [P, 8])
        quad_mask = sb("quad_mask", [P, QH])
        neg_half, neg_one, ln_eps = sb("neg_half", [P, H]), sb("neg_one", [P, H]), sb("ln_eps", [P, H])
        index8 = sb("index8", [P, NR])
        pass_at = sb("pass_at", [1, MAX_PASSES])
        lower = sb("lower", [1, NR + 1, NR])
        w_kv = sb("w_kv", [P, KC, 2 * D])
        w_q = sb("w_q", [P, KC, D])
        w_f1 = sb("w_f1", [P, KC, HD])
        w_f2 = sb("w_f2", [HD, D])
        w_g = sb("w_g", [P, KC, H])
        w_o1 = sb("w_o1", [P, KC, HD])
        w_o2 = sb("w_o2", [HD, D])
        w_out = sb("w_out", [P, KC, D])
        lnw = sb("lnw", [P, D])
        c_q = sb("c_q", [P, KC, D])
        c_o = sb("c_o", [P, KC, D])
        c_bo = sb("c_bo", [1, D])
        cent = sb("cent", [P, KC, 2, NR])
        r_bias = sb("r_bias", [1, 2, NR])
        keys = sb("keys", [P, KC, B, QH, SK])
        vals = sb("vals", [SK, B, H, 2 * HD])

        xin = sb("xin", [P, B, D])
        x1 = sb("x1", [P, B, D])
        xtf = sb("xtf", [P, KC, W])
        qT = sb("qT", [P, KC, W])
        imask = sb("imask", [P, B, SK], I32)
        cap = sb("cap", [P, B, SK])
        probs = sb("probs", [P, B, H, SK])
        least = sb("least", [P, B, H])
        eT = sb("eT", [P, H, P])
        att = eT[:, 0:B * D // P].rearrange("g h d -> g (h d)").rearrange("g (b d) -> g b d", b=B)
        weight_sum = sb("weight_sum", [P, B, H])
        rden = sb("rden", [P, H])
        stats = sb("stats", [P, B, 6])
        mv = sb("mv", [P, B, 2])
        rstd = sb("rstd", [P, B])
        gate = sb("gate", [P, B, D])
        x2 = x1
        xo1T = qT[0:HD, 0]
        o_rows = sb("o_rows", [P, B, D])

        rt = sb("rt", [P, B, 2 * NR])
        rbuf = sb("rbuf", [P, 8, B, NR])
        rone = sb("rone", [P, 8, B])
        chosen = sb("chosen", [P, B + 1, NR])
        w_tok = sb("w_tok", [P, B, NR])
        neg_slot = sb("neg_slot", [P, B, NR])
        over = sb("over", [1, NR, MAX_PASSES])
        passes = sb("passes", [1, NR])
        lterm = sb("lterm", [1, NR + 1, NR])
        first_pass = sb("first_pass", [1, NR + 1])
        pass_base = sb("pass_base", [1, 1])
        bounds = sb("bounds", [1, NR + 1], I32)

        x2f = sb("x2f", [P, B, D])
        x2T = sb("x2T", [P, KC, W])
        fc = sb("fc", [P, 2, KC, F])
        pj = sb("pj", [P, 2, FG, D])
        hT = sb("hT", [P, FG, W])
        sel = sb("sel", [P, 2, B, P])
        sel_w = sb("sel_w", [P, B, P])
        selT = sb("selT", [P, B, P])
        xg = sb("xg", [P, KC, P])
        y = sb("y", [P, D])
        y_out = sb("y_out", [P, B, D])
        tiny = sb("tiny", [1, 1])

        xtp = sb("xtp", [P, 2, KC, B, T])
        xf1T = sb("xf1T", [HD, P])
        graw = sb("graw", [P, H])
        act3 = sb("act3", [P, 2, 3, D])
        fbuf = sb("fbuf", [P, 2, D])
        beta = sb("beta", [P, 2, H])
        ksq = sb("ksq", [P, D])
        fk = sb("fk", [P, D])
        tree = sb("tree", [P, H, 8])
        hsum = sb("hsum", [P, 4, H])
        tm = sb("tm", [P, 3, D])
        rec = sb("rec", [P, 5, HD, T])
        vrec = sb("vrec", [P, HV, T])
        prod = sb("prod", [P, 2, 2, HV, HD + 1])
        u = sb("u", [P, 2, 2, HC])
        terms = sb("terms", [P, 2, 3, HC, HD])
        S = sb("S", [P, RING, HV, HD])
        oprod = sb("oprod", [P, 2 * OG, HV, HD])
        osum = sb("osum", [P, T, HV])
        otm = sb("otm", [P, H, 2, HV])

        ps = ctx.enter_context(nc.psum_tensor("ps", [P, 8, 512], F32))
        ACC, UP, GATHER, A0, A1, PRE = 0, 2, 4, 5, 6, 7
        TURNED = UP, UP + 1, A0, A1
        WEIGHED = GATHER, PRE

        (attn_w_in, xattn_w_in, ctx_in, xt_in0, xt_in1, expert_in0, expert_in1, tile_in, mask_in, o_stored, out_stored,
         pool_set, pool_const, dve_const, ctx_k_ps, ctx_v_ps, ctx_done, prep_a_ps, prep_b_ps, xf1_sb, fq_sb,
         kv_sb, sum_seen, prep_pool, block_laid, block_seen, v_placed, step_done, decayed, o_terms, o_sums, o_ready,
         cap_half, cap_done, x1T_ps, x1T_sb, q_ps, q_sb, sc_ps, sc_sb, capped, min_done, exp_done, eT_ps, eT_sb,
         rden_done, shares_done, attT_ps, attT_sb, wo_ps, resid, x2T_ps, x2f_sb, x2T_sb, rt_ps, rt_sb, route,
         w_done, picked, pos_ps, bounds_done, bounds_seen_pe, bounds_seen_act, gx_ps, gx_sb, xo1_ps, xo1_sb, gate_ps,
         gate_sb, gated, weighted, gT_ps, gT_sb, wout_ps, x_plus, sh_ps, sh_gelu, expert_used0, expert_used1, acc_ps,
         acc_sb, warm, far_first, far_next, sel_first, sel_next, selw_done, gather_ps, xg_sb, up_ps, gelu_done, selT_ps, selT_sb, y_ps, y_sb) = map(sem, """
            attn_w_in xattn_w_in ctx_in xt_in0 xt_in1 expert_in0 expert_in1 tile_in mask_in o_stored out_stored pool_set
            pool_const dve_const ctx_k_ps ctx_v_ps ctx_done prep_a_ps prep_b_ps xf1_sb fq_sb kv_sb sum_seen
            prep_pool block_laid block_seen v_placed step_done decayed o_terms o_sums o_ready cap_half cap_done x1T_ps
            x1T_sb q_ps q_sb sc_ps sc_sb capped min_done exp_done eT_ps eT_sb rden_done shares_done attT_ps
            attT_sb wo_ps resid x2T_ps x2f_sb x2T_sb rt_ps rt_sb route w_done picked pos_ps bounds_done bounds_seen_pe
            bounds_seen_act gx_ps gx_sb xo1_ps xo1_sb gate_ps gate_sb gated weighted gT_ps gT_sb wout_ps x_plus sh_ps
            sh_gelu expert_used0 expert_used1 acc_ps acc_sb warm far_first far_next sel_first sel_next selw_done gather_ps xg_sb up_ps
            gelu_done selT_ps selT_sb y_ps y_sb""".split())
        xt_in = xt_in0, xt_in1
        expert_in, expert_used = (expert_in0, expert_in1), (expert_used0, expert_used1)
        ln_stats, ln_seen, ln_mv, ln_rstd, ln_out = ([sem(f"{what}{kind}") for kind in range(4)] for what in
                                                     ("stats", "stats_seen", "mv", "rstd", "norm"))
        LN_GATE, LN_1, LN_2, LN_3 = range(4)

        xT_v = xT.rearrange("b (c p) t -> p c b t", p=P)
        wfc_v = wfcT.rearrange("e (c p) f -> e p c f", p=P)
        wp_v = wpT.rearrange("e (g p) d -> e p g d", p=P)

        def chunked(w):
            return w.rearrange("(c p) n -> p c n", p=P)

        def one(v, i, n=1):
            return v[i:i + n] if isinstance(i, int) else v[bass.ds(i, n)]

        def row(v):
            return v.rearrange("(a n) -> a n", a=1)

        def later(blk):
            return not isinstance(blk, int) or blk > 0

        def halves(t):
            return t.rearrange("g (a b) d -> g a (b d)", a=2)

        block = ctx.enter_context(nc.Block())

        @block.sync
        def _(sp):
            def load_xt(blk, par):
                if not isinstance(blk, int) or blk >= 2:
                    sp.wait_ge(prep_b_ps, blk - 1)
                for c in range(KC):
                    sp.dma_start(xtp[:, par, c], xT_v[:, c, :, blk * T:(blk + 1) * T] if isinstance(blk, int)
                                 else xT_v[:, c, :, bass.ds(blk * T, T)]).then_inc(xt_in[par], 16)

            def load_expert(i):
                sp.dma_start(fc[:, i % 2], wfc_v[i]).then_inc(expert_in[i % 2], 16)
                sp.dma_start(pj[:, i % 2], wp_v[i]).then_inc(expert_in[i % 2], 16)

            def load_tile(m):
                sp.dma_start(xin[:, :, :], one(x, m).rearrange("m g b d -> g (m b) d")).then_inc(tile_in, 16)
                sp.dma_start(imask[:, :, :], one(mask, m).rearrange("m g b k -> g (m b) k")).then_inc(mask_in, 16)

            def next_tile(m):
                sp.wait_ge(ln_out[LN_1], m * B)
                sp.wait_ge(cap_half, m)
                load_tile(m)

            def next_expert(m, i):
                sp.wait_ge(expert_used[i % 2], m * (NE // 2) + (i // 2 + 1))
                load_expert((i + 2) % NE)

            def store_tile(m):
                sp.wait_ge(ln_out[LN_3], m * B + B)
                sp.dma_start(one(out, m).rearrange("m g b d -> g (m b) d"), y_out[:, :, :]).then_inc(out_stored, 16)

            def store_o(blk):
                sp.wait_ge(o_ready, blk - (KEEP - 1))
                first = max(O_FIRST - blk * T, 0)
                at = blk % Q * T
                for b in range(B):
                    sp.dma_start(o_rows[at + first:at + T, b], otm[b * T + first:(b + 1) * T].rearrange("t h a v -> t (h a v)")
                                 ).then_inc(o_stored, 16)

            def period(p, m=None, f=None, load=None, bound=False, stored=None, blocks=Q, stores=(None,) * Q):
                def xt(q):
                    if q < blocks:
                        load_xt(p * Q + (Q + q), q % 2)

                def used(tile, i):
                    if tile is not None:
                        next_expert(tile, i)

                def outputs(q):
                    if stores[q] is not None:
                        store_o(stores[q])

                xt(0)
                used(f, LATE)
                if load is not None:
                    next_tile(load)
                used(f, LATE + 1)
                outputs(0)
                xt(1)
                used(f, LATE + 2)
                used(f, LATE + 3)
                outputs(1)
                used(f, LATE + 4)
                xt(2)
                used(m, 0)
                if not bound:
                    xt(3)
                used(m, 1)
                if not bound:
                    outputs(2)
                used(m, 2)
                if f is not None:
                    store_tile(f)
                used(m, 3)
                if bound:
                    outputs(2)
                    xt(3)
                    if stored is not None:
                        store_tile(stored)
                    for e in EXPERTS[4:8]:
                        used(m, e)
                outputs(3)
                if not bound:
                    used(m, 4)
                elif m < TILES - 1:
                    used(m, 8)
                    used(m, 9)

            sp.sem_inc(o_stored, 1)
            sp.sem_inc(out_stored, 1)
            load_xt(0, 0)
            for dst, src in ((w_f1, wf1), (w_g, wg), (w_kv, wkv), (w_q, wqr)):
                sp.dma_start(dst[:, :, :], chunked(src)).then_inc(attn_w_in, 16)
            sp.dma_start(w_f2[:, :], wf2).then_inc(attn_w_in, 16)
            load_xt(1, 1)
            for b in range(B):
                sp.dma_start(hT[:, 0:KC, b * SK:(b + 1) * SK], chunked(ctxT[b])).then_inc(ctx_in, 16)
            sp.dma_start(hT[:, 2:4, 0:D], chunked(ckT)).then_inc(ctx_in, 16)
            sp.dma_start(hT[:, 4:6, 0:D], chunked(cvT)).then_inc(ctx_in, 16)
            load_tile(0)
            for dst, src in ((c_q[:, :, :], cqT), (c_o[:, :, :], coT), (cent[:, :, 0], centT), (cent[:, :, 1], centT), (w_o1[:, :, :], wo1), (w_out[:, :, :], wout)):
                sp.dma_start(dst, chunked(src)).then_inc(xattn_w_in, 16)
            sp.dma_start(w_o2[:, :], wo2).then_inc(xattn_w_in, 16)
            sp.dma_start(c_bo[:, :], row(cbo)).then_inc(xattn_w_in, 16)
            sp.dma_start(r_bias[:, 1], row(rbias)).then_inc(xattn_w_in, 16)
            sp.dma_start(lnw[:, :], row(ln_w).to_broadcast([P, D])).then_inc(xattn_w_in, 16)
            load_xt(2, 0)
            load_xt(3, 1)
            load_expert(0)
            load_expert(1)

            period(0, 0, load=1)
            with sp.Fori(1, FIRST_BOUND) as p:
                period(p, p, p - 1, load=p + 1)
            period(5, None, 4, stores=(None, 21, 22, 23))
            period(6, 5, load=6, bound=True, stores=(24, 25, 26, 27))
            period(7, 6, load=7, bound=True, stored=5, blocks=0, stores=(28, 29, 30, 31))
            period(8, 7, bound=True, stored=6, blocks=0)
            store_tile(7)
            sp.wait_ge(out_stored, 16 * TILES + 1)

        @block.tensor
        def _(pe):
            mm = nc.tensor.matmul

            def prepare(pair, par):
                blk = pair * 2 + par
                xt = [xtp[:, par, c].rearrange("p b t -> p (b t)") for c in range(KC)]
                pe.wait_ge(xt_in[par], pair * (16 * KC) + 16 * KC)
                if later(blk):
                    pe.wait_ge(kv_sb, blk)
                for c in range(KC):
                    mm(ps[0:HD, PRE, 0:P], w_f1[:, c], xt[c], start=c == 0, stop=c == KC - 1)
                for c in range(KC):
                    i = mm(ps[:, PRE, P:P + H], xt[c], w_g[:, c], start=c == 0, stop=c == KC - 1)
                i.then_inc(prep_a_ps, 1)
                pe.wait_ge(xf1_sb, blk * 2 + 2)
                for c in range(KC):
                    i = mm(ps[:, A0, :], xt[c], w_kv[:, c], start=c == 0, stop=c == KC - 1)
                for c in range(KC):
                    i = mm(ps[:, A1, 0:D], xt[c], w_q[:, c], start=c == 0, stop=c == KC - 1)
                i = mm(ps[:, PRE, D:2 * D], xf1T[:, :], w_f2[:, :], start=True, stop=True)
                i.then_inc(prep_b_ps, 1)

            def turn(src, done):
                for c in range(KC):
                    for b in range(B):
                        i = nc.tensor.transpose(ps[:, A0 + c, b * P:(b + 1) * P], src[:, b, c * P:(c + 1) * P], ident[:, :])
                    i.then_inc(done, 1)

            def gate_rows(n):
                pe.wait_ge(tile_in, n * 16 + (FIRST_BOUND * 16 + 16))
                turn(xin, gx_ps)
                pe.wait_ge(gx_sb, n * 2 + 2)
                for c in range(KC):
                    i = mm(ps[0:HD, A0, :], w_o1[:, c], xtf[:, c], start=c == 0, stop=c == KC - 1)
                i.then_inc(xo1_ps, 1)
                pe.wait_ge(xo1_sb, n + 1)
                for b in range(B):
                    i = mm(ps[:, A0 + b // 2, (b % 2) * D:(b % 2 + 1) * D], xo1T[:, b * P:(b + 1) * P], w_o2[:, :],
                           start=True, stop=True)
                i.then_inc(gate_ps, 1)

            def project_rows(n):
                pe.wait_ge(weighted, n * B + B)
                turn(att, gT_ps)
                pe.wait_ge(gT_sb, n * 2 + 2)
                for b in range(B):
                    for c in range(KC):
                        i = mm(ps[:, A0 + b // 2, (b % 2) * D:(b % 2 + 1) * D], xtf[:, c, b * P:(b + 1) * P],
                               w_out[:, c], start=c == 0, stop=c == KC - 1)
                i.then_inc(wout_ps, 1)

            def queries(m):
                pe.wait_ge(ln_out[LN_1], m * B + B)
                turn(x1, x1T_ps)
                pe.wait_ge(x1T_sb, m * 2 + 2)
                for half in range(KC):
                    for c in range(KC):
                        i = mm(ps[:, A0 + half, :], c_q[:, c, half * P:(half + 1) * P], xtf[:, c],
                               start=c == 0, stop=c == KC - 1)
                    i.then_inc(q_ps, 1)
                pe.wait_ge(q_sb, m * 2 + 2)

            def scores(m):
                for b in range(B):
                    for half in range(2):
                        if b:
                            pe.wait_ge(sc_sb, m * (2 * B) + (2 * b + half - 1))
                        for g in range(2):
                            rows = slice(QH * HD * g, QH * HD * (g + 1))
                            i = mm(ps[:, (UP, A0)[half] + g, 0:QH * SK],
                                   qT[rows, half, b * P:(b + 1) * P], keys[rows, half, b].rearrange("p h k -> p (h k)"),
                                   start=True, stop=True)
                        i.then_inc(sc_ps, 1)

            def turn_weights(m, b):
                pe.wait_ge(shares_done, m * B + (b + 1))
                for q in range(H // QH):
                    for h in range(QH):
                        i = nc.tensor.transpose(ps[0:SK, TURNED[q], h * P:(h + 1) * P], probs[:, b, q * QH + h], ident[:, :])
                    i.then_inc(eT_ps, 1)

            def weigh_values(m, b):
                pe.wait_ge(eT_sb, m * (4 * B) + (4 * b + 4))
                for h in range(H):
                    rows = slice(h % 8 // 2 * 2 * HD, (h % 8 // 2 + 1) * 2 * HD)
                    i = mm(ps[rows, WEIGHED[h // 8], b * P:(b + 1) * P], vals[:, b, h], eT[0:SK, h], start=h % 2 == 0, stop=h % 2 == 1,
                           tile_position=(0, rows.start))
                    if b == B - 1 and h % 8 == 7:
                        i.then_inc(attT_ps, 1)

            def project(m):
                pe.wait_ge(attT_sb, m * 2 + 2)
                for b in range(B):
                    o = ps[:, A0 + b // 2, (b % 2) * D:(b % 2 + 1) * D]
                    mm(o, ones[0:1, :], c_bo[:, :], start=True, stop=False)
                    for c in range(KC):
                        i = mm(o, xtf[:, c, b * P:(b + 1) * P], c_o[:, c], start=False, stop=c == KC - 1)
                i.then_inc(wo_ps, 1)

            def router(m):
                pe.wait_ge(ln_out[LN_2], m * B + B)
                turn(x2, x2T_ps)
                pe.wait_ge(x2T_sb, m * 2 + 2)
                for b in range(B):
                    o = ps[:, A0, b * 2 * NR:(b + 1) * 2 * NR]
                    for c in range(KC):
                        mm(o, x2T[:, c, b * P:(b + 1) * P], cent[:, c].rearrange("p n e -> p (n e)"), start=c == 0, stop=False)
                    i = mm(o, ones[0:1, :], r_bias[:, :, :].rearrange("a n e -> a (n e)"), start=False, stop=True)
                i.then_inc(rt_ps, 1)

            def places(m):
                pe.wait_ge(picked, m + 1)
                mm(ps[:, GATHER, 0:(B + 1) * NR], before[:, :], chosen[:, :, :].rearrange("g b e -> g (b e)"), start=True, stop=False)
                for b in range(B):
                    i = mm(ps[:, GATHER, (b + 1) * NR:(B + 1) * NR], ones[:, :],
                           chosen[:, b].unsqueeze(1).to_broadcast([P, B - b, NR]), start=False, stop=b == B - 1)
                i.then_inc(pos_ps, 1)

            def shared(m, e, between=lambda: None):
                par = e % 2
                pe.wait_ge(expert_in[par], m * (16 * NE) + 32 * (e // 2 + 1))
                if e == 0:
                    pe.wait_ge(x2T_sb, m * 2 + 2)
                for g in range(FG):
                    pe.wait_ge(sh_gelu, m * (2 * FG) + (e * FG + g + 1))
                    for c in range(KC):
                        ins = mm(ps[:, UP + g % 2, :], fc[:, par, c, g * P:(g + 1) * P], x2T[:, c],
                                 start=c == 0, stop=c == KC - 1)
                    ins.then_inc(sh_ps, 1)
                between()
                if e == 0:
                    pe.wait_ge(acc_sb, m * 2 + 1)
                for g in range(FG):
                    pe.wait_ge(sh_gelu, m * (2 * FG) + (e * FG + g + 3))
                    for b in range(B):
                        ins = mm(ps[:, ACC + b // 2, (b % 2) * D:(b % 2 + 1) * D], hT[:, g, b * P:(b + 1) * P], pj[:, par, g],
                                 start=e == 0 and g == 0 and b % 2 == 0, stop=False)
                ins.then_inc(expert_used[par], 1)

            def load_bounds(m, experts):
                pe.wait_ge(bounds_done, m + 1)
                pe.sem_inc(bounds_seen_pe, 1)
                edges = [pe.value_load(bounds[0:1, e - NSH:e - NSH + 1], min_val=0, max_val=TILES * NR * MAX_PASSES)
                         for e in (*experts, experts[-1] + 1)]
                return dict(zip(experts, zip(edges, edges[1:])))

            def routed(m, e, lo, hi):
                par = e % 2
                pe.wait_ge(expert_in[par], m * (16 * NE) + 32 * (e // 2 + 1))
                pe.wait_ge(sel_first, m * NR + (e - NSH + 1))
                with pe.If(lo < hi), pe.Fori(lo, hi) as n:
                    pe.wait_ge(sel_next, n + 1)
                    for c in range(KC):
                        for b in range(B):
                            i = mm(ps[:, GATHER, c * P:(c + 1) * P], x2f[:, b, c * P:(c + 1) * P], sel[:, par, b],
                                   start=b == 0, stop=b == B - 1)
                    i.then_inc(gather_ps, 1)
                    pe.wait_ge(selw_done, n * B + B)
                    for b in range(B):
                        i = nc.tensor.transpose(ps[:, PRE, b * P:(b + 1) * P], sel_w[:, b], ident[:, :])
                    i.then_inc(selT_ps, 1)
                    pe.wait_ge(xg_sb, n + 1)
                    for g in range(FG):
                        for c in range(KC):
                            i = mm(ps[:, UP + g // 4, g % 4 * P:(g % 4 + 1) * P], fc[:, par, c, g * P:(g + 1) * P], xg[:, c],
                                   start=c == 0, stop=c == KC - 1)
                        if g % 4 == 3:
                            i.then_inc(up_ps, 1)
                    for c in range(KC):
                        for g in range(FG):
                            if c == 0 and g % 4 == 0:
                                pe.wait_ge(gelu_done, n * 2 + (g // 4 + 1))
                            i = mm(ps[:, UP + c, 0:P], hT[:, g, 0:P], pj[:, par, g, c * P:(c + 1) * P],
                                   start=g == 0, stop=g == FG - 1)
                        i.then_inc(y_ps, 1)
                    pe.wait_ge(selT_sb, n + 1)
                    for c in range(KC):
                        pe.wait_ge(y_sb, n * KC + (c + 1))
                        for b in range(B):
                            at = (b % 2) * D + c * P
                            mm(ps[:, ACC + b // 2, at:at + P], selT[:, b], y[:, c * P:(c + 1) * P], start=False, stop=False)
                pe.sem_inc(expert_used[par], 1)

            def residual(m):
                pe.wait_ge(x2f_sb, m + 1)
                for b in range(B):
                    i = mm(ps[:, ACC + b // 2, (b % 2) * D:(b % 2 + 1) * D], twice[:, :], x2f[:, b], start=False, stop=b % 2 == 1)
                i.then_inc(acc_ps, 1)

            def last_experts(f, between):
                bounds_of = load_bounds(f, EXPERTS[LATE:]) if f is not None else {}
                for e, part in zip(EXPERTS[LATE:], between):
                    part()
                    if f is not None:
                        routed(f, e, *bounds_of[e])
                if f is not None:
                    residual(f)

            def period(p, m=None, f=None, bound=False, preps=Q, upcoming=None):
                def prep(q):
                    if q < preps:
                        prepare(p * (Q // 2) + (q // 2 + 1), q % 2)

                def banks_read(q):
                    done = p * Q + (min(q, preps - 1) + 3)
                    pe.wait_ge(kv_sb, min(done, NBLK) if isinstance(p, int) else done)

                def start():
                    prep(0)
                    if bound:
                        banks_read(0)
                        project_rows(m - FIRST_BOUND)

                def attend():
                    if m is not None:
                        banks_read(0)
                        queries(m)
                        scores(m)
                        pe.wait_ge(sc_sb, m * (2 * B) + 2 * B)

                def weigh():
                    if bound and upcoming is not None:
                        gate_rows(upcoming - FIRST_BOUND)
                        pe.wait_ge(gate_sb, upcoming - FIRST_BOUND + 1)
                    if m is not None:
                        for b in range(B):
                            turn_weights(m, b)
                            weigh_values(m, b)
                        pe.wait_ge(attT_sb, m * 2 + 2)
                    prep(1)

                def finish():
                    if m is not None:
                        banks_read(1)
                        project(m)

                def place():
                    if m is not None:
                        places(m)
                    if not bound:
                        prep(2)

                last_experts(f, (start, attend, weigh, finish, lambda: None))
                if m is None:
                    place()
                    prep(3)
                else:
                    router(m)
                    shared(m, 0, place)
                    shared(m, 1, lambda: prep(2 if bound else 3))
                if upcoming is not None and not bound:
                    banks_read(3)
                    gate_rows(upcoming - FIRST_BOUND)
                if m is not None:
                    own = EXPERTS[NSH:] if bound else EXPERTS[NSH:LATE]
                    bounds_of = load_bounds(m, own)
                    for e in own:
                        if bound and e == NSH + 2:
                            prep(3)
                        routed(m, e, *bounds_of[e])
                if bound:
                    residual(m)

            pe.wait_ge(pool_const, 1)
            pe.wait_ge(attn_w_in, 5 * 16)
            prepare(0, 0)
            prepare(0, 1)
            pe.wait_ge(ctx_in, 6 * 16)
            for half in range(KC):
                for c in range(KC):
                    i = mm(ps[:, UP + half, 0:B * SK], hT[:, 2 + c, half * P:(half + 1) * P], hT[:, c, 0:B * SK],
                           start=c == 0, stop=c == KC - 1)
                i.then_inc(ctx_k_ps, 1)
            for b in range(B):
                for c in range(KC):
                    i = mm(ps[0:SK, ACC + b // 2, (b % 2) * D:(b % 2 + 1) * D], hT[:, c, b * SK:(b + 1) * SK],
                           hT[:, 4 + c, 0:D], start=c == 0, stop=c == KC - 1)
                i.then_inc(ctx_v_ps, 1)
            pe.wait_ge(xattn_w_in, 10 * 16)
            pe.wait_ge(ctx_done, KC + 2 * B)
            period(0, 0)
            with pe.Fori(1, FIRST_BOUND) as p:
                period(p, p, p - 1)
            period(5, None, 4, upcoming=5)
            period(6, 5, bound=True, upcoming=6)
            period(7, 6, bound=True, preps=NBLK - 7 * Q - 2, upcoming=7)
            period(8, 7, bound=True, preps=0)

        @block.scalar
        def _(act):
            fn = nc.scalar.activation

            def prepare(blk, par):
                act.wait_ge(prep_a_ps, blk + 1)
                fn(xf1T[:, :], ps[0:HD, PRE, 0:P], ACT.Copy).then_inc(xf1_sb, 1)
                fn(graw[:, :], ps[:, PRE, P:P + H], ACT.Copy).then_inc(xf1_sb, 1)
                act.wait_ge(xf1_sb, blk * 2 + 2)
                if not isinstance(blk, int) or blk >= 2:
                    act.wait_ge(block_laid, blk * LAY - LAY)
                fn(beta[:, par], graw[:, :], ACT.Sigmoid).then_inc(fq_sb, 1)
                act.wait_ge(prep_b_ps, blk + 1)
                fn(fbuf[:, par], ps[:, PRE, D:2 * D], ACT.Sigmoid).then_inc(fq_sb, 1)
                fn(act3[:, par, 2], ps[:, A1, 0:D], ACT.Silu).then_inc(fq_sb, 1)
                fn(act3[:, par, 0:2].rearrange("p c d -> p (c d)"), ps[:, A0, :], ACT.Silu).then_inc(kv_sb, 1)

            def out_of_banks(dst, ready, done, m, scale=1.0):
                for c in range(KC):
                    act.wait_ge(ready, m * 2 + (c + 1))
                    fn(dst[:, c], ps[:, A0 + c, :], ACT.Copy, scale=scale).then_inc(done, 1)

            def gate_rows(n):
                out_of_banks(xtf, gx_ps, gx_sb, n)
                act.wait_ge(xo1_ps, n + 1)
                fn(xo1T, ps[0:HD, A0, :], ACT.Copy).then_inc(xo1_sb, 1)
                act.wait_ge(gate_ps, n + 1)
                fn(halves(gate[:, :, :]), ps[:, A0:A0 + 2, :], ACT.Sigmoid).then_inc(gate_sb, 1)

            def project_rows(n):
                out_of_banks(xtf, gT_ps, gT_sb, n)

            def queries(m):
                out_of_banks(xtf, x1T_ps, x1T_sb, m)
                out_of_banks(qT, q_ps, q_sb, m, -QSCALE)

            def scores(m):
                for b in range(B):
                    for half in range(2):
                        act.wait_ge(sc_ps, m * (2 * B) + (2 * b + half + 1))
                        first = (UP, A0)[half]
                        fn(probs[:, b, half * 8:(half + 1) * 8].rearrange("g (q h) k -> g q (h k)", q=2),
                           ps[:, first:first + 2, 0:QH * SK], ACT.Copy).then_inc(sc_sb, 1)

            def exponentials(m, b):
                act.wait_ge(min_done, m * B + (b + 1))
                for h in range(H):
                    i = fn(probs[:, b, h], probs[:, b, h], ACT.Exp, bias=least[:, b, h:h + 1], scale=-1.0,
                           accum_out=weight_sum[:, b, h:h + 1])
                i.then_inc(exp_done, 1)

            def turn_weights(m, b):
                for q in range(H // QH):
                    act.wait_ge(eT_ps, m * (4 * B) + (4 * b + q + 1))
                    fn(eT[0:SK, q * QH:(q + 1) * QH].rearrange("k h g -> k (h g)"), ps[0:SK, TURNED[q], :], ACT.Copy
                       ).then_inc(eT_sb, 1)

            def weighed(m):
                for c in range(KC):
                    act.wait_ge(attT_ps, m * 2 + (c + 1))
                    fn(xtf[:, c], ps[:, WEIGHED[c], :], ACT.Copy).then_inc(attT_sb, 1)

            def router(m):
                out_of_banks(x2T, x2T_ps, x2T_sb, m)
                act.wait_ge(rt_ps, m + 1)
                fn(rt[:, :, :].rearrange("g b e -> g (b e)"), ps[:, A0, 0:B * 2 * NR], ACT.Sigmoid).then_inc(rt_sb, 1)
                act.wait_ge(ln_out[LN_2], m * B + B)
                fn(x2f[:, :, :].rearrange("g b d -> g (b d)"), x2[:, :, :].rearrange("g b d -> g (b d)"), ACT.Copy
                   ).then_inc(x2f_sb, 1)

            def weights(m):
                act.wait_ge(route, m * ROUTE + 14)
                fn(rone[:, 5], rone[:, 4], ACT.Sigmoid).then_inc(w_done, 1)
                fn(rone[:, 6], rone[:, 4], ACT.Sigmoid, scale=-1.0).then_inc(w_done, 1)

            def shared(m, e, between=lambda: None):
                for g in range(FG):
                    act.wait_ge(sh_ps, m * (2 * FG) + (e * FG + g + 1))
                    fn(hT[:, g], ps[:, UP + g % 2, :], ACT.Gelu).then_inc(sh_gelu, 1)
                between()

            def load_bounds(m, experts):
                act.wait_ge(bounds_done, m + 1)
                act.sem_inc(bounds_seen_act, 1)
                edges = [act.value_load(bounds[0:1, e - NSH:e - NSH + 1], min_val=0, max_val=TILES * NR * MAX_PASSES)
                         for e in (*experts, experts[-1] + 1)]
                return dict(zip(experts, zip(edges, edges[1:])))

            def select(e, at, far, far_count, done):
                for b in range(B):
                    fn(sel[:, e % 2, b], slots[:, at], ACT.Abs, bias=neg_slot[:, b, e - NSH:e - NSH + 1]).then_inc(far, 1)
                act.wait_ge(far, far_count)
                fn(sel[:, e % 2], sel[:, e % 2], ACT.Relu, scale=-1.0, bias=1.0).then_inc(done, 1)

            def select_first(m, e, n):
                count = m * NR + (e - NSH)
                act.wait_ge(sel_first, count)
                act.wait_ge(sel_next, n + 1)
                select(e, slice(0, P), far_first, count * B + B, sel_first)

            def routed_experts(m, experts, before=()):
                bounds_of = load_bounds(m, experts)
                select_first(m, experts[0], bounds_of[experts[0]][0])
                for i, e in enumerate(experts):
                    if e + 1 in experts:
                        select_first(m, e + 1, bounds_of[e][0])
                    if i < len(before):
                        before[i]()
                    routed(m, e, *bounds_of[e])

            def routed(m, e, lo, hi):
                r = e - NSH
                act.wait_ge(sel_first, m * NR + (r + 1))
                fn(tiny[:, :], tiny[:, :], ACT.Gelu).then_inc(warm, 1)
                with act.If(lo < hi), act.Fori(lo, hi) as n:
                    following = nc.s_assert_within(n + 1 - lo, 1, MAX_PASSES, skip_runtime_bounds_check_because=
                                                   "a pass is counted for each 128 of the tile's 512 tokens at most")
                    act.wait_ge(sel_next, n + 1)
                    for b in range(B):
                        fn(sel_w[:, b], sel[:, e % 2, b], ACT.Relu, scale=w_tok[:, b, r:r + 1]).then_inc(selw_done, 1)
                    act.wait_ge(gather_ps, n + 1)
                    fn(xg[:, :, :].rearrange("p c n -> p (c n)"), ps[:, GATHER, 0:KC * P], ACT.Copy).then_inc(xg_sb, 1)
                    act.wait_ge(selT_ps, n + 1)
                    fn(selT[:, :, :].rearrange("p b n -> p (b n)"), ps[:, PRE, :], ACT.Copy).then_inc(selT_sb, 1)
                    for k in range(2):
                        act.wait_ge(up_ps, n * 2 + (k + 1))
                        fn(hT[:, 4 * k:4 * k + 4, 0:P], ps[:, UP + k, :].rearrange("p (g n) -> p g n", g=4), ACT.Gelu
                           ).then_inc(gelu_done, 1)
                    select(e, bass.ds(following * P, P), far_next, n * B + B, sel_next)
                    for c in range(KC):
                        act.wait_ge(y_ps, n * KC + (c + 1))
                        fn(y[:, c * P:(c + 1) * P], ps[:, UP + c, 0:P], ACT.Copy).then_inc(y_sb, 1)

            def sums(m):
                act.wait_ge(acc_ps, m + 1)
                act.wait_ge(out_stored, m * 16 + 1)
                for a in range(2):
                    fn(halves(y_out[:, :, :])[:, a], ps[:, ACC + a, :], ACT.Copy).then_inc(acc_sb, 1)

            def last_experts(f, between):
                if f is not None:
                    routed_experts(f, EXPERTS[LATE:], between)
                    sums(f)
                else:
                    for part in between:
                        part()

            def period(p, m=None, f=None, bound=False, preps=Q, upcoming=None):
                def prep(q):
                    if q < preps:
                        prepare(p * Q + (q + 2), q % 2)

                def start():
                    prep(0)
                    if bound:
                        project_rows(m - FIRST_BOUND)

                def attend():
                    if m is not None:
                        queries(m)
                        scores(m)

                def weigh():
                    if bound and upcoming is not None:
                        gate_rows(upcoming - FIRST_BOUND)
                    if m is not None:
                        exponentials(m, 0)
                        for b in range(B):
                            if b + 1 < B:
                                exponentials(m, b + 1)
                            turn_weights(m, b)
                        weighed(m)
                    prep(1)

                def place():
                    if m is not None:
                        weights(m)
                    if not bound:
                        prep(2)

                last_experts(f, (start, attend, weigh, lambda: None, lambda: None))
                if m is None:
                    place()
                    prep(3)
                else:
                    router(m)
                    shared(m, 0, place)
                    shared(m, 1, lambda: prep(2 if bound else 3))
                if upcoming is not None and not bound:
                    gate_rows(upcoming - FIRST_BOUND)
                if m is not None:
                    own = EXPERTS[NSH:] if bound else EXPERTS[NSH:LATE]
                    routed_experts(m, own, (lambda: None, lambda: None, lambda: prep(3)) if bound else ())
                if bound:
                    sums(m)

            act.sem_inc(sh_gelu, 2)
            act.sem_inc(acc_sb, 1)
            act.sem_inc(sel_next, 1)
            prepare(0, 0)
            prepare(1, 1)
            act.wait_ge(pool_const, 1)
            period(0, 0)
            with act.Fori(1, FIRST_BOUND) as p:
                period(p, p, p - 1)
            period(5, None, 4, upcoming=5)
            period(6, 5, bound=True, upcoming=6)
            period(7, 6, bound=True, preps=NBLK - 7 * Q - 2, upcoming=7)
            period(8, 7, bound=True, preps=0)

        @block.gpsimd
        def _(pool):
            tt = nc.gpsimd.tensor_tensor

            def rsqrt(kind, n):
                pool.wait_ge(ln_mv[kind], n * B + B)
                tt(rstd[:, :], mv[:, :, 1], ln_eps[:, 0:B], ALU.add).then_inc(ln_rstd[kind], 1)
                pool.wait_ge(ln_rstd[kind], n * 2 + 1)
                tt(rstd[:, :], rstd[:, :], neg_half[:, 0:B], ALU.pow).then_inc(ln_rstd[kind], 1)

            heads = lambda a: a.rearrange("p (h d) -> p h d", h=H)
            by_head = lambda a: a.unsqueeze(2).to_broadcast([P, H, HD])

            def preparations(blk, par):
                k_silu = act3[:, par, 0]

                def tree_sum(src, dst):
                    return [lambda: tt(tree[:, :, 0:8], heads(src)[:, :, 0:8], heads(src)[:, :, 8:16], ALU.add),
                            lambda: tt(tree[:, :, 0:4], tree[:, :, 0:4], tree[:, :, 4:8], ALU.add),
                            lambda: tt(tree[:, :, 0:2], tree[:, :, 0:2], tree[:, :, 2:4], ALU.add),
                            lambda: tt(dst, tree[:, :, 0], tree[:, :, 1], ALU.add)]

                def k_square():
                    pool.wait_ge(kv_sb, blk + 1)
                    return tt(ksq[:, :], k_silu, k_silu, ALU.mult)

                def norm_floor():
                    pool.sem_inc(sum_seen, 1)
                    return nc.gpsimd.tensor_scalar(hsum[:, 0], hsum[:, 0], NORM_EPS * NORM_EPS, None, ALU.max)

                def power(some):
                    return tt(hsum[:, 1, some], hsum[:, 0, some], neg_half[:, some], ALU.pow)

                def k_normal():
                    if later(blk):
                        pool.wait_ge(block_laid, blk * LAY)
                    return tt(heads(tm[:, 1]), heads(k_silu), by_head(hsum[:, 1]), ALU.mult)

                ops = [k_square]
                ops += tree_sum(ksq[:, :], hsum[:, 0])
                ops += [norm_floor,
                        *[lambda h=h: power(slice(h, h + QH)) for h in range(0, H, QH)],
                        k_normal,
                        lambda: tt(fk[:, :], fbuf[:, par], tm[:, 1], ALU.mult),
                        lambda: tt(ksq[:, :], fk[:, :], tm[:, 1], ALU.mult)]
                ops += tree_sum(ksq[:, :], hsum[:, 2])
                ops += [lambda: tt(hsum[:, 3], beta[:, par], neg_one[:, :], ALU.mult),
                        lambda: tt(hsum[:, 2], hsum[:, 2], hsum[:, 3], ALU.mult),
                        lambda: tt(heads(tm[:, 0]), heads(fk[:, :]), by_head(hsum[:, 3]), ALU.mult),
                        lambda: tt(heads(ksq[:, :]), heads(tm[:, 1]), by_head(hsum[:, 2]), ALU.mult),
                        lambda: tt(ksq[:, :], ksq[:, :], fk[:, :], ALU.add),
                        lambda: tt(heads(tm[:, 2]), heads(ksq[:, :]), by_head(hsum[:, 3]), ALU.mult)]
                assert len(ops) == PREP
                return ops

            def prepare(blk, i, op):
                if i:
                    pool.wait_ge(prep_pool, blk * PREP + i)
                op().then_inc(prep_pool, 1)

            def steps(blk, par, keep, following=True, norms=()):
                ops = list(enumerate(preparations(blk + 1, 1 - par))) if following else []

                def place_v(t):
                    return nc.gpsimd.tensor_copy(prod[:, t % 2, 1, :, HD], vrec[:, :, t])

                def output_terms(t):
                    tt(oprod[:, t % (2 * OG):t % (2 * OG) + 2], S[:, t % RING:t % RING + 2],
                       rec[:, 4, :, t:t + 2].rearrange("p d t -> p t d").unsqueeze(2).to_broadcast([P, 2, HV, HD]),
                       ALU.mult).then_inc(o_terms, 1)

                pool.wait_ge(block_laid, blk * LAY + LAY)
                pool.sem_inc(block_seen, 1)
                place_v(0).then_inc(v_placed, 1)
                for t in range(T):
                    for h in range(2):
                        pool.wait_ge(step_done, blk * (T * STEP) + (t * STEP + 1 + h))
                        tt(terms[:, h, 0], S[:, (t - 1) % RING, h * HC:(h + 1) * HC],
                           rec[:, 3, :, t].unsqueeze(1).to_broadcast([P, HC, HD]), ALU.mult).then_inc(decayed, 1)
                        if h == 0 and t + 1 < T:
                            place_v(t + 1)
                    if keep and t and t % 2 == 0:
                        output_terms(t - 2)
                    for at, kind, n in norms:
                        if t == at:
                            rsqrt(kind, n)
                    budget = 1 if keep and t % 2 == 0 else 4
                    while t >= PREP_FROM and ops and PREP_COST[ops[0][0]] <= budget:
                        i, op = ops.pop(0)
                        prepare(blk + 1, i, op)
                        budget -= PREP_COST[i]
                assert not ops
                if keep:
                    pool.wait_ge(step_done, blk * (T * STEP) + (T * STEP + 2))
                    output_terms(T - 2)

            consts = 0

            def const(ins):
                nonlocal consts
                consts += 1
                ins.then_inc(pool_set, 1)

            def ordered():
                pool.wait_ge(pool_set, consts)

            memset, select = nc.gpsimd.memset, nc.gpsimd.affine_select
            for dst, value in ((ident[:, :], 0.0), (twice[:, :], 0.0), (before[:, :], 1.0), (ones[:, :], 1.0), (head_mask[:, :], 1.0),
                               (lower[:, :, :], 1.0), (neg_half[:, :], -0.5), (neg_one[:, :], -1.0), (ln_eps[:, :], LN_EPS),
                               (o_rows[:, :, :], 0.0), (r_bias[:, 0], 0.0), (chosen[:, B], 0.0), (tiny[:, :], 0.0)):
                const(memset(dst, value))
            for dst, step, n, base in ((index8[:, :], 1, NR, -NR), (slots[:, :], 1, W + P, 0), (pass_at[:, :], P, MAX_PASSES, 0)):
                const(nc.gpsimd.iota(dst, pattern=[[step, n]], base=base, channel_multiplier=0,
                                     allow_small_or_imprecise_dtypes=True))
            ordered()
            const(select(out=ident[:, :], in_=ident[:, :], compare_op=ALU.not_equal, fill=1.0, base=0, pattern=[[-1, P]],
                         channel_multiplier=1))
            const(select(out=twice[:, :], in_=twice[:, :], compare_op=ALU.not_equal, fill=2.0, base=0, pattern=[[-1, P]],
                         channel_multiplier=1))
            const(select(out=before[:, :], in_=before[:, :], compare_op=ALU.is_gt, fill=0.0, base=0, pattern=[[1, P]],
                         channel_multiplier=-1))
            const(select(out=lower[:, :, :], in_=lower[:, :, :], compare_op=ALU.is_gt, fill=0.0, base=0,
                         pattern=[[1, NR + 1], [-1, NR]], channel_multiplier=0))
            const(select(out=head_mask[:, :], in_=head_mask[:, :], compare_op=ALU.is_ge, fill=0.0, base=0, pattern=[[-HD, 8]],
                         channel_multiplier=1))
            ordered()
            select(out=head_mask[:, :], in_=head_mask[:, :], compare_op=ALU.is_ge, fill=0.0, base=HD - 1, pattern=[[HD, 8]],
                   channel_multiplier=-1).then_inc(pool_const, 1)
            for i, op in enumerate(preparations(0, 0)):
                prepare(0, i, op)

            def period(p, at, norms, keep=False):
                for q in range(Q):
                    blk = p * Q + q
                    steps(blk, q % 2, keep and blk >= KEEP, not isinstance(p, int) or blk + 1 < NBLK,
                          [(at[kind] + 1 - q * T, kind, n) for kind, n in norms])

            period(0, FREE_AT, ((LN_1, 0), (LN_2, 0)))
            with pool.Fori(1, FIRST_BOUND) as p:
                period(p, FREE_AT, ((LN_1, p), (LN_2, p), (LN_3, p - 1)))
            period(5, FREE_AT, ((LN_3, 4),), True)
            period(6, BOUND_AT, ((LN_GATE, 0), (LN_1, 5), (LN_2, 5)), True)
            period(7, BOUND_AT, ((LN_GATE, 1), (LN_1, 6), (LN_2, 6), (LN_3, 5)), True)
            for kind, n in (LN_GATE, 2), (LN_1, 7), (LN_2, 7), (LN_3, 6), (LN_3, 7):
                rsqrt(kind, n)

        @block.vector
        def _(dve):
            tt = nc.vector.tensor_tensor
            red = nc.vector.tensor_reduce

            def due(t, first, count, at_once=1):
                return [i for i in range(count) if first + i // at_once == t]

            def layer_norm(t, at, kind, n, src, dst, ready=None):
                if t == at:
                    if ready is not None:
                        dve.wait_ge(*ready)
                    for b in range(B):
                        nc.vector.bn_stats(stats[:, b], src[:, b]).then_inc(ln_stats[kind], 1)
                    dve.wait_ge(ln_stats[kind], n * B + B)
                    dve.sem_inc(ln_seen[kind], 1)
                    for b in range(B):
                        nc.vector.bn_aggr(mv[:, b], stats[:, b]).then_inc(ln_mv[kind], 1)
                if t == at + 1:
                    dve.wait_ge(ln_rstd[kind], n * 2 + 2)
                    for b in range(B):
                        nc.vector.tensor_scalar(dst[:, b], src[:, b], mv[:, b, 0:1], rstd[:, b:b + 1], ALU.subtract, ALU.mult
                                                ).then_inc(ln_out[kind], 1)

            def add_banks(t, at, dst, ready, done):
                for a in due(t, at, 2, 2):
                    dve.wait_ge(*ready)
                    tt(halves(dst)[:, a], ps[:, A0 + a, :], halves(dst)[:, a], ALU.add).then_inc(done, 1)

            def caps(t, m):
                if t == 0:
                    dve.wait_ge(mask_in, m * 16 + 16)
                    nc.vector.tensor_scalar(cap[:, :, :], imask[:, :, :], 0.0, -HUGE, ALU.not_equal, ALU.mult).then_inc(cap_half, 1)
                if t == 1:
                    dve.wait_ge(cap_half, m + 1)
                    nc.vector.tensor_scalar(cap[:, :, :], cap[:, :, :], MASKED, None, ALU.add).then_inc(cap_done, 1)

            def bound_rows(t, n, at):
                for a in due(t, at["gated"], 2, 2):
                    dve.wait_ge(gate_sb, n + 1)
                    dve.wait_ge(o_stored, n * (Q * B * 16) + ((FIRST_BOUND * Q + Q - KEEP) * B * 16 + 1))
                    tt(halves(att)[:, a], halves(o_rows[:, :, :])[:, a], halves(gate[:, :, :])[:, a], ALU.mult).then_inc(gated, 1)
                layer_norm(t, at[LN_GATE], LN_GATE, n, att, att, (gated, n * 2 + 2))
                for b in due(t, at["weighted"], B, B):
                    dve.wait_ge(ln_out[LN_GATE], n * B + (b + 1))
                    tt(att[:, b], att[:, b], lnw[:, :], ALU.mult).then_inc(weighted, 1)
                add_banks(t, at["x_plus"], xin[:, :, :], (wout_ps, n + 1), x_plus)

            def minima(t, m, at):
                for i in due(t, at, 2 * B, 2):
                    b = i // 2
                    if i % 2 == 0:
                        dve.wait_ge(cap_done, m + 1)
                        dve.wait_ge(sc_sb, m * (2 * B) + (2 * b + 2))
                        tt(probs[:, b], probs[:, b], cap[:, b].unsqueeze(1).to_broadcast([P, H, SK]), ALU.max).then_inc(capped, 1)
                    else:
                        dve.wait_ge(capped, m * B + (b + 1))
                        red(least[:, b], probs[:, b], AX.X, ALU.min).then_inc(min_done, 1)

            def shares(t, m, b, at):
                if t == at:
                    dve.wait_ge(exp_done, m * B + (b + 1))
                    if b:
                        dve.wait_ge(shares_done, m * B + b)
                    nc.vector.reciprocal(rden[:, :], weight_sum[:, b]).then_inc(rden_done, 1)
                    dve.wait_ge(rden_done, m * B + (b + 1))
                    tt(probs[:, b], probs[:, b], rden[:, :].unsqueeze(2).to_broadcast([P, H, SK]), ALU.mult).then_inc(shares_done, 1)

            def routing(m, part):
                raw_s, biased = rt[:, :, 0:NR], rt[:, :, NR:2 * NR]
                wide = lambda i: rone[:, i].unsqueeze(2).to_broadcast([P, B, NR])
                index = index8[:, :].unsqueeze(1).to_broadcast([P, B, NR])
                first_hot, second_hot = rbuf[:, 2], rbuf[:, 6]
                ts, copy = nc.vector.tensor_scalar, nc.vector.tensor_copy
                n = ROUTE_PARTS[part]

                def then(ins):
                    nonlocal n
                    n += 1
                    ins.then_inc(route, 1)

                def after():
                    dve.wait_ge(route, m * ROUTE + n)

                def highest(scores, top):
                    then(red(rone[:, top], scores, AX.X, ALU.max))

                def equal_first(scores, top, r):
                    after()
                    then(tt(rbuf[:, r], scores, wide(top), ALU.is_equal))
                    after()
                    then(tt(rbuf[:, r + 1], rbuf[:, r], index, ALU.mult))
                    after()
                    then(red(rone[:, top + 1], rbuf[:, r + 1], AX.X, ALU.min))
                    after()
                    then(tt(rbuf[:, r + 2], index, wide(top + 1), ALU.is_equal))

                if part == 0:
                    dve.wait_ge(rt_sb, m + 1)
                    highest(biased, 0)
                if part == 1:
                    equal_first(biased, 0, 0)
                if part == 2:
                    after()
                    then(nc.vector.scalar_tensor_tensor(rbuf[:, 3], first_hot, -4.0, biased, ALU.mult, ALU.add))
                    after()
                    highest(rbuf[:, 3], 2)
                if part == 3:
                    equal_first(rbuf[:, 3], 2, 4)
                if part == 4:
                    after()
                    tt(chosen[:, 0:B], first_hot, second_hot, ALU.add).then_inc(picked, 1)
                    then(tt(rbuf[:, 7], first_hot, second_hot, ALU.subtract))
                    after()
                    then(tt(rbuf[:, 7], rbuf[:, 7], raw_s, ALU.mult))
                    after()
                    then(red(rone[:, 4], rbuf[:, 7], AX.X, ALU.add))
                if part == 5:
                    dve.wait_ge(picked, m + 1)
                    then(ts(neg_slot[:, :, :], chosen[:, 0:B], FAR, -FAR, ALU.mult, ALU.add))
                    after()
                    dve.wait_ge(pos_ps, m + 1)
                    then(tt(neg_slot[:, :, :], neg_slot[:, :, :], ps[:, GATHER, 0:B * NR].rearrange("g (b e) -> g b e", b=B),
                            ALU.subtract))
                    total = ps[0:1, GATHER, B * NR:B * NR + NR].unsqueeze(2).to_broadcast([1, NR, MAX_PASSES])
                    then(tt(over[:, :, :], total, pass_at[:, :].unsqueeze(1).to_broadcast([1, NR, MAX_PASSES]), ALU.is_gt))
                    after()
                    then(red(passes[:, :], over[:, :, :], AX.X, ALU.add))
                    after()
                    then(tt(lterm[:, :, :], lower[:, :, :], passes[:, :].unsqueeze(1).to_broadcast([1, NR + 1, NR]), ALU.mult))
                    after()
                    then(red(first_pass[:, :], lterm[:, :, :], AX.X, ALU.add))
                    after()
                    then(tt(first_pass[:, :], first_pass[:, :], pass_base[:, :].to_broadcast([1, NR + 1]), ALU.add))
                    after()
                    then(copy(pass_base[:, :], first_pass[:, NR:NR + 1]))
                if part == 6:
                    dve.wait_ge(w_done, m * 2 + 2)
                    then(tt(rbuf[:, 0], first_hot, wide(5), ALU.mult))
                    then(tt(rbuf[:, 1], second_hot, wide(6), ALU.mult))
                    after()
                    then(tt(w_tok[:, :, :], rbuf[:, 0], rbuf[:, 1], ALU.add))
                    after()
                    copy(bounds[:, :], first_pass[:, :]).then_inc(bounds_done, 1)
                assert n == ROUTE_PARTS[part + 1]

            def attention_after(t, m, bound, at):
                caps(t, m)
                if bound:
                    n = m - FIRST_BOUND
                    bound_rows(t, n, at)
                    layer_norm(t, at[LN_1], LN_1, m, xin[:, :, :], x1[:, :, :], (x_plus, n * 2 + 2))
                else:
                    layer_norm(t, at[LN_1], LN_1, m, xin[:, :, :], x1[:, :, :], (tile_in, m * 16 + 16))
                minima(t, m, at["minima"])
                for b in range(B):
                    shares(t, m, b, at["shares"][b])
                add_banks(t, at["resid"], x1[:, :, :], (wo_ps, m + 1), resid)
                layer_norm(t, at[LN_2], LN_2, m, x1[:, :, :], x2[:, :, :], (resid, m * 2 + 2))
                for part, lag in enumerate(ROUTE_LAGS):
                    if t == at["routing"] + lag:
                        routing(m, part)

            def last_norm(t, m, at):
                layer_norm(t, at, LN_3, m, y_out[:, :, :], y_out[:, :, :], (acc_sb, m * 2 + 3))

            def lay_out(blk, par, kept=False):
                dve.wait_ge(prep_pool, blk * PREP + PREP)
                if later(blk):
                    dve.wait_ge(decayed, blk * (2 * T))
                    dve.wait_ge(step_done, blk * (T * STEP) + 2)
                nc.vector.transpose(vrec[:, :, :], act3[:, par, 1].rearrange("p (g v) -> p v g", v=HV)).then_inc(block_laid, 1)
                for i, src in enumerate((tm[:, 0], tm[:, 1], tm[:, 2], fbuf[:, par], act3[:, par, 2])):
                    wide = src.rearrange("p (h d) -> p d h", h=H).unsqueeze(3).to_broadcast([P, HD, H, 2])
                    if i == 4 and kept:
                        dve.wait_ge(o_terms, (blk - KEEP) * (T // 2))
                    nc.vector.transpose(rec[:, i], wide).then_inc(block_laid, 1)

            def outputs(blk, g):
                dve.wait_ge(o_terms, (blk - KEEP) * (T // 2) + (g + 1) * (OG // 2))
                red(osum[:, g * OG:(g + 1) * OG].rearrange("p t v -> p (t v)"),
                    oprod[:, g % 2 * OG:(g % 2 + 1) * OG].rearrange("p t v d -> p (t v) d"), AX.X, ALU.add).then_inc(o_sums, 1)

            def steps(blk, keep, after=lambda t: None):
                base = blk * (T * STEP) + 2
                dve.wait_ge(block_laid, blk * LAY + LAY)
                for t in range(T):
                    at = base + t * STEP
                    for h in range(2):
                        cols = slice(h * HC, (h + 1) * HC)
                        dve.wait_ge(step_done, at + (h - 1))
                        tt(prod[:, t % 2, :, cols, 0:HD],
                           S[:, (t - 1) % RING, cols].unsqueeze(1).to_broadcast([P, 2, HC, HD]),
                           rec[:, 1:3, :, t].unsqueeze(2).to_broadcast([P, 2, HC, HD]), ALU.mult).then_inc(step_done, 1)
                    for h in range(2):
                        dve.wait_ge(step_done, at + (1 + h))
                        if h == 0 and t == 0:
                            dve.wait_ge(v_placed, blk + 1)
                        red(u[:, h], prod[:, t % 2, :, h * HC:(h + 1) * HC], AX.X, ALU.add).then_inc(step_done, 1)
                    for h in range(2):
                        dve.wait_ge(step_done, at + (3 + h))
                        if h == 0:
                            dve.wait_ge(decayed, blk * (2 * T) + (2 * t + 2))
                        tt(terms[:, h, 1:3], u[:, h].unsqueeze(3).to_broadcast([P, 2, HC, HD]),
                           rec[:, 0:2, :, t].unsqueeze(2).to_broadcast([P, 2, HC, HD]), ALU.mult).then_inc(step_done, 1)
                    for h in range(2):
                        dve.wait_ge(step_done, at + (5 + h))
                        red(S[:, t % RING, h * HC:(h + 1) * HC].rearrange("p v d -> p (v d)"),
                            terms[:, h].rearrange("p n v d -> p (v d) n"), AX.X, ALU.add).then_inc(step_done, 1)
                    if keep and t > OG and t % OG == OG // 2:
                        outputs(blk, t // OG - 1)
                    after(t)

            def last_outputs(blk):
                n = blk - KEEP
                outputs(blk, T // OG - 1)
                dve.wait_ge(o_sums, n * (T // OG) + T // OG)
                dve.wait_ge(o_stored, n * (B * 16) + 1)
                nc.vector.transpose(otm[:, :, :, :].rearrange("p h a v -> p v (h a)"),
                                    osum[:, :, :].rearrange("p t v -> p v t")).then_inc(o_ready, 1)

            def period(p, m=None, f=None, bound=False, keep=False):
                at = BOUND_AT if bound else FREE_AT

                def after(t):
                    if m is not None:
                        attention_after(t, m, bound, at)
                    if f is not None:
                        last_norm(t, f, at[LN_3])

                for q in range(Q):
                    blk = p * Q + q
                    kept = keep and blk >= KEEP
                    steps(blk, kept, lambda t: after(q * T + t))
                    if not isinstance(p, int) or blk + 1 < NBLK:
                        lay_out(blk + 1, (q + 1) % 2, kept)
                    if kept:
                        last_outputs(blk)

            for h in range(2):
                nc.vector.memset(S[:, RING - 1, h * HC:(h + 1) * HC], 0.0).then_inc(step_done, 1)
            nc.vector.memset(prod[:, :, 0, :, HD], 0.0).then_inc(dve_const, 1)
            nc.vector.memset(vals[:, :, :, :], 0.0).then_inc(dve_const, 1)
            nc.vector.memset(pass_base[:, :], 0.0).then_inc(dve_const, 1)
            dve.wait_ge(pool_const, 1)
            red(quad_mask[:, :], head_mask[:, :].rearrange("p (g j) -> p j g", j=QH), AX.X, ALU.add).then_inc(dve_const, 1)
            dve.wait_ge(dve_const, 4)
            for c in range(KC):
                dve.wait_ge(ctx_k_ps, c + 1)
                tt(keys[:, c], ps[:, UP + c, 0:B * SK].rearrange("p (b k) -> p b k", b=B).unsqueeze(2).to_broadcast([P, B, QH, SK]),
                   quad_mask[:, :].unsqueeze(1).unsqueeze(3).to_broadcast([P, B, QH, SK]), ALU.mult).then_inc(ctx_done, 1)
            for b in range(B):
                dve.wait_ge(ctx_v_ps, b // 2 * 2 + 2)
                for odd in range(2):
                    nc.vector.tensor_copy(
                        vals[:, b].rearrange("k (h o) d -> k o h d", o=2)[:, odd, :, odd * HD:(odd + 1) * HD],
                        ps[0:SK, ACC + b // 2, (b % 2) * D:(b % 2 + 1) * D].rearrange("k (h o d) -> k o h d", o=2, d=HD)[:, odd]
                    ).then_inc(ctx_done, 1)
            lay_out(0, 0)
            period(0, 0)
            with dve.Fori(1, FIRST_BOUND) as p:
                period(p, p, p - 1)
            period(5, None, 4, keep=True)
            period(6, 5, bound=True, keep=True)
            period(7, 6, 5, bound=True, keep=True)
            for t in range(P):
                attention_after(t, 7, True, BOUND_AT)
                last_norm(t, 6, BOUND_AT[LN_3])
            for t in range(2):
                last_norm(t, 7, 0)


ROUTE_PARTS = 0, 1, 5, 7, 11, 14, 22, ROUTE
ROUTE_LAGS = 0, 0, 1, 1, 2, 16, 17
FREE_AT = {1: 0, "minima": 33, "shares": (42, 44, 46, 49), "resid": 73, 2: 73, "routing": 84, 3: 104}
BOUND_AT = {"gated": 2, 0: 2, "weighted": 3, "x_plus": 8, 1: 8, "minima": 16, "shares": (23, 25, 27, 30), "resid": 39, 2: 39, "routing": 50, 3: 86}


def kernel(x, ctx_1024, mask_Bx1xSxS2_if1, L0_attn_Wq, L0_attn_Wk, L0_attn_Wv, L0_attn_Wf1, L0_attn_Wf2, L0_attn_Wg,
           L0_attn_Wo1, L0_attn_Wo2, L0_attn_ln_w, L0_attn_Wout, L0_xattn_Wq, L0_xattn_Wk, L0_xattn_Wv, L0_xattn_Wo,
           L0_xattn_bo, L0_ffn_centroids, L0_ffn_routing_bias, L0_ffn_Wfc_r, L0_ffn_Wproj_r, L0_ffn_Wfc_sh,
           L0_ffn_Wproj_sh):
    import numpy as np
    import concourse.bacc as bacc
    from concourse.bass_utils import run_bass_kernel_spmd as run

    x, mask = np.asarray(x), np.asarray(mask_Bx1xSxS2_if1)[:, 0]
    order = np.argsort(np.arange(N) % 3 == 0, kind="stable")
    tiled = lambda a: a[:, order].reshape(B, TILES, P, -1).transpose(1, 2, 0, 3)
    t = lambda a: np.swapaxes(np.asarray(a), -1, -2)
    arrays = dict(
        x=tiled(x), xT=t(x), ctxT=t(ctx_1024), mask=tiled(mask),
        wkv=np.concatenate([np.asarray(L0_attn_Wk), np.asarray(L0_attn_Wv)], 1), wqr=L0_attn_Wq, wf1=L0_attn_Wf1,
        wf2=L0_attn_Wf2, wg=L0_attn_Wg, wo1=L0_attn_Wo1, wo2=L0_attn_Wo2, ln_w=L0_attn_ln_w, wout=L0_attn_Wout,
        cqT=t(L0_xattn_Wq), ckT=t(L0_xattn_Wk), cvT=t(L0_xattn_Wv), coT=t(L0_xattn_Wo), cbo=L0_xattn_bo,
        centT=t(L0_ffn_centroids), rbias=L0_ffn_routing_bias,
        wfcT=t(np.concatenate([np.asarray(L0_ffn_Wfc_sh), np.asarray(L0_ffn_Wfc_r)])),
        wpT=t(np.concatenate([np.asarray(L0_ffn_Wproj_sh), np.asarray(L0_ffn_Wproj_r)])))
    arrays = {f"in_{k}": np.ascontiguousarray(v) for k, v in arrays.items()}
    nc = bacc.Bacc("TRN2", target_bir_lowering=False, num_devices=1)
    args = [nc.dram_tensor(k, a.shape, mybir.dt.from_np(a.dtype), kind="ExternalInput").ap() for k, a in arrays.items()]
    args.append(nc.dram_tensor("out_0", (TILES, P, B, D), F32, kind="ExternalOutput").ap())
    decoder_layer(nc, *args)
    r = run(nc, [arrays], core_ids=[0])
    rows = r.results[0]["out_0"].transpose(2, 0, 1, 3).reshape(B, N, D)
    return rows[:, np.argsort(order)]
```
